# Optimizing a Trainium2 kernel written in Bass

```python
import numpy as np
import jax
import jax.numpy as jnp

def _softmax(x, axis=-1):
    return jax.nn.softmax(x, axis=axis)

def _gelu(x):
    return jax.nn.gelu(x, approximate=True)

def _silu(x):
    return jax.nn.silu(x)

def _sigmoid(x):
    return jax.nn.sigmoid(x)

def _layernorm(x, axis=-1, eps=1e-05):
    m = jnp.mean(x, axis=axis, keepdims=True)
    v = jnp.var(x, axis=axis, keepdims=True)
    return (x - m) / jnp.sqrt(v + eps)

def _scatter_add(tgt, idx, src, axis=0):
    return tgt.at[idx].add(src)

def _segment_sum(src, seg, n):
    return jax.ops.segment_sum(src, seg, n)
kernel_name = 'mk_decoder_preln_d2_seqx_r8_a326c5'

def setup_inputs(seed: int=0):
    np.random.seed(seed)
    _w = jnp.asarray

    def _rec_inputs():
        import jax
        import jax.numpy as jnp
        _rk = jax.random.key(seed)
        x = 7.22e-05 + 1 * jax.random.normal(jax.random.fold_in(_rk, 1), (4, 512, 128), jnp.float32)
        _lenS = 512 - jax.random.randint(jax.random.fold_in(_rk, 7), (4,), 0, max(1, 512 // 4) + 1, jnp.int32)
        _lenS2 = 77 - jax.random.randint(jax.random.fold_in(_rk, 8), (4,), 0, max(1, 77 // 4) + 1, jnp.int32)
        _ctx_1024P = jax.random.normal(jax.random.fold_in(_rk, 11), (4, 16, 128), jnp.float32)
        _ctx_1024c = jax.random.dirichlet(jax.random.fold_in(_rk, 511), 0.3 * jnp.ones((16,), jnp.float32), (4, 77))
        _ctx_1024t = jnp.einsum('bsk,bkd->bsd', _ctx_1024c, _ctx_1024P)
        _ctx_1024t = _ctx_1024t * jax.lax.rsqrt(jnp.mean(jnp.square(_ctx_1024t)) + 1e-12) * 0.953939
        ctx_1024 = 4.13588e-05 + 0.999923 * (_ctx_1024t + 0.3 * jax.random.normal(jax.random.fold_in(_rk, 611), (4, 77, 128), jnp.float32))
        return (x, ctx_1024)
    x, ctx_1024 = _rec_inputs()

    def _L0_attn_setup():
        import jax, jax.numpy as jnp
        import numpy as np
        import math
        N_HEAD = 16
        ROPE_BASE = 10000.0

        def _rope_cos_sin(seq_len, head_dim, dtype):
            half = head_dim // 2
            inv_freq = ROPE_BASE ** (-(jnp.arange(half, dtype=jnp.float32) * 2.0 / head_dim))
            t = jnp.arange(seq_len, dtype=jnp.float32)
            ang = t[:, None] * inv_freq[None, :]
            return (jnp.cos(ang).astype(dtype), jnp.sin(ang).astype(dtype))

        def _apply_rope(x, cos, sin):
            x1 = x[..., 0::2]
            x2 = x[..., 1::2]
            c = cos[None, :, None, :]
            s = sin[None, :, None, :]
            out = jnp.stack([x1 * c - x2 * s, x1 * s + x2 * c], axis=-1)
            return out.reshape(x.shape)
        key = jax.random.key(seed)
        kx, kq, kk, kv, ko = jax.random.split(key, 5)
        B, S, H = (2, 256, 128)
        x = jax.random.normal(kx, (B, S, H), dtype=jnp.float32)
        scale = 0.02
        w_q = jax.random.normal(kq, (H, H), dtype=jnp.float32) * scale
        w_k = jax.random.normal(kk, (H, H), dtype=jnp.float32) * scale
        w_v = jax.random.normal(kv, (H, H), dtype=jnp.float32) * scale
        w_o = jax.random.normal(ko, (H, H), dtype=jnp.float32) * scale
        return {'x': x, 'w_q': w_q, 'w_k': w_k, 'w_v': w_v, 'w_o': w_o}
    _L0_attn_all = _L0_attn_setup()
    _L0_attn_in = {k: v for k, v in _L0_attn_all.items() if k in ('w_q', 'w_k', 'w_v', 'w_o')}
    del _L0_attn_all

    def _L0_xattn_setup():
        import jax, jax.numpy as jnp
        import numpy as np
        D_MODEL = 128
        NUM_HEADS = 16
        HEAD_DIM = D_MODEL // NUM_HEADS
        key = jax.random.key(seed)
        ks = jax.random.split(key, 11)
        N, S = (4, 256)
        s = 1.0 / np.sqrt(D_MODEL)
        return {'query': jax.random.normal(ks[0], (N, S, D_MODEL), jnp.float32), 'key': jax.random.normal(ks[1], (N, S, D_MODEL), jnp.float32), 'value': jax.random.normal(ks[2], (N, S, D_MODEL), jnp.float32), 'Wq': jax.random.normal(ks[3], (D_MODEL, D_MODEL), jnp.float32) * s, 'bq': jnp.zeros((D_MODEL,), jnp.float32), 'Wk': jax.random.normal(ks[4], (D_MODEL, D_MODEL), jnp.float32) * s, 'bk': jnp.zeros((D_MODEL,), jnp.float32), 'Wv': jax.random.normal(ks[5], (D_MODEL, D_MODEL), jnp.float32) * s, 'bv': jnp.zeros((D_MODEL,), jnp.float32), 'Wo': jax.random.normal(ks[6], (D_MODEL, D_MODEL), jnp.float32) * s, 'bo': jnp.zeros((D_MODEL,), jnp.float32)}
    _L0_xattn_all = _L0_xattn_setup()
    _L0_xattn_in = {k: v for k, v in _L0_xattn_all.items() if k in ('Wq', 'bq', 'Wk', 'bk', 'Wv', 'bv', 'Wo', 'bo')}
    del _L0_xattn_all

    def _L0_ffn_setup():
        import jax, jax.numpy as jnp
        import numpy as np
        TOP_K = 2
        key = jax.random.key(seed)
        ks = jax.random.split(key, 8)
        B, S, D = (2, 256, 128)
        N_r, N_s = (16, 2)
        u = jax.random.normal(ks[0], (B, S, D), dtype=jnp.float32)
        centroids = jax.random.normal(ks[1], (N_r, D), dtype=jnp.float32)
        expert_biases = jnp.zeros((N_r,), dtype=jnp.float32)
        Wr = jax.random.normal(ks[2], (N_r, D, D), dtype=jnp.float32) * (1.0 / np.sqrt(D))
        br = jax.random.normal(ks[3], (N_r, D), dtype=jnp.float32) * 0.01
        Ws = jax.random.normal(ks[4], (N_s, D, D), dtype=jnp.float32) * (1.0 / np.sqrt(D))
        bs = jax.random.normal(ks[5], (N_s, D), dtype=jnp.float32) * 0.01
        return {'u': u, 'centroids': centroids, 'expert_biases': expert_biases, 'Wr': Wr, 'br': br, 'Ws': Ws, 'bs': bs}
    _L0_ffn_all = _L0_ffn_setup()
    _L0_ffn_in = {k: v for k, v in _L0_ffn_all.items() if k in ('centroids', 'expert_biases', 'Wr', 'br', 'Ws', 'bs')}
    del _L0_ffn_all

    def _L1_attn_setup():
        import jax, jax.numpy as jnp
        import numpy as np
        from jax import lax
        N_LAYER = 4
        D_MODEL = 128
        EXPAND = 2
        D_INNER = EXPAND * D_MODEL
        D_STATE = 16
        D_CONV = 4
        DT_RANK = 64
        EPS = 1e-05

        def _layer_norm(x, w, b):
            mu = jnp.mean(x, axis=-1, keepdims=True)
            var = jnp.var(x, axis=-1, keepdims=True)
            return (x - mu) * lax.rsqrt(var + EPS) * w + b

        def _mamba_block(h, in_w, cw, cb, xp_w, dtp_w, dtp_b, A_log, Dp, out_w):
            B, L, _ = h.shape
            xz = jnp.einsum('bld,ed->ble', h, in_w)
            x, z = jnp.split(xz, 2, axis=-1)
            xT = x.transpose(0, 2, 1)
            xT = lax.conv_general_dilated(xT, cw[:, None, :], window_strides=(1,), padding=[(D_CONV - 1, 0)], feature_group_count=D_INNER)
            x = jax.nn.silu((xT + cb[None, :, None]).transpose(0, 2, 1))
            x_dbl = jnp.einsum('bld,ed->ble', x, xp_w)
            dt = jax.nn.softplus(jnp.einsum('blr,dr->bld', x_dbl[..., :DT_RANK], dtp_w) + dtp_b)
            Bc = x_dbl[..., DT_RANK:DT_RANK + D_STATE]
            Cc = x_dbl[..., DT_RANK + D_STATE:]
            A = -jnp.exp(A_log)

            def step(hstate, inp):
                dt_i, B_i, C_i, x_i = inp
                dA = jnp.exp(dt_i[..., None] * A)
                hstate = dA * hstate + (dt_i * x_i)[..., None] * B_i[:, None, :]
                y = jnp.einsum('bdn,bn->bd', hstate, C_i)
                return (hstate, y)
            h0 = jnp.zeros((B, D_INNER, D_STATE), x.dtype)
            _, ys = lax.scan(step, h0, (dt.transpose(1, 0, 2), Bc.transpose(1, 0, 2), Cc.transpose(1, 0, 2), x.transpose(1, 0, 2)))
            y = ys.transpose(1, 0, 2) + Dp * x
            y = y * jax.nn.silu(z)
            return jnp.einsum('ble,de->bld', y, out_w)
        key = jax.random.key(seed)
        ks = jax.random.split(key, 16)
        s = 0.02
        hidden_states = jax.random.normal(ks[0], (2, 256, D_MODEL), jnp.float32)
        norm_w = jnp.ones((N_LAYER, D_MODEL), jnp.float32)
        norm_b = jnp.zeros((N_LAYER, D_MODEL), jnp.float32)
        in_proj_w = jax.random.normal(ks[1], (N_LAYER, 2 * D_INNER, D_MODEL), jnp.float32) * s
        conv_w = jax.random.normal(ks[2], (N_LAYER, D_INNER, D_CONV), jnp.float32) * 0.2
        conv_b = jnp.zeros((N_LAYER, D_INNER), jnp.float32)
        x_proj_w = jax.random.normal(ks[3], (N_LAYER, DT_RANK + 2 * D_STATE, D_INNER), jnp.float32) * s
        dt_proj_w = jax.random.normal(ks[4], (N_LAYER, D_INNER, DT_RANK), jnp.float32) * DT_RANK ** (-0.5)
        dt = jnp.exp(jax.random.uniform(ks[5], (N_LAYER, D_INNER)) * (np.log(0.1) - np.log(0.001)) + np.log(0.001))
        dt_proj_b = jnp.log(jnp.expm1(dt))
        A_log = jnp.log(jnp.broadcast_to(jnp.arange(1, D_STATE + 1, dtype=jnp.float32), (N_LAYER, D_INNER, D_STATE)))
        D_param = jnp.ones((N_LAYER, D_INNER), jnp.float32)
        out_proj_w = jax.random.normal(ks[6], (N_LAYER, D_MODEL, D_INNER), jnp.float32) * s / np.sqrt(N_LAYER)
        fnorm_w = jnp.ones((D_MODEL,), jnp.float32)
        fnorm_b = jnp.zeros((D_MODEL,), jnp.float32)
        return dict(hidden_states=hidden_states, norm_w=norm_w, norm_b=norm_b, in_proj_w=in_proj_w, conv_w=conv_w, conv_b=conv_b, x_proj_w=x_proj_w, dt_proj_w=dt_proj_w, dt_proj_b=dt_proj_b, A_log=A_log, D_param=D_param, out_proj_w=out_proj_w, fnorm_w=fnorm_w, fnorm_b=fnorm_b)
    _L1_attn_all = _L1_attn_setup()
    _L1_attn_in = {k: v for k, v in _L1_attn_all.items() if k in ('norm_w', 'norm_b', 'in_proj_w', 'conv_w', 'conv_b', 'x_proj_w', 'dt_proj_w', 'dt_proj_b', 'A_log', 'D_param', 'out_proj_w', 'fnorm_w', 'fnorm_b')}
    del _L1_attn_all

    def _L1_xattn_setup():
        import jax, jax.numpy as jnp
        import numpy as np
        from jax import lax
        BIG = jnp.float32(1e+30)

        def _pairwise_euclidean(a, b):
            aa = jnp.sum(a * a, axis=-1)[:, None]
            bb = jnp.sum(b * b, axis=-1)[None, :]
            ab = a @ b.T
            return jnp.sqrt(jnp.maximum(aa + bb - 2.0 * ab, 0.0))

        def _dtw_cost(D):
            row0 = jnp.cumsum(D[0])

            def row_step(prev_row, d_row):
                first = d_row[0] + prev_row[0]

                def col_step(left, inp):
                    d_ij, up, diag = inp
                    r = d_ij + jnp.minimum(jnp.minimum(up, left), diag)
                    return (r, r)
                _, rest = lax.scan(col_step, first, (d_row[1:], prev_row[1:], prev_row[:-1]))
                row = jnp.concatenate([first[None], rest])
                return (row, row)
            _, rows = lax.scan(row_step, row0, D[1:])
            return jnp.concatenate([row0[None], rows], axis=0)

        def _backtrack(R, T1, T2):
            L = T1 + T2 - 1

            def step(carry, _):
                i, j, done = carry
                valid = jnp.logical_not(done)
                cd = jnp.where((i > 0) & (j > 0), R[jnp.maximum(i - 1, 0), jnp.maximum(j - 1, 0)], BIG)
                cu = jnp.where(i > 0, R[jnp.maximum(i - 1, 0), j], BIG)
                cl = jnp.where(j > 0, R[i, jnp.maximum(j - 1, 0)], BIG)
                choice = jnp.argmin(jnp.stack([cd, cu, cl]))
                ni = jnp.where(choice <= 1, i - 1, i)
                nj = jnp.where((choice == 0) | (choice == 2), j - 1, j)
                at_origin = (i == 0) & (j == 0)
                ni = jnp.where(at_origin, 0, ni)
                nj = jnp.where(at_origin, 0, nj)
                return ((ni, nj, done | at_origin), (i, j, valid))
            init = (jnp.int32(T1 - 1), jnp.int32(T2 - 1), jnp.bool_(False))
            _, (i_idx, j_idx, valid) = lax.scan(step, init, None, length=L)
            return (i_idx, j_idx, valid)

        def _align_one(small, large):
            T_small, d = small.shape
            T_large = large.shape[0]
            D = _pairwise_euclidean(small, large)
            R = _dtw_cost(D)
            i_idx, j_idx, valid = _backtrack(R, T_small, T_large)
            contrib = small[i_idx] * valid[:, None].astype(small.dtype)
            expanded = jnp.zeros((T_large, d), dtype=small.dtype).at[j_idx].add(contrib)
            return expanded
        key = jax.random.key(seed)
        k1, k2 = jax.random.split(key)
        teacher = jax.random.normal(k1, (16, 50, 128), dtype=jnp.float32)
        student = jax.random.normal(k2, (16, 75, 128), dtype=jnp.float32)
        return {'teacher_features': teacher, 'student_features': student}
    _L1_xattn_all = _L1_xattn_setup()
    _L1_xattn_in = {k: v for k, v in _L1_xattn_all.items() if k in ()}
    del _L1_xattn_all

    def _L1_ffn_setup():
        import jax, jax.numpy as jnp
        import numpy as np
        HIDDEN = 128
        INNER = 512

        def _weight_quant(w):
            scale = 1.0 / jnp.clip(jnp.mean(jnp.abs(w)), 1e-05)
            wq = jnp.clip(jnp.round(w * scale), -1.0, 1.0) / scale
            return w + jax.lax.stop_gradient(wq - w)

        def _act_quant(x):
            scale = 127.0 / jnp.clip(jnp.max(jnp.abs(x), axis=-1, keepdims=True), 1e-05)
            xq = jnp.clip(jnp.round(x * scale), -128.0, 127.0) / scale
            return x + jax.lax.stop_gradient(xq - x)

        def _bitlinear(x, w):
            return jnp.einsum('bsi,oi->bso', _act_quant(x), _weight_quant(w))
        key = jax.random.key(seed)
        k0, k1, k2, k3 = jax.random.split(key, 4)
        x = jax.random.normal(k0, (4, 256, HIDDEN), dtype=jnp.float32)
        w_gate = jax.random.normal(k1, (INNER, HIDDEN), dtype=jnp.float32) / np.sqrt(HIDDEN)
        w_up = jax.random.normal(k2, (INNER, HIDDEN), dtype=jnp.float32) / np.sqrt(HIDDEN)
        w_down = jax.random.normal(k3, (HIDDEN, INNER), dtype=jnp.float32) / np.sqrt(INNER)
        return {'x': x, 'w_gate': w_gate, 'w_up': w_up, 'w_down': w_down}
    _L1_ffn_all = _L1_ffn_setup()
    _L1_ffn_in = {k: v for k, v in _L1_ffn_all.items() if k in ('w_gate', 'w_up', 'w_down')}
    del _L1_ffn_all
    return {'x': x, 'ctx_1024': ctx_1024, 'L0_attn_w_q': _L0_attn_in['w_q'], 'L0_attn_w_k': _L0_attn_in['w_k'], 'L0_attn_w_v': _L0_attn_in['w_v'], 'L0_attn_w_o': _L0_attn_in['w_o'], 'L0_xattn_Wq': _L0_xattn_in['Wq'], 'L0_xattn_bq': _L0_xattn_in['bq'], 'L0_xattn_Wk': _L0_xattn_in['Wk'], 'L0_xattn_bk': _L0_xattn_in['bk'], 'L0_xattn_Wv': _L0_xattn_in['Wv'], 'L0_xattn_bv': _L0_xattn_in['bv'], 'L0_xattn_Wo': _L0_xattn_in['Wo'], 'L0_xattn_bo': _L0_xattn_in['bo'], 'L0_ffn_centroids': _L0_ffn_in['centroids'], 'L0_ffn_expert_biases': _L0_ffn_in['expert_biases'], 'L0_ffn_Wr': _L0_ffn_in['Wr'], 'L0_ffn_br': _L0_ffn_in['br'], 'L0_ffn_Ws': _L0_ffn_in['Ws'], 'L0_ffn_bs': _L0_ffn_in['bs'], 'L1_attn_norm_w': _L1_attn_in['norm_w'], 'L1_attn_norm_b': _L1_attn_in['norm_b'], 'L1_attn_in_proj_w': _L1_attn_in['in_proj_w'], 'L1_attn_conv_w': _L1_attn_in['conv_w'], 'L1_attn_conv_b': _L1_attn_in['conv_b'], 'L1_attn_x_proj_w': _L1_attn_in['x_proj_w'], 'L1_attn_dt_proj_w': _L1_attn_in['dt_proj_w'], 'L1_attn_dt_proj_b': _L1_attn_in['dt_proj_b'], 'L1_attn_A_log': _L1_attn_in['A_log'], 'L1_attn_D_param': _L1_attn_in['D_param'], 'L1_attn_out_proj_w': _L1_attn_in['out_proj_w'], 'L1_attn_fnorm_w': _L1_attn_in['fnorm_w'], 'L1_attn_fnorm_b': _L1_attn_in['fnorm_b'], 'L1_ffn_w_gate': _L1_ffn_in['w_gate'], 'L1_ffn_w_up': _L1_ffn_in['w_up'], 'L1_ffn_w_down': _L1_ffn_in['w_down']}

def reference(x, ctx_1024, L0_attn_w_q, L0_attn_w_k, L0_attn_w_v, L0_attn_w_o, L0_xattn_Wq, L0_xattn_bq, L0_xattn_Wk, L0_xattn_bk, L0_xattn_Wv, L0_xattn_bv, L0_xattn_Wo, L0_xattn_bo, L0_ffn_centroids, L0_ffn_expert_biases, L0_ffn_Wr, L0_ffn_br, L0_ffn_Ws, L0_ffn_bs, L1_attn_norm_w, L1_attn_norm_b, L1_attn_in_proj_w, L1_attn_conv_w, L1_attn_conv_b, L1_attn_x_proj_w, L1_attn_dt_proj_w, L1_attn_dt_proj_b, L1_attn_A_log, L1_attn_D_param, L1_attn_out_proj_w, L1_attn_fnorm_w, L1_attn_fnorm_b, L1_ffn_w_gate, L1_ffn_w_up, L1_ffn_w_down):
    import jax
    import jax.numpy as jnp

    def _L0_attn_ref(x, w_q, w_k, w_v, w_o):
        import jax, jax.numpy as jnp
        import numpy as np
        import math
        N_HEAD = 16
        ROPE_BASE = 10000.0

        def _rope_cos_sin(seq_len, head_dim, dtype):
            half = head_dim // 2
            inv_freq = ROPE_BASE ** (-(jnp.arange(half, dtype=jnp.float32) * 2.0 / head_dim))
            t = jnp.arange(seq_len, dtype=jnp.float32)
            ang = t[:, None] * inv_freq[None, :]
            return (jnp.cos(ang).astype(dtype), jnp.sin(ang).astype(dtype))

        def _apply_rope(x, cos, sin):
            x1 = x[..., 0::2]
            x2 = x[..., 1::2]
            c = cos[None, :, None, :]
            s = sin[None, :, None, :]
            out = jnp.stack([x1 * c - x2 * s, x1 * s + x2 * c], axis=-1)
            return out.reshape(x.shape)
        B, S, H = x.shape
        d = H // N_HEAD
        q = (x @ w_q.T).reshape(B, S, N_HEAD, d)
        k = (x @ w_k.T).reshape(B, S, N_HEAD, d)
        v = (x @ w_v.T).reshape(B, S, N_HEAD, d)
        cos, sin = _rope_cos_sin(S, d, x.dtype)
        q = _apply_rope(q, cos, sin)
        k = _apply_rope(k, cos, sin)
        scores = jnp.einsum('bqhd,bkhd->bhqk', q, k) / math.sqrt(d)
        coefs = jax.nn.softmax(scores, axis=-1)
        causal = jnp.tril(jnp.ones((S, S), dtype=bool))
        coefs = jnp.where(causal[None, None], coefs, 0.0)
        out = jnp.einsum('bhqk,bkhd->bqhd', coefs, v).reshape(B, S, H)
        return out @ w_o.T

    def _L0_xattn_ref(query, key, value, Wq, bq, Wk, bk, Wv, bv, Wo, bo):
        import jax, jax.numpy as jnp
        import numpy as np
        D_MODEL = 128
        NUM_HEADS = 16
        HEAD_DIM = D_MODEL // NUM_HEADS
        N, Q, _ = query.shape
        K = key.shape[1]
        q = (query @ Wq.T + bq).reshape(N, Q, NUM_HEADS, HEAD_DIM)
        k = (key @ Wk.T + bk).reshape(N, K, NUM_HEADS, HEAD_DIM)
        v = (value @ Wv.T + bv).reshape(N, K, NUM_HEADS, HEAD_DIM)
        scores = jnp.einsum('nqhd,nkhd->nhqk', q, k)
        attn = jax.nn.softmax(scores, axis=3)
        out = jnp.einsum('nhqk,nkhd->nqhd', attn, v).reshape(N, Q, D_MODEL)
        return out @ Wo.T + bo

    def _L0_ffn_ref(u, centroids, expert_biases, Wr, br, Ws, bs):
        import jax, jax.numpy as jnp
        import numpy as np
        TOP_K = 2
        N_r = centroids.shape[0]
        N_s = Ws.shape[0]
        raw_scores = jnp.einsum('bsd,ed->bse', u, centroids)
        s = jax.nn.softmax(raw_scores + expert_biases, axis=-1)
        topk_vals, topk_idx = jax.lax.top_k(s, TOP_K)
        g_topk = jnp.sum(jax.nn.one_hot(topk_idx, N_r, dtype=s.dtype) * topk_vals[..., None], axis=-2)
        xe = jnp.einsum('bsd,eod->bseo', u, Wr) + br
        routed = jnp.einsum('bse,bseo->bso', g_topk, xe)
        shared = (jnp.einsum('bsd,eod->bso', u, Ws) + jnp.sum(bs, axis=0)) / N_s
        return u + routed + shared

    def _L1_attn_ref(hidden_states, norm_w, norm_b, in_proj_w, conv_w, conv_b, x_proj_w, dt_proj_w, dt_proj_b, A_log, D_param, out_proj_w, fnorm_w, fnorm_b):
        import jax, jax.numpy as jnp
        import numpy as np
        from jax import lax
        N_LAYER = 4
        D_MODEL = 128
        EXPAND = 2
        D_INNER = EXPAND * D_MODEL
        D_STATE = 16
        D_CONV = 4
        DT_RANK = 64
        EPS = 1e-05

        def _layer_norm(x, w, b):
            mu = jnp.mean(x, axis=-1, keepdims=True)
            var = jnp.var(x, axis=-1, keepdims=True)
            return (x - mu) * lax.rsqrt(var + EPS) * w + b

        def _mamba_block(h, in_w, cw, cb, xp_w, dtp_w, dtp_b, A_log, Dp, out_w):
            B, L, _ = h.shape
            xz = jnp.einsum('bld,ed->ble', h, in_w)
            x, z = jnp.split(xz, 2, axis=-1)
            xT = x.transpose(0, 2, 1)
            xT = lax.conv_general_dilated(xT, cw[:, None, :], window_strides=(1,), padding=[(D_CONV - 1, 0)], feature_group_count=D_INNER)
            x = jax.nn.silu((xT + cb[None, :, None]).transpose(0, 2, 1))
            x_dbl = jnp.einsum('bld,ed->ble', x, xp_w)
            dt = jax.nn.softplus(jnp.einsum('blr,dr->bld', x_dbl[..., :DT_RANK], dtp_w) + dtp_b)
            Bc = x_dbl[..., DT_RANK:DT_RANK + D_STATE]
            Cc = x_dbl[..., DT_RANK + D_STATE:]
            A = -jnp.exp(A_log)

            def step(hstate, inp):
                dt_i, B_i, C_i, x_i = inp
                dA = jnp.exp(dt_i[..., None] * A)
                hstate = dA * hstate + (dt_i * x_i)[..., None] * B_i[:, None, :]
                y = jnp.einsum('bdn,bn->bd', hstate, C_i)
                return (hstate, y)
            h0 = jnp.zeros((B, D_INNER, D_STATE), x.dtype)
            _, ys = lax.scan(step, h0, (dt.transpose(1, 0, 2), Bc.transpose(1, 0, 2), Cc.transpose(1, 0, 2), x.transpose(1, 0, 2)))
            y = ys.transpose(1, 0, 2) + Dp * x
            y = y * jax.nn.silu(z)
            return jnp.einsum('ble,de->bld', y, out_w)
        hs = hidden_states
        residual = None
        for i in range(norm_w.shape[0]):
            residual = hs + residual if residual is not None else hs
            hs = _layer_norm(residual, norm_w[i], norm_b[i])
            hs = _mamba_block(hs, in_proj_w[i], conv_w[i], conv_b[i], x_proj_w[i], dt_proj_w[i], dt_proj_b[i], A_log[i], D_param[i], out_proj_w[i])
        residual = hs + residual
        return _layer_norm(residual, fnorm_w, fnorm_b)

    def _L1_xattn_ref(teacher_features, student_features):
        import jax, jax.numpy as jnp
        import numpy as np
        from jax import lax
        BIG = jnp.float32(1e+30)

        def _pairwise_euclidean(a, b):
            aa = jnp.sum(a * a, axis=-1)[:, None]
            bb = jnp.sum(b * b, axis=-1)[None, :]
            ab = a @ b.T
            return jnp.sqrt(jnp.maximum(aa + bb - 2.0 * ab, 0.0))

        def _dtw_cost(D):
            row0 = jnp.cumsum(D[0])

            def row_step(prev_row, d_row):
                first = d_row[0] + prev_row[0]

                def col_step(left, inp):
                    d_ij, up, diag = inp
                    r = d_ij + jnp.minimum(jnp.minimum(up, left), diag)
                    return (r, r)
                _, rest = lax.scan(col_step, first, (d_row[1:], prev_row[1:], prev_row[:-1]))
                row = jnp.concatenate([first[None], rest])
                return (row, row)
            _, rows = lax.scan(row_step, row0, D[1:])
            return jnp.concatenate([row0[None], rows], axis=0)

        def _backtrack(R, T1, T2):
            L = T1 + T2 - 1

            def step(carry, _):
                i, j, done = carry
                valid = jnp.logical_not(done)
                cd = jnp.where((i > 0) & (j > 0), R[jnp.maximum(i - 1, 0), jnp.maximum(j - 1, 0)], BIG)
                cu = jnp.where(i > 0, R[jnp.maximum(i - 1, 0), j], BIG)
                cl = jnp.where(j > 0, R[i, jnp.maximum(j - 1, 0)], BIG)
                choice = jnp.argmin(jnp.stack([cd, cu, cl]))
                ni = jnp.where(choice <= 1, i - 1, i)
                nj = jnp.where((choice == 0) | (choice == 2), j - 1, j)
                at_origin = (i == 0) & (j == 0)
                ni = jnp.where(at_origin, 0, ni)
                nj = jnp.where(at_origin, 0, nj)
                return ((ni, nj, done | at_origin), (i, j, valid))
            init = (jnp.int32(T1 - 1), jnp.int32(T2 - 1), jnp.bool_(False))
            _, (i_idx, j_idx, valid) = lax.scan(step, init, None, length=L)
            return (i_idx, j_idx, valid)

        def _align_one(small, large):
            T_small, d = small.shape
            T_large = large.shape[0]
            D = _pairwise_euclidean(small, large)
            R = _dtw_cost(D)
            i_idx, j_idx, valid = _backtrack(R, T_small, T_large)
            contrib = small[i_idx] * valid[:, None].astype(small.dtype)
            expanded = jnp.zeros((T_large, d), dtype=small.dtype).at[j_idx].add(contrib)
            return expanded
        return jax.vmap(_align_one)(teacher_features, student_features)

    def _L1_ffn_ref(x, w_gate, w_up, w_down):
        import jax, jax.numpy as jnp
        import numpy as np
        HIDDEN = 128
        INNER = 512

        def _weight_quant(w):
            scale = 1.0 / jnp.clip(jnp.mean(jnp.abs(w)), 1e-05)
            wq = jnp.clip(jnp.round(w * scale), -1.0, 1.0) / scale
            return w + jax.lax.stop_gradient(wq - w)

        def _act_quant(x):
            scale = 127.0 / jnp.clip(jnp.max(jnp.abs(x), axis=-1, keepdims=True), 1e-05)
            xq = jnp.clip(jnp.round(x * scale), -128.0, 127.0) / scale
            return x + jax.lax.stop_gradient(xq - x)

        def _bitlinear(x, w):
            return jnp.einsum('bsi,oi->bso', _act_quant(x), _weight_quant(w))
        gate = jax.nn.silu(_bitlinear(x, w_gate))
        up = _bitlinear(x, w_up)
        return _bitlinear(gate * up, w_down)
    x = x + _L0_attn_ref(_layernorm(x, axis=-1), L0_attn_w_q, L0_attn_w_k, L0_attn_w_v, L0_attn_w_o)
    x = x + _L0_xattn_ref(_layernorm(x, axis=-1), ctx_1024, ctx_1024, L0_xattn_Wq, L0_xattn_bq, L0_xattn_Wk, L0_xattn_bk, L0_xattn_Wv, L0_xattn_bv, L0_xattn_Wo, L0_xattn_bo)
    x = x + _L0_ffn_ref(_layernorm(x, axis=-1), L0_ffn_centroids, L0_ffn_expert_biases, L0_ffn_Wr, L0_ffn_br, L0_ffn_Ws, L0_ffn_bs)
    x = x + _L1_attn_ref(_layernorm(x, axis=-1), L1_attn_norm_w, L1_attn_norm_b, L1_attn_in_proj_w, L1_attn_conv_w, L1_attn_conv_b, L1_attn_x_proj_w, L1_attn_dt_proj_w, L1_attn_dt_proj_b, L1_attn_A_log, L1_attn_D_param, L1_attn_out_proj_w, L1_attn_fnorm_w, L1_attn_fnorm_b)
    x = x + _L1_xattn_ref(ctx_1024, _layernorm(x, axis=-1))
    x = x + _L1_ffn_ref(_layernorm(x, axis=-1), L1_ffn_w_gate, L1_ffn_w_up, L1_ffn_w_down)
    return x

_drawn_inputs = setup_inputs


def setup_inputs(seed=0):
    import zlib

    import numpy as np

    out = dict(_drawn_inputs(seed))
    spreads = {'L0_xattn_bq': (0.0, 0.1),
     'L0_xattn_bk': (0.0, 0.8),
     'L0_xattn_bv': (0.0, 0.1),
     'L0_xattn_bo': (0.0, 0.1),
     'L0_ffn_expert_biases': (0.0, 0.292),
     'L1_attn_norm_w': (1.0, 0.6),
     'L1_attn_norm_b': (0.0, 0.8),
     'L1_attn_conv_b': (0.0, 0.8),
     'L1_attn_D_param': (1.0, 0.6),
     'L1_attn_fnorm_w': (1.0, 0.2),
     'L1_attn_fnorm_b': (0.0, 0.1)}
    factors = {'L0_attn_w_q': 8.0,
     'L0_attn_w_k': 8.0,
     'L0_attn_w_v': 8.0,
     'L0_attn_w_o': 3.141,
     'L0_ffn_br': 3.123,
     'L0_ffn_bs': 3.138,
     'L1_attn_in_proj_w': 3.179,
     'L1_attn_conv_w': 8.0,
     'L1_attn_x_proj_w': 8.0,
     'L1_attn_dt_proj_w': 8.0,
     'L1_attn_dt_proj_b': 8.0,
     'L1_attn_A_log': 8.0,
     'L1_attn_out_proj_w': 3.178}
    for name, (base, spread) in spreads.items():
        noise = np.random.default_rng([zlib.crc32(name.encode()), seed]).standard_normal(out[name].shape)
        drawn = base * np.exp(spread * noise) if base else spread * noise
        out[name] = jnp.asarray(drawn.astype(out[name].dtype))
    for name, factor in factors.items():
        out[name] = (out[name] * factor).astype(out[name].dtype)
    return out
```

```python
from contextlib import ExitStack

import numpy as np
import concourse.bass as bass
from concourse import mybir

F32 = mybir.dt.float32
BF16 = mybir.dt.bfloat16
F16 = mybir.dt.float16
U32 = mybir.dt.uint32
ALU = mybir.AluOpType
ACT = mybir.ActivationFunctionType
AX = mybir.AxisListType

P = 128
D = 128
B, S = 4, 512
TOK = B * S
NT = TOK // P
ST = S // P
H, HD = 16, 8
CTX = 77
LN_EPS = 1e-5


class Chip:

    def __init__(self, nc, ctx, dram):
        self.nc, self.ctx, self.dram = nc, ctx, dram
        nc.disable_value_cache = True
        self.sem_ctx, self.stage_sems = ctx, []
        self.x = self.sb(ctx, "x_resid", [P, NT, D])
        self.ident = self.sb(ctx, "ident", [P, P])
        self.eps = self.sb(ctx, "eps_col", [P, 1])
        self.bank = ctx.enter_context(nc.psum_tensor("bank", [P, 8, 512], F32))

    def sb(self, ctx, name, shape, dt=F32):
        return ctx.enter_context(self.nc.sbuf_tensor(name, shape, dt))

    def sem(self, name):
        sem = self.sem_ctx.enter_context(self.nc.semaphore(name))
        self.stage_sems.append(sem)
        return sem

    def clear(self, sems):
        with self.nc.Block() as block:
            for n, engine in enumerate((block.vector, block.scalar, block.gpsimd, block.sync, block.tensor)):
                @engine
                def _(e, n=n):
                    for sem in sems[n::5]:
                        e.sem_clear(sem)

    def run(self, stage, *args):
        with ExitStack() as self.sem_ctx:
            self.stage_sems = []
            stage(self, *args)
            self.clear(self.stage_sems)


class Chain:

    def __init__(self, engine, done, at=0):
        self.engine, self.done, self.at = engine, done, at

    def do(self, instruction):
        self.at += 1
        instruction.then_inc(self.done, 1)
        self.engine.wait_ge(self.done, self.at)


class LayerNorm:

    def __init__(self, chip, ctx, name, src, dst):
        self.src, self.dst, self.chip = src, dst, chip
        sb = lambda n, shape: chip.sb(ctx, f"{name}_{n}", shape)
        self.stats, self.mean = sb("stats", [P, NT, 6]), sb("mean", [P, NT])
        self.var, self.tmp = sb("var", [P, NT]), sb("tmp", [P, NT])
        self.log, self.rstd = sb("log", [P, NT]), sb("rstd", [P, NT])
        self.stats_done = chip.sem(f"{name}_stats_done")
        self.step_done = chip.sem(f"{name}_step_done")
        self.var_ready = chip.sem(f"{name}_var_ready")
        self.log_ready = chip.sem(f"{name}_log_ready")
        self.rough_ready = chip.sem(f"{name}_rough_ready")
        self.ready = chip.sem(f"{name}_ready")

    def sems(self):
        return [self.stats_done, self.step_done, self.var_ready, self.log_ready, self.rough_ready, self.ready]

    def vector(self, v):
        st, mean, var, tmp, rstd = self.stats, self.mean, self.var, self.tmp, self.rstd
        for t in range(NT):
            v.bn_stats(st[:, t, :], self.src[:, t, :]).then_inc(self.stats_done, 1)
        v.wait_ge(self.stats_done, NT)
        chain = Chain(v, self.step_done)
        v.tensor_tensor(mean[:], st[:, :, 1], st[:, :, 4], ALU.add)\
            .then_inc(self.step_done, 1)
        v.tensor_tensor(tmp[:], st[:, :, 1], st[:, :, 4], ALU.subtract).then_inc(self.step_done, 1)
        v.tensor_tensor(var[:], st[:, :, 2], st[:, :, 5], ALU.add).then_inc(self.step_done, 1)
        chain.at = 3
        v.wait_ge(self.step_done, 3)
        v.tensor_scalar(mean[:], mean[:], 0.5, None, ALU.mult).then_inc(self.step_done, 1)
        v.scalar_tensor_tensor(tmp[:], tmp[:], 0.25, tmp[:], ALU.mult, ALU.mult).then_inc(self.step_done, 1)
        v.tensor_scalar(var[:], var[:], 1.0 / D, LN_EPS, ALU.mult, ALU.add).then_inc(self.step_done, 1)
        chain.at = 6
        v.wait_ge(self.step_done, 6)
        v.tensor_tensor(var[:], var[:], tmp[:], ALU.add).then_inc(self.var_ready, 1)
        v.tensor_tensor(self.dst[:], self.src[:], mean[:].unsqueeze(2).broadcast_to([P, NT, D]), ALU.subtract)\
            .then_inc(self.step_done, 1)
        chain.at = 7
        v.wait_ge(self.rough_ready, 1)
        chain.do(v.tensor_tensor(tmp[:], rstd[:], rstd[:], ALU.mult))
        chain.do(v.scalar_tensor_tensor(tmp[:], tmp[:], -0.5, var[:], ALU.mult, ALU.mult))
        chain.do(v.scalar_tensor_tensor(rstd[:], tmp[:], 1.5, rstd[:], ALU.add, ALU.mult))
        v.tensor_tensor(self.dst[:], self.dst[:], rstd[:].unsqueeze(2).broadcast_to([P, NT, D]), ALU.mult)\
            .then_inc(self.ready, 1)

    def scalar(self, a):
        a.wait_ge(self.var_ready, 1)
        a.activation(self.log[:], self.var[:], ACT.Ln).then_inc(self.log_ready, 1)
        a.wait_ge(self.log_ready, 1)
        a.activation(self.rstd[:], self.log[:], ACT.Exp, scale=-0.5).then_inc(self.rough_ready, 1)


def feature_major(eng, chip, src, per_bank_done, banks=range(4)):
    for g, bank in enumerate(banks):
        for j in range(ST):
            last = eng.transpose(chip.bank[:, bank, j * P:(j + 1) * P], src[:, g * ST + j, :], chip.ident[:])
        last.then_inc(per_bank_done, 1)


def self_attention_inputs(chip, qstack_src, kstack_src, values):
    nc, dram, bank = chip.nc, chip.dram, chip.bank
    with ExitStack() as ctx:
        xn = chip.sb(ctx, "a_xn", [P, NT, D])
        xnt = chip.sb(ctx, "a_xnt", [P, TOK])
        names = ("wq", "wq_swap", "wk", "wk_swap", "wv")
        w = {n: chip.sb(ctx, "a_" + n, [D, D]) for n in names}
        cos, sin = chip.sb(ctx, "a_cos", [P, S]), chip.sb(ctx, "a_sin", [P, S])
        prod_cos, prod_sin = chip.sb(ctx, "a_pc", [P, 2, S]), chip.sb(ctx, "a_ps", [P, 2, S])
        turned, rest = chip.sb(ctx, "a_turned", [P, 2, S]), chip.sb(ctx, "a_rest", [P, 2, S])
        ln = LayerNorm(chip, ctx, "a_ln", chip.x, xn)
        x_here, w_here = chip.sem("a_x_here"), chip.sem("a_w_here")
        t_done, xnt_ready = chip.sem("a_t_done"), chip.sem("a_xnt_ready")
        qk_done, qk_read = chip.sem("a_qk_done"), chip.sem("a_qk_read")
        v_done = chip.sem("a_v_done")
        prods, turned_ready = chip.sem("a_prods"), chip.sem("a_turned_ready")
        part1, rest_ready = chip.sem("a_part1"), chip.sem("a_rest_ready")
        part2, part3 = chip.sem("a_part2"), chip.sem("a_part3")
        v_out = chip.sem("a_v_out")
        items = [(b, which) for b in range(B) for which in range(2)]
        def remainder(v, n):
            b, which = items[n]
            parts = kstack_src if which else qstack_src
            v.wait_ge(part1, n + 1)
            v.wait_ge(turned_ready, n + 1)
            if n >= 2:
                v.wait_ge(part2, n - 1)
                v.wait_ge(part3, n - 1)
            v.tensor_tensor(rest[:, n % 2, :], turned[:, n % 2, :], parts[:, 0, b * S:(b + 1) * S],
                            ALU.subtract).then_inc(rest_ready, 1)

        with nc.Block() as block:
            @block.sync
            def _(sp):
                sp.dma_start(chip.x[:], dram["x"].rearrange("b (t p) d -> p (b t) d", p=P)).then_inc(x_here, 16)
                sp.dma_start(chip.ident[:], dram["ident"][:, :]).then_inc(w_here, 16)
                for n in names:
                    sp.dma_start(w[n][:], dram[n][:, :]).then_inc(w_here, 16)
                sp.dma_start(cos[:], dram["rope_cos"][:, :]).then_inc(w_here, 16)
                sp.dma_start(sin[:], dram["rope_sin"][:, :]).then_inc(w_here, 16)

            @block.vector
            def _(v):
                v.wait_ge(x_here, 16)
                ln.vector(v)
                v.wait_ge(w_here, 16 * 8)
                for n, (b, which) in enumerate(items):
                    v.wait_ge(qk_done, n + 1)
                    s = n % 2
                    if n >= 2:
                        v.wait_ge(turned_ready, n - 1)
                    v.tensor_tensor(prod_cos[:, s, :], bank[:, 4 + 2 * which, :], cos[:], ALU.mult).then_inc(prods, 1)
                    v.tensor_tensor(prod_sin[:, s, :], bank[:, 5 + 2 * which, :], sin[:], ALU.mult)\
                        .then_inc(qk_read, 1)
                    v.wait_ge(prods, n + 1)
                    v.wait_ge(qk_read, n + 1)
                    if n >= 2:
                        v.wait_ge(part1, n - 1)
                        v.wait_ge(rest_ready, n - 1)
                    v.tensor_tensor(turned[:, s, :], prod_cos[:, s, :], prod_sin[:, s, :], ALU.add)\
                        .then_inc(turned_ready, 1)
                    if n >= 1:
                        remainder(v, n - 1)
                remainder(v, len(items) - 1)

            @block.scalar
            def _(a):
                ln.scalar(a)
                for g in range(B):
                    a.wait_ge(t_done, g + 1)
                    a.activation(xnt[:, g * S:(g + 1) * S], bank[:, g, :], ACT.Copy).then_inc(xnt_ready, 1)
                for n, (b, which) in enumerate(items):
                    parts = kstack_src if which else qstack_src
                    cols = slice(b * S, (b + 1) * S)
                    a.wait_ge(turned_ready, n + 1)
                    a.activation(parts[:, 0, cols], turned[:, n % 2, :], ACT.Copy).then_inc(part1, 1)
                    if which:
                        a.wait_ge(v_done, b + 1)
                        a.activation(values[:, b * ST:(b + 1) * ST, :].rearrange("p t d -> p (t d)"),
                                     bank[:, b, :], ACT.Copy).then_inc(v_out, 1)
                    a.wait_ge(rest_ready, n + 1)
                    a.activation(parts[:, 1, cols], rest[:, n % 2, :], ACT.Copy).then_inc(part2, 1)

            @block.gpsimd
            def _(g):
                for n, (b, which) in enumerate(items):
                    parts = kstack_src if which else qstack_src
                    cols = slice(b * S, (b + 1) * S)
                    g.wait_ge(part2, n + 1)
                    g.wait_ge(rest_ready, n + 1)
                    g.tensor_tensor(parts[:, 2, cols], rest[:, n % 2, :], parts[:, 1, cols], ALU.subtract)\
                        .then_inc(part3, 1)

            @block.tensor
            def _(pe):
                pe.wait_ge(w_here, 16 * 8)
                pe.wait_ge(ln.ready, 1)
                feature_major(pe, chip, xn, t_done)
                for b in range(B):
                    pe.wait_ge(xnt_ready, b + 1)
                    cols = xnt[:, b * S:(b + 1) * S]
                    for which in range(2):
                        n = 2 * b + which
                        if n >= 2:
                            pe.wait_ge(qk_read, n - 1)
                        name = ("wq", "wk")[which]
                        pe.matmul(bank[:, 4 + 2 * which, :], w[name][:], cols, start=True, stop=True)
                        pe.matmul(bank[:, 5 + 2 * which, :], w[name + "_swap"][:], cols, start=True, stop=True)\
                            .then_inc(qk_done, 1)
                    for j in range(ST):
                        last = pe.matmul(bank[:, b, j * P:(j + 1) * P], xnt[:, (b * ST + j) * P:(b * ST + j + 1) * P],
                                         w["wv"][:], start=True, stop=True)
                    last.then_inc(v_done, 1)


QPART = (0, 0, 1, 1, 0, 2)
KPART = (0, 1, 0, 1, 2, 0)


def self_attention(chip, qparts, kparts, values, mixed):
    nc, bank = chip.nc, chip.bank
    SCALE = float(HD) ** -0.5
    SLOTS = len(QPART)
    units = [(qt, hp) for qt in range(ST) for hp in range(H // 2)]
    NU = len(units)
    with ExitStack() as ctx:
        qs = chip.sb(ctx, "s_q", [P, 2, H, S], BF16)
        ks = chip.sb(ctx, "s_k", [P, 2, H, S], BF16)
        keep = chip.sb(ctx, "s_keep", [P, 4, P])
        prob = chip.sb(ctx, "s_prob", [P, 2, 2, S])
        probt = chip.sb(ctx, "s_probt", [P, 2, 2 * ST, P])
        top = chip.sb(ctx, "s_top", [P, 2, 2])
        shift = chip.sb(ctx, "s_shift", [P, 2, 2])
        total = chip.sb(ctx, "s_total", [P, 2, H])
        rtotal = chip.sb(ctx, "s_rtotal", [P, H])
        zeroed, keep_here = chip.sem("s_zeroed"), chip.sem("s_keep_here")
        stacked, scored, topped = chip.sem("s_stacked"), chip.sem("s_scored"), chip.sem("s_topped")
        shifted, expd = chip.sem("s_shifted"), chip.sem("s_expd")
        turned, below_out, diag_out = chip.sem("s_turned"), chip.sem("s_below_out"), chip.sem("s_diag_out")
        weighed, rt_ready, mixed_out = chip.sem("s_weighed"), chip.sem("s_rt_ready"), chip.sem("s_mixed_out")

        def ptb(hh, kb):
            i = 2 * kb + hh
            return bank[:, 4 + i // 4, (i % 4) * P:(i % 4 + 1) * P]

        def stack(sp, b, slot):
            for n in range(SLOTS):
                for parts, st, which in ((qparts, qs, QPART), (kparts, ks, KPART)):
                    src = parts[:, which[n], :].rearrange("p (b s) -> p b s", b=B)
                    sp.dma_start(st[n * HD:(n + 1) * HD, slot, :, :], src[:, b, :]).then_inc(stacked, 16)

        with nc.Block() as block:
            @block.sync
            def _(sp):
                sp.dma_start(keep[:].rearrange("p k q -> p (k q)"), chip.dram["keep"][:, :]).then_inc(keep_here, 16)
                sp.wait_ge(zeroed, 2)
                for b in range(2):
                    stack(sp, b, b)
                    sp.wait_ge(stacked, 16 * 2 * SLOTS * (b + 1))
                for b in range(2, B):
                    sp.wait_ge(scored, NU * (b - 1))
                    stack(sp, b, b % 2)
                    sp.wait_ge(stacked, 16 * 2 * SLOTS * (b + 1))

            @block.gpsimd
            def _(g):
                g.memset(qs[:], 0.0).then_inc(zeroed, 1)
                g.memset(ks[:], 0.0).then_inc(zeroed, 1)

            @block.tensor
            def _(pe):
                with pe.Fori(0, B) as b:
                    pe.wait_ge(stacked, 16 * 2 * SLOTS * (b + 1))
                    for n in range(NU + 2):
                        if n < NU:
                            qt, hp = units[n]
                            if n >= 2:
                                pe.wait_ge(expd, 2 * (NU * b + n - 1))
                            for hh in range(2):
                                h = 2 * hp + hh
                                last = pe.matmul(bank[:, 2 * (n % 2) + hh, :], qs[:, b % 2, h, qt * P:(qt + 1) * P],
                                                 ks[:, b % 2, h, :], start=True, stop=True)
                            last.then_inc(scored, 1)
                        if 1 <= n <= NU:
                            qt, hp = units[n - 1]
                            pe.wait_ge(expd, 2 * (NU * b + n))
                            if n >= 2:
                                pe.wait_ge(diag_out, NU * b + n - 1)
                                pe.wait_ge(below_out, NU * b + n - 1)
                            for kb in range(qt + 1):
                                for hh in range(2):
                                    last = pe.transpose(ptb(hh, kb), prob[:, (n - 1) % 2, hh, kb * P:(kb + 1) * P],
                                                        chip.ident[:])
                            last.then_inc(turned, 1)
                        if n >= 2:
                            qt, hp = units[n - 2]
                            pe.wait_ge(diag_out, NU * b + n - 1)
                            pe.wait_ge(below_out, NU * b + n - 1)
                            if hp == 0 and qt >= 2:
                                pe.wait_ge(mixed_out, ST * b + qt - 1)
                            for hh in range(2):
                                h = 2 * hp + hh
                                for kb in range(qt + 1):
                                    last = pe.matmul(bank[:, 6 + qt % 2, h * HD:(h + 1) * HD],
                                                     probt[:, (n - 2) % 2, 2 * kb + hh, :],
                                                     values[:, b * ST + kb, h * HD:(h + 1) * HD],
                                                     start=(kb == 0), stop=(kb == qt))
                            last.then_inc(weighed, 1)
                    pe.wait_ge(mixed_out, ST * (b + 1))

            @block.vector
            def _(v):
                v.wait_ge(keep_here, 16)
                with v.Fori(0, B) as b:
                    for n in range(NU + 3):
                        if n < NU:
                            qt, hp = units[n]
                            v.wait_ge(scored, NU * b + n + 1)
                            v.tensor_reduce(top[:, n % 2, :], bank[:, 2 * (n % 2):2 * (n % 2) + 2, :], AX.X, ALU.max)\
                                .then_inc(topped, 1)
                            v.wait_ge(topped, NU * b + n + 1)
                            if n >= 2:
                                v.wait_ge(expd, 2 * (NU * b + n - 1))
                            v.tensor_scalar(shift[:, n % 2, :], top[:, n % 2, :], -SCALE, None, ALU.mult)\
                                .then_inc(shifted, 1)
                        if 1 <= n <= NU:
                            qt, hp = units[n - 1]
                            v.wait_ge(turned, NU * b + n)
                            if n >= 3:
                                v.wait_ge(weighed, NU * b + n - 2)
                            odd = qt % 2
                            v.tensor_tensor(probt[:, (n - 1) % 2, 2 * (qt - odd):2 * qt + 2, :],
                                            bank[:, 4 + qt // 2, 0:(2 + 2 * odd) * P].rearrange("p (k q) -> p k q", q=P),
                                            keep[:, 2 - 2 * odd:4, :], ALU.mult)\
                                .then_inc(diag_out, 1)
                        if n >= 3 and units[n - 3][1] == H // 2 - 1:
                            qt = units[n - 3][0]
                            v.wait_ge(weighed, NU * b + n - 2)
                            v.reciprocal(rtotal[:], total[:, qt % 2, :]).then_inc(rt_ready, 1)
                            v.wait_ge(rt_ready, ST * b + qt + 1)
                            v.tensor_tensor(mixed[:, b * ST + qt, :].rearrange("p (h d) -> p h d", h=H),
                                            bank[:, 6 + qt % 2, 0:D].rearrange("p (h d) -> p h d", h=H),
                                            rtotal[:].unsqueeze(2).broadcast_to([P, H, HD]), ALU.mult)\
                                .then_inc(mixed_out, 1)

            @block.scalar
            def _(a):
                with a.Fori(0, B) as b:
                    for n in range(NU + 1):
                        if n < NU:
                            qt, hp = units[n]
                            a.wait_ge(shifted, NU * b + n + 1)
                            if n >= 2:
                                a.wait_ge(turned, NU * b + n - 1)
                            if hp == 0 and qt >= 2:
                                a.wait_ge(mixed_out, ST * b + qt - 1)
                            for hh in range(2):
                                h = 2 * hp + hh
                                a.activation(prob[:, n % 2, hh, :], bank[:, 2 * (n % 2) + hh, :], ACT.Exp,
                                             bias=shift[:, n % 2, hh:hh + 1], scale=SCALE,
                                             accum_out=total[:, qt % 2, h:h + 1]).then_inc(expd, 1)
                        if n >= 1:
                            qt, hp = units[n - 1]
                            a.wait_ge(turned, NU * b + n)
                            if n >= 3:
                                a.wait_ge(weighed, NU * b + n - 2)
                            if qt < 2:
                                a.sem_inc(below_out, 1)
                                continue
                            a.activation(probt[:, (n - 1) % 2, 0:4, :].rearrange("p t q -> p (t q)"),
                                         bank[:, 4, :], ACT.Copy).then_inc(below_out, 1)


def project_and_add(chip, name, mixed, w_name, bias_name=None):
    nc, bank = chip.nc, chip.bank
    with ExitStack() as ctx:
        w = chip.sb(ctx, name + "_w", [D, D])
        mixt = chip.sb(ctx, name + "_mixt", [P, TOK])
        bias = chip.sb(ctx, name + "_bias", [P, D])
        here, t_done, t_out, o_done = (chip.sem(f"{name}_{n}") for n in ("here", "t_done", "t_out", "o_done"))
        added = chip.sem(name + "_added")
        with nc.Block() as block:
            @block.sync
            def _(sp):
                sp.dma_start(w[:], chip.dram[w_name][:, :]).then_inc(here, 16)
                if bias_name:
                    sp.dma_start(bias[:], chip.dram[bias_name][0:1, :].broadcast_to([P, D])).then_inc(here, 16)

            @block.tensor
            def _(pe):
                feature_major(pe, chip, mixed, t_done)
                pe.wait_ge(here, 32 if bias_name else 16)
                for g in range(B):
                    pe.wait_ge(t_out, g + 1)
                    for j in range(ST):
                        t = g * ST + j
                        last = pe.matmul(bank[:, 4 + g, j * D:(j + 1) * D], mixt[:, t * P:(t + 1) * P], w[:],
                                         start=True, stop=True)
                    last.then_inc(o_done, 1)

            @block.scalar
            def _(a):
                for g in range(B):
                    a.wait_ge(t_done, g + 1)
                    a.activation(mixt[:, g * S:(g + 1) * S], bank[:, g, :], ACT.Copy).then_inc(t_out, 1)

            @block.vector
            def _(v):
                if bias_name:
                    v.wait_ge(here, 32)
                    v.tensor_tensor(chip.x[:], chip.x[:], bias[:].unsqueeze(1).broadcast_to([P, NT, D]), ALU.add)\
                        .then_inc(added, 1)
                    v.wait_ge(added, 1)
                for g in range(B):
                    v.wait_ge(o_done, g + 1)
                    xg = chip.x[:, g * ST:(g + 1) * ST, :].rearrange("p t d -> p (t d)")
                    v.tensor_tensor(xg, xg, bank[:, 4 + g, :], ALU.add).then_inc(added, 1)


XG, XH = 3, 6
XW = XH * CTX


def cross_attention(chip):
    nc, dram, bank = chip.nc, chip.dram, chip.bank
    with ExitStack() as stage:
        mixed = chip.sb(stage, "x_mixed", [P, NT, D])
        qt_ = chip.sb(stage, "x_qt", [P, TOK])
        kblk = chip.sb(stage, "x_kblk", [P, B, XG * XH, CTX])
        v1 = chip.sb(stage, "x_v1", [CTX, B, H, HD + 1])
        cross_inputs(chip, qt_, kblk, v1)
        cross_core(chip, qt_, kblk, v1, mixed)
        project_and_add(chip, "x_out", mixed, "x_wo", "x_bo")


def cross_inputs(chip, q_t, kblk, v1):
    nc, dram, bank = chip.nc, chip.dram, chip.bank
    with ExitStack() as ctx:
        xn = chip.sb(ctx, "xi_xn", [P, NT, D])
        xnt = chip.sb(ctx, "xi_xnt", [P, TOK])
        w = {n: chip.sb(ctx, "xi_" + n, [D, D]) for n in ("x_wq", "x_wk", "x_wv")}
        bq, bk = chip.sb(ctx, "xi_bq", [D, 1]), chip.sb(ctx, "xi_bk", [D, 1])
        bv = chip.sb(ctx, "xi_bv", [CTX, D])
        own = chip.sb(ctx, "xi_own", [P, XG * XH])
        c = chip.sb(ctx, "xi_c", [CTX, B, D])
        ct, kt = chip.sb(ctx, "xi_ct", [D, B * CTX]), chip.sb(ctx, "xi_kt", [D, B * CTX])
        ln = LayerNorm(chip, ctx, "xi_ln", chip.x, xn)
        here, t_done, xnt_ready = chip.sem("xi_here"), chip.sem("xi_t_done"), chip.sem("xi_xnt_ready")
        ct_done, ct_ready, k_done, v_done = (chip.sem("xi_" + n) for n in ("ct_done", "ct_ready", "k_done", "v_done"))
        kt_ready, q_done, ones, out = (chip.sem("xi_" + n) for n in ("kt_ready", "q_done", "ones", "out"))
        with nc.Block() as block:
            @block.sync
            def _(sp):
                sp.dma_start(c[:], dram["ctx"].rearrange("b k d -> k b d")).then_inc(here, 16)
                for n in w:
                    sp.dma_start(w[n][:], dram[n][:, :]).then_inc(here, 16)
                sp.dma_start(bq[:], dram["x_bq"][:, :]).then_inc(here, 16)
                sp.dma_start(bk[:], dram["x_bk"][:, :]).then_inc(here, 16)
                sp.dma_start(bv[:], dram["x_bv"][0:1, :].broadcast_to([CTX, D])).then_inc(here, 16)
                sp.dma_start(own[:], dram["own_head"][:, :]).then_inc(here, 16)

            @block.tensor
            def _(pe):
                pe.wait_ge(here, 16 * 8)
                for b in range(B):
                    last = pe.transpose(bank[:, 4, b * CTX:(b + 1) * CTX], c[:, b, :], chip.ident[0:CTX, 0:CTX])
                last.then_inc(ct_done, 1)
                pe.wait_ge(ct_ready, 1)
                pe.matmul(bank[:, 5, 0:B * CTX], w["x_wk"][:], ct[:], start=True, stop=True).then_inc(k_done, 1)
                for b in range(B):
                    last = pe.matmul(bank[0:CTX, 6, b * D:(b + 1) * D], ct[:, b * CTX:(b + 1) * CTX], w["x_wv"][:],
                                     start=True, stop=True)
                last.then_inc(v_done, 1)
                pe.wait_ge(ln.ready, 1)
                feature_major(pe, chip, xn, t_done)
                for b in range(B):
                    pe.wait_ge(xnt_ready, b + 1)
                    pe.matmul(bank[:, b, :], w["x_wq"][:], xnt[:, b * S:(b + 1) * S], start=True, stop=True)\
                        .then_inc(q_done, 1)

            @block.scalar
            def _(a):
                a.wait_ge(here, 16 * 8)
                a.wait_ge(ct_done, 1)
                a.activation(ct[:], bank[:, 4, 0:B * CTX], ACT.Copy).then_inc(ct_ready, 1)
                a.wait_ge(k_done, 1)
                a.activation(kt[:], bank[:, 5, 0:B * CTX], ACT.Identity, bias=bk[:, 0:1]).then_inc(kt_ready, 1)
                ln.scalar(a)
                for b in range(B):
                    a.wait_ge(t_done, b + 1)
                    a.activation(xnt[:, b * S:(b + 1) * S], bank[:, b, :], ACT.Copy).then_inc(xnt_ready, 1)
                for b in range(B):
                    a.wait_ge(q_done, b + 1)
                    a.activation(q_t[:, b * S:(b + 1) * S], bank[:, b, :], ACT.Identity, bias=bq[:, 0:1])\
                        .then_inc(out, 1)

            @block.gpsimd
            def _(g):
                g.memset(v1[:, :, :, HD:HD + 1], 1.0).then_inc(ones, 1)
                g.wait_ge(kt_ready, 1)
                for b in range(B):
                    g.tensor_tensor(kblk[:, b, :, :],
                                    kt[:, b * CTX:(b + 1) * CTX].unsqueeze(1).broadcast_to([P, XG * XH, CTX]),
                                    own[:].unsqueeze(2).broadcast_to([P, XG * XH, CTX]), ALU.mult).then_inc(out, 1)

            @block.vector
            def _(v):
                ln.vector(v)
                v.wait_ge(v_done, 1)
                v.wait_ge(here, 16 * 8)
                v.tensor_tensor(v1[:, :, :, 0:HD], bank[0:CTX, 6, :].rearrange("k (b h d) -> k b h d", b=B, h=H),
                                bv[:].rearrange("k (h d) -> k h d", h=H).unsqueeze(1).broadcast_to([CTX, B, H, HD]),
                                ALU.add).then_inc(out, 1)


def cross_core(chip, q_t, kblk, v1, mixed):
    nc, bank = chip.nc, chip.bank
    HALF = H // 2
    with ExitStack() as ctx:
        top = chip.sb(ctx, "xc_top", [P, XG, XH])
        low = chip.sb(ctx, "xc_low", [P, 2, XG, XH, CTX])
        probt = chip.sb(ctx, "xc_probt", [CTX, 2, HALF, P])
        rtotal = chip.sb(ctx, "xc_rtotal", [P, H])
        scored, topped, lowered, expd = (chip.sem("xc_" + n) for n in ("scored", "topped", "lowered", "expd"))
        turned, turned_out, weighed = (chip.sem("xc_" + n) for n in ("turned", "turned_out", "weighed"))
        rt_ready, mixed_out = chip.sem("xc_rt_ready"), chip.sem("xc_mixed_out")
        scores = bank[:, 0:XG, 0:XW].rearrange("p g (h k) -> p g h k", h=XH)

        def tile_scores(pe, t, batch):
            for g in range(XG):
                last = pe.matmul(bank[:, g, 0:XW], q_t[:, bass.ds(t * P, P)] if not isinstance(t, int) else q_t[:, t * P:(t + 1) * P],
                                 kblk[:, batch, g * XH:(g + 1) * XH, :].rearrange("p h k -> p (h k)"),
                                 start=True, stop=True)
            last.then_inc(scored, 1)

        with nc.Block() as block:
            @block.tensor
            def _(pe):
                for t in range(NT):
                    if t == 0:
                        tile_scores(pe, 0, 0)
                    for half in range(2):
                        n = 2 * t + half
                        if half == 0:
                            pe.wait_ge(expd, t + 1)
                        if n >= 2:
                            pe.wait_ge(turned_out, n - 1)
                        for j in range(HALF):
                            h = half * HALF + j
                            last = pe.transpose(bank[0:CTX, 3 + 2 * half + j // 4, (j % 4) * P:(j % 4 + 1) * P],
                                                low[:, t % 2, h // XH, h % XH, :], chip.ident[:])
                        last.then_inc(turned, 1)
                    if t + 1 < NT:
                        pe.wait_ge(lowered, t + 1)
                        tile_scores(pe, t + 1, (t + 1) // ST)
                    if t >= 1:
                        pe.wait_ge(mixed_out, t)
                    for half in range(2):
                        pe.wait_ge(turned_out, 2 * t + half + 1)
                        for j in range(HALF):
                            h = half * HALF + j
                            last = pe.matmul(bank[:, 7, h * (HD + 1):(h + 1) * (HD + 1)], probt[:, half, j, :],
                                             v1[:, t // ST, h, :], start=True, stop=True)
                    last.then_inc(weighed, 1)

            @block.vector
            def _(v):
                for t in range(NT + 1):
                    if t < NT:
                        v.wait_ge(scored, t + 1)
                        v.tensor_reduce(top[:], scores, AX.X, ALU.max).then_inc(topped, 1)
                        v.wait_ge(topped, t + 1)
                        if t >= 2:
                            v.wait_ge(turned, 2 * (t - 1))
                        v.tensor_tensor(low[:, t % 2], scores, top[:].unsqueeze(3).broadcast_to([P, XG, XH, CTX]),
                                        ALU.subtract).then_inc(lowered, 1)
                    if t >= 1:
                        v.wait_ge(weighed, t)
                        o = bank[:, 7, 0:H * (HD + 1)].rearrange("p (h d) -> p h d", h=H)
                        v.reciprocal(rtotal[:], o[:, :, HD]).then_inc(rt_ready, 1)
                        v.wait_ge(rt_ready, t)
                        v.tensor_tensor(mixed[:, t - 1, :].rearrange("p (h d) -> p h d", h=H), o[:, :, 0:HD],
                                        rtotal[:].unsqueeze(2).broadcast_to([P, H, HD]), ALU.mult)\
                            .then_inc(mixed_out, 1)

            @block.scalar
            def _(a):
                for t in range(NT):
                    a.wait_ge(lowered, t + 1)
                    flat = low[:, t % 2].rearrange("p g h k -> p (g h k)")
                    a.activation(flat, flat, ACT.Exp).then_inc(expd, 1)
                    for half in range(2):
                        a.wait_ge(turned, 2 * t + half + 1)
                        if t >= 1:
                            a.wait_ge(weighed, t)
                        a.activation(probt[:, half].rearrange("k h q -> k (h q)"),
                                     bank[0:CTX, 3 + 2 * half:5 + 2 * half, :].rearrange("k b q -> k (b q)"),
                                     ACT.Copy).then_inc(turned_out, 1)


def more(r, a):
    f = np.float32
    col = lambda n: a[n].reshape(-1, 1)
    row = lambda n: a[n].reshape(1, -1)
    own = (np.arange(P)[:, None] // HD == np.arange(XG * XH)[None, :]).astype(f)
    r.update(x_wq=a["L0_xattn_Wq"].T, x_wk=a["L0_xattn_Wk"].T, x_wv=a["L0_xattn_Wv"].T, x_wo=a["L0_xattn_Wo"].T,
             x_bq=col("L0_xattn_bq"), x_bk=col("L0_xattn_bk"), x_bv=row("L0_xattn_bv"), x_bo=row("L0_xattn_bo"),
             own_head=own)


NE, NSH, TOPK = 16, 2, 2
QE = 4
ACT_E = 1


def experts(chip):
    with ExitStack() as stage:
        u = chip.sb(stage, "e_u", [P, NT, D])
        ut = chip.sb(stage, "e_ut", [P, TOK])
        gates = chip.sb(stage, "e_gates", [P, NT, NE + NSH])
        wr = chip.sb(stage, "e_wr", [D, NE, D])
        ws = chip.sb(stage, "e_ws", [D, NSH, D])
        brs = chip.sb(stage, "e_brs", [NE + NSH, D])
        weights_here = chip.sem("e_weights_here")
        route(chip, u, ut, gates, wr, ws, brs, weights_here)
        mix_experts(chip, u, ut, gates, wr, ws, brs, weights_here)


def route(chip, u, ut, gates, wr, ws, brs, weights_here):
    nc, dram, bank = chip.nc, chip.dram, chip.bank
    with ExitStack() as ctx:
        sb = lambda n, shape, dt=F32: chip.sb(ctx, "r_" + n, shape, dt)
        cent, bias, iota = sb("cent", [D, NE]), sb("bias", [P, NE]), sb("iota", [P, NE])
        score, hit = sb("score", [P, NT, NE]), sb("hit", [P, NT, NE])
        top, tot, rtot = sb("top", [P, NT]), sb("tot", [P, NT]), sb("rtot", [P, NT])
        best, where, wheref = sb("best", [P, NT, 8]), sb("where", [P, NT, 8], U32), sb("wheref", [P, NT, 8])
        ln = LayerNorm(chip, ctx, "r_ln", chip.x, u)
        here, t_done, ut_ready, raw_done = (chip.sem("r_" + n) for n in ("here", "t_done", "ut_ready", "raw_done"))
        step, centred, expd = chip.sem("r_step"), chip.sem("r_centred"), chip.sem("r_expd")
        summed = chip.sem("r_summed")
        with nc.Block() as block:
            @block.sync
            def _(sp):
                sp.dma_start(cent[:], dram["e_cent"][:, :]).then_inc(here, 16)
                sp.dma_start(bias[:], dram["e_bias"][0:1, :].broadcast_to([P, NE])).then_inc(here, 16)
                sp.dma_start(iota[:], dram["iota"][0:1, 0:NE].broadcast_to([P, NE])).then_inc(here, 16)
                sp.dma_start(wr[:], dram["e_wr"].rearrange("e d o -> d e o")).then_inc(weights_here, 16)
                sp.dma_start(ws[:], dram["e_ws"].rearrange("e d o -> d e o")).then_inc(weights_here, 16)
                sp.dma_start(brs[0:NE, :], dram["e_br"][:, :]).then_inc(weights_here, 16)
                sp.dma_start(brs[NE:NE + NSH, :], dram["e_bs"][:, :]).then_inc(weights_here, 16)

            @block.tensor
            def _(pe):
                pe.wait_ge(ln.ready, 1)
                feature_major(pe, chip, u, t_done)
                pe.wait_ge(here, 48)
                pe.wait_ge(ut_ready, B)
                for t in range(NT):
                    last = pe.matmul(bank[:, 4, t * NE:(t + 1) * NE], ut[:, t * P:(t + 1) * P], cent[:],
                                     start=True, stop=True)
                last.then_inc(raw_done, 1)

            @block.scalar
            def _(a):
                ln.scalar(a)
                for g in range(B):
                    a.wait_ge(t_done, g + 1)
                    a.activation(ut[:, g * S:(g + 1) * S], bank[:, g, :], ACT.Copy).then_inc(ut_ready, 1)
                a.wait_ge(centred, 1)
                a.activation(score[:], score[:], ACT.Exp).then_inc(expd, 1)

            @block.gpsimd
            def _(g):
                g.memset(gates[:, :, NE:NE + NSH], 1.0 / NSH).then_inc(summed, 1)
                g.wait_ge(weights_here, 64)
                g.tensor_tensor(ws[:, 0, :], ws[:, 0, :], ws[:, 1, :], ALU.add).then_inc(summed, 1)
                g.wait_ge(summed, 2)
                g.tensor_scalar(ws[:, 0, :], ws[:, 0, :], 1.0 / NSH, None, ALU.mult).then_inc(summed, 1)

            @block.vector
            def _(v):
                over_e = lambda col: col.unsqueeze(2).broadcast_to([P, NT, NE])
                over_t = lambda row: row.unsqueeze(1).broadcast_to([P, NT, NE])
                ln.vector(v)
                v.wait_ge(here, 48)
                v.wait_ge(raw_done, 1)
                chain = Chain(v, step)
                chain.do(v.tensor_tensor(score[:], bank[:, 4, 0:NT * NE].rearrange("p (t e) -> p t e", t=NT),
                                         over_t(bias[:]), ALU.add))
                chain.do(v.tensor_reduce(top[:], score[:], AX.X, ALU.max))
                v.tensor_tensor(score[:], score[:], over_e(top[:]), ALU.subtract).then_inc(centred, 1)
                v.wait_ge(expd, 1)
                chain.do(v.tensor_reduce(tot[:], score[:], AX.X, ALU.add))
                chain.do(v.reciprocal(rtot[:], tot[:]))
                chain.do(v.tensor_tensor(score[:], score[:], over_e(rtot[:]), ALU.mult))
                for t in range(NT):
                    v.max(best[:, t, :], score[:, t, :]).then_inc(step, 1)
                chain.at += NT
                v.wait_ge(step, chain.at)
                for t in range(NT):
                    v.max_index(where[:, t, :], best[:, t, :], score[:, t, :]).then_inc(step, 1)
                chain.at += NT
                v.wait_ge(step, chain.at)
                chain.do(v.tensor_copy(wheref[:], where[:]))
                routed = gates[:, :, 0:NE]
                chain.do(v.tensor_tensor(routed, over_t(iota[:]), over_e(wheref[:, :, 0]), ALU.is_equal))
                chain.do(v.tensor_tensor(routed, routed, over_e(best[:, :, 0]), ALU.mult))
                for k in range(1, TOPK):
                    chain.do(v.tensor_tensor(hit[:], over_t(iota[:]), over_e(wheref[:, :, k]), ALU.is_equal))
                    chain.do(v.tensor_tensor(hit[:], hit[:], over_e(best[:, :, k]), ALU.mult))
                    chain.do(v.tensor_tensor(routed, routed, hit[:], ALU.add))


def mix_experts(chip, u, ut, gates, wr, ws, brs, weights_here):
    nc, bank = chip.nc, chip.bank
    NQ = NE // QE
    DVE_E = QE - ACT_E
    with ExitStack() as ctx:
        gatest = chip.sb(ctx, "m_gatest", [NE + NSH, TOK])
        gated = chip.sb(ctx, "m_gated", [P, 2, NE, D])
        routed = chip.sb(ctx, "m_routed", [P, 2, D])
        gt_done, gt_out = chip.sem("m_gt_done"), chip.sem("m_gt_out")
        made, by_vector, by_scalar = chip.sem("m_made"), chip.sem("m_by_vector"), chip.sem("m_by_scalar")
        shared, reduced, joined, plus_u = (chip.sem("m_" + n) for n in ("shared", "reduced", "joined", "plus_u"))
        with nc.Block() as block:
            @block.gpsimd
            def _(g):
                g.tensor_tensor(chip.x[:], chip.x[:], u[:], ALU.add).then_inc(plus_u, 1)

            @block.tensor
            def _(pe):
                for g in range(4):
                    for j in range(ST):
                        t = g * ST + j
                        last = pe.transpose(bank[0:NE + NSH, g, j * P:(j + 1) * P], gates[:, t, :], chip.ident[:])
                    last.then_inc(gt_done, 1)
                pe.wait_ge(weights_here, 64)
                for t in range(NT):
                    for q in range(NQ):
                        n = t * NQ + q
                        if n < 4:
                            pe.wait_ge(gt_out, n + 1)
                        if n >= 6:
                            pe.wait_ge(by_vector, n - 5)
                            pe.wait_ge(by_scalar, n - 5)
                        pe.matmul(bank[:, n % 6, :], ut[:, t * P:(t + 1) * P],
                                  wr[:, q * QE:(q + 1) * QE, :].rearrange("d e o -> d (e o)"), start=True, stop=True)\
                            .then_inc(made, 1)
                    if t == 0:
                        pe.wait_ge(gt_out, 4)
                    if t >= 2:
                        pe.wait_ge(joined, t - 1)
                    s = bank[:, 6 + t % 2, 0:D]
                    pe.matmul(s, ut[:, t * P:(t + 1) * P], ws[:, 0, :], start=True, stop=False)
                    pe.matmul(s, gatest[:, t * P:(t + 1) * P], brs[:], start=False, stop=True).then_inc(shared, 1)

            @block.scalar
            def _(a):
                for g in range(4):
                    a.wait_ge(gt_done, g + 1)
                    a.activation(gatest[:, g * S:(g + 1) * S], bank[0:NE + NSH, g, :], ACT.Copy).then_inc(gt_out, 1)
                for n in range(NT * NQ):
                    t, q = n // NQ, n % NQ
                    a.wait_ge(by_vector, n + 1)
                    if q == 0 and t >= 2:
                        a.wait_ge(reduced, t - 1)
                    for e in range(DVE_E, QE):
                        last = a.activation(gated[:, t % 2, q * QE + e, :], bank[:, n % 6, e * D:(e + 1) * D],
                                            ACT.Copy, scale=gates[:, t, q * QE + e:q * QE + e + 1])
                    last.then_inc(by_scalar, 1)

            @block.vector
            def _(v):
                v.wait_ge(plus_u, 1)
                for t in range(NT + 1):
                    if t < NT:
                        for q in range(NQ):
                            n = t * NQ + q
                            v.wait_ge(made, n + 1)
                            e = slice(q * QE, q * QE + DVE_E)
                            v.tensor_tensor(gated[:, t % 2, e, :],
                                            bank[:, n % 6, 0:DVE_E * D].rearrange("p (e o) -> p e o", o=D),
                                            gates[:, t, e].unsqueeze(2).broadcast_to([P, DVE_E, D]), ALU.mult)\
                                .then_inc(by_vector, 1)
                    if t >= 1:
                        v.wait_ge(by_scalar, NQ * t)
                        s = (t - 1) % 2
                        v.tensor_reduce(routed[:, s, :], gated[:, s].rearrange("p e o -> p o e"), AX.X, ALU.add)\
                            .then_inc(reduced, 1)
                        v.wait_ge(shared, t)
                        v.tensor_tensor(chip.x[:, t - 1, :], chip.x[:, t - 1, :], bank[:, 6 + s, 0:D], ALU.add)\
                            .then_inc(joined, 1)
                        v.wait_ge(joined, t)
                        v.wait_ge(reduced, t)
                        v.tensor_tensor(chip.x[:, t - 1, :], chip.x[:, t - 1, :], routed[:, s, :], ALU.add)


def more_experts(r, a):
    T = lambda n: a[n].transpose(0, 2, 1)
    r.update(e_cent=a["L0_ffn_centroids"].T, e_bias=a["L0_ffn_expert_biases"].reshape(1, -1),
             e_wr=T("L0_ffn_Wr"), e_ws=T("L0_ffn_Ws"), e_br=a["L0_ffn_br"], e_bs=a["L0_ffn_bs"],
             iota=np.arange(S, dtype=np.float32).reshape(1, -1))


NL = 4
DI, DS, DR, DC = 256, 16, 64, 4
NCH = DI // P
PAD = DC - 1
HB = B // 2
HT = HB * S
SMALL = 1 / 16
SERIES = (1.0, -0.49999176, 0.33253264, -0.22751441)
REP = 96


class MambaTiles:
    def __init__(self, chip, ctx):
        sb = lambda n, shape, dt=F32: chip.sb(ctx, "m_" + n, shape, dt)
        self.res = sb("res", [P, NT, D])
        self.h_t = sb("h_t", [P, B, PAD + S])
        self.xs, self.zs = sb("xs", [P, NCH, TOK]), sb("zs", [P, NCH, TOK])
        self.dt, self.u = sb("dt", [P, NCH, TOK]), sb("u", [P, NCH, TOK])
        self.bc = sb("bc", [REP, TOK], BF16)
        self.pick = sb("pick", [REP, 2 * DS, P], BF16)
        self.in_w, self.taps = sb("in_w", [D, 2 * DI]), sb("taps", [D, DC, DI])
        self.conv_w = sb("conv_w", [D, DC, DI])
        self.xp_w, self.dtp_w = sb("xp_w", [P, NCH, DR + 2 * DS]), sb("dtp_w", [DR, DI])
        self.out_w = sb("out_w", [P, NCH, D])
        self.col = sb("col", [P, 2 + 3 * NCH])
        self.a = sb("a", [P, NCH, DS])


def mamba(chip):
    nc, dram = chip.nc, chip.dram
    with ExitStack() as stage:
        m = MambaTiles(chip, stage)
        first = LayerNorm(chip, stage, "m_first", chip.x, m.res)
        here, zero, cast = chip.sem("m_here"), chip.sem("m_zero"), chip.sem("m_cast")
        with ExitStack() as ctx:
            pick32 = chip.sb(ctx, "m_pick32", [REP, 2 * DS * P])
            with nc.Block() as block:
                @block.sync
                def _(sp):
                    sp.dma_start(pick32[:], dram["pick"][:, :]).then_inc(here, 16)

                @block.gpsimd
                def _(g):
                    g.memset(m.h_t[:], 0.0).then_inc(zero, 1)
                    g.wait_ge(here, 16)
                    g.tensor_copy(m.pick[:].rearrange("r n p -> r (n p)"), pick32[:]).then_inc(cast, 1)

                @block.vector
                def _(v):
                    first.vector(v)

                @block.scalar
                def _(a):
                    first.scalar(a)
        with ExitStack() as loop:
            front = MambaFront(chip, m)
            core = MambaCore(chip, m)
            with nc.Fori(0, NL) as layer:
                front.block(layer)
                core.block()
                chip.clear(front.sems() + core.sems())
        mamba_out(chip, m)


class MambaFront:

    def __init__(self, chip, m):
        self.chip, self.m = chip, m
        names = ("w_here", "taps", "a_exp", "a_neg", "t_done", "h_ready", "conv", "gate", "x_silu", "z_silu", "rank",
                 "bc_done", "rank_out", "bc_hi", "bc_rest", "bc_mid", "bc_midcopy", "bc_lo", "dt_raw", "dt_out",
                 "abs_ready", "exp_ready", "ones", "log_small", "big_e", "log_ready", "step", "series", "kept", "dt_ready",
                 "u_ready")
        self.s = {n: chip.sem("mf_" + n) for n in names}
        self.ln = None

    def sems(self):
        return list(self.s.values()) + self.ln.sems()

    def block(self, layer):
        chip, m, s = self.chip, self.m, self.s
        nc, dram, bank = chip.nc, chip.dram, chip.bank
        with ExitStack() as ctx:
            sb = lambda n, shape, dt=F32: chip.sb(ctx, "mf_" + n, shape, dt)
            xn = sb("xn", [P, NT, D])
            self.ln = ln = LayerNorm(chip, ctx, "mf_ln", m.res, xn)
            rank = sb("rank", [DR, TOK])
            rest, mid = sb("rest", [2 * DS, 2, S]), sb("mid", [2 * DS, 2, S], BF16)
            mag, big, series = sb("mag", [P, 2, HT]), sb("big", [P, 2, HT]), sb("series", [P, 2, HT])
            one, log_small = sb("one", [P, 1]), sb("log_small", [P, 1])
            pieces = [(c, hf) for hf in range(2) for c in range(NCH)]
            cols = lambda b: slice(b * S, (b + 1) * S)
            half = lambda hf: slice(hf * HT, (hf + 1) * HT)
            NW = 10
            def logarithm(a, n):
                a.wait_ge(s["big_e"], n + 1)
                a.activation(big[:, n % 2, :], big[:, n % 2, :], ACT.Ln, bias=one[:]).then_inc(s["log_ready"], 1)

            with nc.Block() as block:
                @block.sync
                def _(sp):
                    def load(dst, name):
                        sp.dma_start(dst, dram[name][bass.ds(layer, 1)].rearrange(
                            "l p n -> (l p) n")).then_inc(s["w_here"], 16)
                    flat = lambda t: t[:].rearrange("p a b -> p (a b)")
                    load(m.in_w[:], "mb_in")
                    load(flat(m.xp_w), "mb_xp")
                    load(m.dtp_w[:], "mb_dtp")
                    load(flat(m.out_w), "mb_out")
                    load(m.col[:], "mb_col")
                    load(flat(m.a), "mb_a")
                    sp.dma_start(flat(m.conv_w), dram["mb_conv"][bass.ds(layer, 1), :].broadcast_to([D, DC * DI]))\
                        .then_inc(s["w_here"], 16)

                @block.gpsimd
                def _(g):
                    g.wait_ge(s["w_here"], 16 * 7)
                    g.tensor_tensor(m.taps[:], m.in_w[:, 0:DI].unsqueeze(1).broadcast_to([D, DC, DI]), m.conv_w[:],
                                    ALU.mult).then_inc(s["taps"], 1)
                    g.wait_ge(s["a_exp"], 1)
                    g.tensor_scalar(m.a[:], m.a[:], -1.0, None, ALU.mult).then_inc(s["a_neg"], 1)
                    for b in range(B):
                        g.wait_ge(s["bc_rest"], b + 1)
                        if b >= 2:
                            g.wait_ge(s["bc_lo"], b - 1)
                        g.tensor_copy(mid[:, b % 2, :], rest[:, b % 2, :]).then_inc(s["bc_mid"], 1)
                    for n, (c, hf) in enumerate(pieces):
                        g.wait_ge(s["dt_ready"], n + 1)
                        g.wait_ge(s["x_silu"], B)
                        g.tensor_tensor(m.u[:, c, half(hf)], m.dt[:, c, half(hf)], m.xs[:, c, half(hf)], ALU.mult)\
                            .then_inc(s["u_ready"], 1)

                @block.tensor
                def _(pe):
                    pe.wait_ge(ln.ready, 1)
                    feature_major(pe, chip, xn, s["t_done"], banks=range(4, 8))
                    pe.wait_ge(s["w_here"], 16 * 7)
                    pe.wait_ge(s["taps"], 1)
                    for n in range(B + 1):
                        if n < B:
                            b, o = n, 4 * (n % 2)
                            pe.wait_ge(s["h_ready"], b + 1 if b == 0 else B)
                            if b >= 2:
                                pe.wait_ge(s["dt_out"], b - 1)
                            for c in range(NCH):
                                for k in range(DC):
                                    last = pe.matmul(bank[:, o + c, :], m.taps[:, k, c * P:(c + 1) * P],
                                                     m.h_t[:, b, k:k + S], start=(k == 0), stop=(k == DC - 1))
                            last.then_inc(s["conv"], 1)
                            for c in range(NCH):
                                last = pe.matmul(bank[:, o + 2 + c, :], m.in_w[:, DI + c * P:DI + (c + 1) * P],
                                                 m.h_t[:, b, PAD:], start=True, stop=True)
                            last.then_inc(s["gate"], 1)
                        if n >= 1:
                            b, o = n - 1, 4 * ((n - 1) % 2)
                            pe.wait_ge(s["x_silu"], b + 1)
                            for c in range(NCH):
                                last = pe.matmul(bank[0:DR, o, :], m.xp_w[:, c, 0:DR], m.xs[:, c, cols(b)],
                                                 start=(c == 0), stop=(c == NCH - 1))
                            last.then_inc(s["rank"], 1)
                            for c in range(NCH):
                                last = pe.matmul(bank[0:2 * DS, o + 1, :], m.xp_w[:, c, DR:], m.xs[:, c, cols(b)],
                                                 start=(c == 0), stop=(c == NCH - 1))
                            last.then_inc(s["bc_done"], 1)
                            pe.wait_ge(s["rank_out"], b + 1)
                            pe.wait_ge(s["z_silu"], b + 1)
                            for c in range(NCH):
                                last = pe.matmul(bank[:, o + 2 + c, :], m.dtp_w[:, c * P:(c + 1) * P], rank[:, cols(b)],
                                                 start=True, stop=True)
                            last.then_inc(s["dt_raw"], 1)
                            pe.wait_ge(s["bc_rest"], b + 1)

                @block.scalar
                def _(a):
                    a.wait_ge(s["w_here"], 16 * 7)
                    a.activation(m.a[:], m.a[:], ACT.Exp).then_inc(s["a_exp"], 1)
                    ln.scalar(a)
                    for b in range(B):
                        a.wait_ge(s["t_done"], b + 1)
                        a.activation(m.h_t[:, b, PAD:], bank[:, 4 + b, :], ACT.Identity, scale=m.col[:, 0:1],
                                     bias=m.col[:, 1:2]).then_inc(s["h_ready"], 1)
                    for n in range(B + 1):
                        if n < B:
                            b, o = n, 4 * (n % 2)
                            a.wait_ge(s["conv"], b + 1)
                            for c in range(NCH):
                                last = a.activation(m.xs[:, c, cols(b)], bank[:, o + c, :], ACT.Silu,
                                                    bias=m.col[:, 2 + c:3 + c])
                            last.then_inc(s["x_silu"], 1)
                            a.wait_ge(s["gate"], b + 1)
                            for c in range(NCH):
                                last = a.activation(m.zs[:, c, cols(b)], bank[:, o + 2 + c, :], ACT.Silu)
                            last.then_inc(s["z_silu"], 1)
                        if n >= 1:
                            b, o = n - 1, 4 * ((n - 1) % 2)
                            a.wait_ge(s["rank"], b + 1)
                            a.activation(rank[:, cols(b)], bank[0:DR, o, :], ACT.Copy).then_inc(s["rank_out"], 1)
                            a.wait_ge(s["bc_done"], b + 1)
                            a.activation(m.bc[0:2 * DS, cols(b)], bank[0:2 * DS, o + 1, :], ACT.Copy)\
                                .then_inc(s["bc_hi"], 1)
                            a.wait_ge(s["dt_raw"], b + 1)
                            for c in range(NCH):
                                last = a.activation(m.dt[:, c, cols(b)], bank[:, o + 2 + c, :], ACT.Identity,
                                                    bias=m.col[:, 2 + NCH + c:3 + NCH + c])
                            last.then_inc(s["dt_out"], 1)
                            a.wait_ge(s["bc_rest"], b + 1)
                            a.activation(m.bc[2 * DS:4 * DS, cols(b)], rest[:, b % 2, :], ACT.Copy)\
                                .then_inc(s["bc_midcopy"], 1)
                    a.wait_ge(s["ones"], 2)
                    a.activation(log_small[:], log_small[:], ACT.Ln, bias=one[:]).then_inc(s["log_small"], 1)
                    for n, (c, hf) in enumerate(pieces):
                        if n >= 2:
                            a.wait_ge(s["kept"], n - 1)
                        a.activation(mag[:, n % 2, :], m.dt[:, c, half(hf)], ACT.Abs).then_inc(s["abs_ready"], 1)
                        a.wait_ge(s["abs_ready"], n + 1)
                        a.activation(mag[:, n % 2, :], mag[:, n % 2, :], ACT.Exp, scale=-1.0)\
                            .then_inc(s["exp_ready"], 1)
                        if n >= 1:
                            logarithm(a, n - 1)
                    logarithm(a, len(pieces) - 1)

                @block.vector
                def _(v):
                    v.memset(one[:], 1.0).then_inc(s["ones"], 1)
                    v.memset(log_small[:], SMALL).then_inc(s["ones"], 1)
                    ln.vector(v)
                    chain = Chain(v, s["step"])
                    for b in range(B):
                        o = 4 * (b % 2)
                        v.wait_ge(s["bc_hi"], b + 1)
                        if b >= 2:
                            v.wait_ge(s["bc_midcopy"], b - 1)
                            v.wait_ge(s["bc_lo"], b - 1)
                        v.tensor_tensor(rest[:, b % 2, :], bank[0:2 * DS, o + 1, :], m.bc[0:2 * DS, cols(b)],
                                        ALU.subtract).then_inc(s["bc_rest"], 1)
                        v.wait_ge(s["bc_mid"], b + 1)
                        v.wait_ge(s["bc_rest"], b + 1)
                        v.tensor_tensor(m.bc[4 * DS:6 * DS, cols(b)], rest[:, b % 2, :], mid[:, b % 2, :],
                                        ALU.subtract).then_inc(s["bc_lo"], 1)
                    v.wait_ge(s["dt_out"], B)
                    v.wait_ge(s["log_small"], 1)
                    for n in range(len(pieces) + 1):
                        if n < len(pieces):
                            c, hf = pieces[n]
                            e, p = mag[:, n % 2, :], series[:, n % 2, :]
                            v.wait_ge(s["exp_ready"], n + 1)
                            if n >= 2:
                                v.wait_ge(s["dt_ready"], n - 1)
                            v.tensor_scalar(big[:, n % 2, :], e, SMALL, None, ALU.max).then_inc(s["big_e"], 1)
                            chain.do(v.tensor_scalar(e, e, SMALL, None, ALU.min))
                            chain.do(v.tensor_scalar(p, e, SERIES[-1], None, ALU.mult))
                            for k in range(len(SERIES) - 2, 0, -1):
                                chain.do(v.scalar_tensor_tensor(p, p, SERIES[k], e, ALU.add, ALU.mult))
                            v.scalar_tensor_tensor(p, p, SERIES[0], e, ALU.add, ALU.mult).then_inc(s["series"], 1)
                            v.wait_ge(s["series"], n + 1)
                            v.scalar_tensor_tensor(p, m.dt[:, c, half(hf)], 0.0, p, ALU.max, ALU.add)\
                                .then_inc(s["kept"], 1)
                        if n >= 1:
                            c, hf = pieces[n - 1]
                            v.wait_ge(s["log_ready"], n)
                            v.wait_ge(s["kept"], n)
                            v.scalar_tensor_tensor(m.dt[:, c, half(hf)], big[:, (n - 1) % 2, :], log_small[:],
                                                   series[:, (n - 1) % 2, :], ALU.subtract, ALU.add)\
                                .then_inc(s["dt_ready"], 1)


class MambaCore:

    RA = 3

    def __init__(self, chip, m):
        self.chip, self.m = chip, m
        names = ("zero", "reps_b", "reps_c", "decay", "c_out", "input", "state", "read", "summed", "direct", "gated",
                 "projected", "added")
        self.s = {n: chip.sem("mc_" + n) for n in names}

    def sems(self):
        return list(self.s.values())

    def block(self):
        chip, m, s, RA = self.chip, self.m, self.s, self.RA
        nc, bank = chip.nc, chip.bank
        NU = DS * NCH
        with ExitStack() as ctx:
            sb = lambda n, shape, dt=F32: chip.sb(ctx, "mc_" + n, shape, dt)
            decay, inp, state = sb("decay", [P, RA, HB, S]), sb("inp", [P, RA, HT]), sb("state", [P, RA, HT])
            c_rep, read = sb("c_rep", [P, 2, HT]), sb("read", [P, 2, HT])
            y = sb("y", [P, NCH, HT])
            wide = lambda i: bank[:, i:i + 2, :].rearrange("p k q -> p (k q)")

            def replicate(pe, which, n, hf):
                for bb in range(HB):
                    last = pe.matmul(bank[:, 4 + 2 * which + bb, :], m.pick[:, which * DS + n, :],
                                     m.bc[:, bass.ds(hf * HT + bb * S, S)], start=True, stop=True)
                last.then_inc(s[("reps_b", "reps_c")[which]], 1)

            with nc.Block() as block:
                @block.tensor
                def _(pe):
                    with pe.Fori(0, 2) as hf:
                        replicate(pe, 0, 0, hf)
                        replicate(pe, 1, 0, hf)
                        for n in range(DS):
                            if n + 1 < DS:
                                pe.wait_ge(s["input"], hf * NU + NCH * (n + 1))
                                replicate(pe, 0, n + 1, hf)
                                pe.wait_ge(s["c_out"], hf * DS + n + 1)
                                replicate(pe, 1, n + 1, hf)
                            for c in range(NCH):
                                u = n * NCH + c
                                pe.wait_ge(s["read"], hf * NU + u + 1)
                                for bb in range(HB):
                                    last = pe.matmul(bank[:, 2 * c + bb, :], chip.ident[:],
                                                     read[:, u % 2, bb * S:(bb + 1) * S],
                                                     start=(n == 0), stop=(n == DS - 1))
                                last.then_inc(s["summed"], 1)
                        pe.wait_ge(s["gated"], NCH * hf + NCH)
                        for t in range(HT // P):
                            for c in range(NCH):
                                last = pe.matmul(bank[:, 4 + t // 4, (t % 4) * D:(t % 4 + 1) * D],
                                                 y[:, c, t * P:(t + 1) * P], m.out_w[:, c, :],
                                                 start=(c == 0), stop=(c == NCH - 1))
                        last.then_inc(s["projected"], 1)
                        pe.wait_ge(s["added"], hf + 1)

                @block.scalar
                def _(a):
                    a.wait_ge(s["zero"], 1)
                    with a.Fori(0, 2) as hf:
                        for n in range(DS):
                            for c in range(NCH):
                                u = n * NCH + c
                                if u >= RA:
                                    a.wait_ge(s["state"], hf * NU + u - RA + 1)
                                a.activation(decay[:, u % RA, :, 1:],
                                             m.dt[:, c, bass.ds(hf * HT, HT)].rearrange("p (b t) -> p b t", b=HB)[:, :, 1:],
                                             ACT.Exp, scale=m.a[:, c, n:n + 1]).then_inc(s["decay"], 1)
                            a.wait_ge(s["reps_c"], hf * DS + n + 1)
                            if n >= 2:
                                a.wait_ge(s["read"], hf * NU + NCH * (n - 1))
                            a.activation(c_rep[:, n % 2, :], wide(6), ACT.Copy).then_inc(s["c_out"], 1)
                        a.wait_ge(s["read"], hf * NU + NU)

                @block.vector
                def _(v):
                    v.memset(decay[:], 0.0).then_inc(s["zero"], 1)
                    with v.Fori(0, 2) as hf:
                        for n in range(DS):
                            v.wait_ge(s["reps_b"], hf * DS + n + 1)
                            for c in range(NCH):
                                u = n * NCH + c
                                if u >= RA:
                                    v.wait_ge(s["state"], hf * NU + u - RA + 1)
                                v.tensor_tensor(inp[:, u % RA, :], m.u[:, c, bass.ds(hf * HT, HT)], wide(4), ALU.mult)\
                                    .then_inc(s["input"], 1)
                            for c in range(NCH):
                                u = n * NCH + c
                                v.wait_ge(s["input"], hf * NU + u + 1)
                                v.wait_ge(s["decay"], hf * NU + u + 1)
                                if u >= RA:
                                    v.wait_ge(s["read"], hf * NU + u - RA + 1)
                                v.tensor_tensor_scan(state[:, u % RA, :],
                                                     decay[:, u % RA].rearrange("p b t -> p (b t)"), inp[:, u % RA, :],
                                                     0.0, ALU.mult, ALU.add).then_inc(s["state"], 1)
                        v.wait_ge(s["state"], hf * NU + NU)
                        for c in range(NCH):
                            v.wait_ge(s["summed"], hf * NU + NU)
                            v.scalar_tensor_tensor(y[:, c, :], m.xs[:, c, bass.ds(hf * HT, HT)],
                                                   m.col[:, 2 + 2 * NCH + c:3 + 2 * NCH + c], wide(2 * c),
                                                   ALU.mult, ALU.add).then_inc(s["direct"], 1)
                        v.wait_ge(s["projected"], hf + 1)
                        r = m.res[:, bass.ds(hf * (HT // P), HT // P), :].rearrange("p t d -> p (t d)")
                        v.tensor_tensor(r, r, wide(4), ALU.add).then_inc(s["added"], 1)

                @block.gpsimd
                def _(g):
                    with g.Fori(0, 2) as hf:
                        for n in range(DS):
                            g.wait_ge(s["c_out"], hf * DS + n + 1)
                            for c in range(NCH):
                                u = n * NCH + c
                                g.wait_ge(s["state"], hf * NU + u + 1)
                                if u >= 2:
                                    g.wait_ge(s["summed"], hf * NU + u - 1)
                                g.tensor_tensor(read[:, u % 2, :], state[:, u % RA, :], c_rep[:, n % 2, :], ALU.mult)\
                                    .then_inc(s["read"], 1)
                        for c in range(NCH):
                            g.wait_ge(s["direct"], hf * NCH + c + 1)
                            g.tensor_tensor(y[:, c, :], y[:, c, :], m.zs[:, c, bass.ds(hf * HT, HT)], ALU.mult)\
                                .then_inc(s["gated"], 1)


def mamba_out(chip, m):
    nc, dram = chip.nc, chip.dram
    with ExitStack() as ctx:
        w, b = chip.sb(ctx, "mo_w", [P, D]), chip.sb(ctx, "mo_b", [P, D])
        xn = chip.sb(ctx, "mo_xn", [P, NT, D])
        ln = LayerNorm(chip, ctx, "mo_ln", m.res, xn)
        here, step = chip.sem("mo_here"), chip.sem("mo_step")
        over_t = lambda row: row[:].unsqueeze(1).broadcast_to([P, NT, D])
        with nc.Block() as block:
            @block.sync
            def _(sp):
                sp.dma_start(w[:], dram["mb_fw"][0:1, :].broadcast_to([P, D])).then_inc(here, 16)
                sp.dma_start(b[:], dram["mb_fb"][0:1, :].broadcast_to([P, D])).then_inc(here, 16)

            @block.scalar
            def _(a):
                ln.scalar(a)

            @block.gpsimd
            def _(g):
                g.wait_ge(here, 32)
                g.tensor_tensor(chip.x[:], chip.x[:], over_t(b), ALU.add).then_inc(step, 1)

            @block.vector
            def _(v):
                ln.vector(v)
                v.wait_ge(here, 32)
                v.wait_ge(ln.ready, 1)
                v.wait_ge(step, 1)
                v.tensor_tensor(xn[:], xn[:], over_t(w), ALU.mult).then_inc(step, 1)
                v.wait_ge(step, 2)
                v.tensor_tensor(chip.x[:], chip.x[:], xn[:], ALU.add).then_inc(step, 1)


def more_mamba(r, a):
    g = lambda n: a["L1_attn_" + n]
    f = np.float32
    by_chunk = lambda v: v.reshape(NL, NCH, P, -1).transpose(0, 2, 1, 3).reshape(NL, P, -1)
    rows, n = np.arange(REP), np.arange(2 * DS)
    pick = np.repeat((rows[:, None] % (2 * DS) == n[None, :]).astype(f)[:, :, None], P, axis=2)
    r.update(
        mb_in=g("in_proj_w").transpose(0, 2, 1), mb_xp=by_chunk(g("x_proj_w").transpose(0, 2, 1)),
        mb_dtp=g("dt_proj_w").transpose(0, 2, 1), mb_out=by_chunk(g("out_proj_w").transpose(0, 2, 1)),
        mb_col=np.concatenate([g("norm_w")[:, :, None], g("norm_b")[:, :, None], by_chunk(g("conv_b")),
                               by_chunk(g("dt_proj_b")), by_chunk(g("D_param"))], axis=2),
        mb_a=by_chunk(g("A_log")), mb_conv=g("conv_w").transpose(0, 2, 1).reshape(NL, -1),
        mb_fw=g("fnorm_w").reshape(1, -1), mb_fb=g("fnorm_b").reshape(1, -1), pick=pick.reshape(REP, -1))


NC = 7
CW = 74
LAST_CW = S - (NC - 1) * CW
LANES = 32
STEPS = CTX + NC - 1
RING = 8
BIG = 1e30


def alignment(chip):
    nc = chip.nc
    dist_dram = nc.dram_tensor("dist_scratch", (CTX, B, S), F32, kind="Internal").ap()
    cost_dram = nc.dram_tensor("cost_scratch", (CTX + 1, B, S + 1), F32, kind="Internal").ap()
    with ExitStack() as stage:
        c = chip.sb(stage, "d_c", [CTX, B, D])
        big_row = chip.sb(stage, "d_big", [CTX + 1, B, S + 1])
        distances(chip, c, dist_dram, cost_dram, big_row)
        accumulate_costs(chip, dist_dram, cost_dram)
        trace_back(chip, c, cost_dram)


def distances(chip, c, dist_dram, cost_dram, big):
    nc, dram, bank = chip.nc, chip.dram, chip.bank
    with ExitStack() as ctx:
        sb = lambda n, shape, dt=F32: chip.sb(ctx, "dd_" + n, shape, dt)
        xn, xnt, sq = sb("xn", [P, NT, D]), sb("xnt", [P, TOK]), sb("sq", [P, TOK])
        ct, ones = sb("ct", [D, B * CTX]), sb("ones", [D, CTX])
        csq, cc = sb("csq", [CTX, B, D]), sb("cc", [CTX, B])
        d2, safe = sb("d2", [CTX, B, S]), sb("safe", [CTX, B, S])
        log, inv = sb("log", [CTX, B, S]), sb("inv", [CTX, B, S])
        root, err = sb("root", [CTX, B, S]), sb("err", [CTX, B, S])
        ln = LayerNorm(chip, ctx, "dd_ln", chip.x, xn)
        names = ("here", "ct_done", "ct_ready", "t_done", "xnt_ready", "sq_ready", "ones_set", "prod", "csqd", "ccd",
                 "d2d", "safed", "logd", "invd", "step", "dist", "stored", "big_set", "border")
        s = {n: chip.sem("dd_" + n) for n in names}
        with nc.Block() as block:
            @block.sync
            def _(sp):
                sp.dma_start(c[:], dram["ctx"].rearrange("b k d -> k b d")).then_inc(s["here"], 16)
                sp.wait_ge(s["big_set"], 1)
                sp.dma_start(cost_dram[:, :, :], big[:]).then_inc(s["border"], 16)
                sp.wait_ge(s["border"], 16)
                for b in range(B):
                    sp.wait_ge(s["dist"], b + 1)
                    sp.dma_start(dist_dram[:, b, :], root[:, b, :]).then_inc(s["stored"], 16)
                sp.wait_ge(s["stored"], 16 * B)

            @block.gpsimd
            def _(g):
                g.memset(big[:], BIG).then_inc(s["big_set"], 1)
                g.memset(ones[:], 1.0).then_inc(s["ones_set"], 1)

            @block.tensor
            def _(pe):
                pe.wait_ge(s["here"], 16)
                for b in range(B):
                    last = pe.transpose(bank[:, 4, b * CTX:(b + 1) * CTX], c[:, b, :], chip.ident[0:CTX, 0:CTX])
                last.then_inc(s["ct_done"], 1)
                pe.wait_ge(ln.ready, 1)
                feature_major(pe, chip, xn, s["t_done"])
                pe.wait_ge(s["ones_set"], 1)
                pe.wait_ge(s["ct_ready"], 1)
                for b in range(B):
                    cols = slice(b * S, (b + 1) * S)
                    pe.wait_ge(s["xnt_ready"], b + 1)
                    pe.wait_ge(s["sq_ready"], b + 1)
                    pe.matmul(bank[0:CTX, b, :], ones[:], sq[:, cols], start=True, stop=False)
                    pe.matmul(bank[0:CTX, b, :], ct[:, b * CTX:(b + 1) * CTX], xnt[:, cols], start=False, stop=True)\
                        .then_inc(s["prod"], 1)

            @block.scalar
            def _(a):
                a.wait_ge(s["ct_done"], 1)
                a.activation(ct[:], bank[:, 4, 0:B * CTX], ACT.Copy, scale=-2.0).then_inc(s["ct_ready"], 1)
                ln.scalar(a)
                for b in range(B):
                    cols = slice(b * S, (b + 1) * S)
                    a.wait_ge(s["t_done"], b + 1)
                    a.activation(xnt[:, cols], bank[:, b, :], ACT.Copy).then_inc(s["xnt_ready"], 1)
                    a.activation(sq[:, cols], bank[:, b, :], ACT.Square).then_inc(s["sq_ready"], 1)
                for b in range(B):
                    a.wait_ge(s["safed"], b + 1)
                    a.activation(log[:, b, :], safe[:, b, :], ACT.Ln).then_inc(s["logd"], 1)
                    a.wait_ge(s["logd"], b + 1)
                    a.activation(inv[:, b, :], log[:, b, :], ACT.Exp, scale=-0.5).then_inc(s["invd"], 1)

            @block.vector
            def _(v):
                v.wait_ge(s["here"], 16)
                v.tensor_tensor(csq[:], c[:], c[:], ALU.mult).then_inc(s["csqd"], 1)
                v.wait_ge(s["csqd"], 1)
                v.tensor_reduce(cc[:], csq[:], AX.X, ALU.add).then_inc(s["ccd"], 1)
                ln.vector(v)
                v.wait_ge(s["ccd"], 1)
                for b in range(B):
                    v.wait_ge(s["prod"], b + 1)
                    v.tensor_scalar(d2[:, b, :], bank[0:CTX, b, :], cc[:, b:b + 1], 0.0, ALU.add, ALU.max)\
                        .then_inc(s["d2d"], 1)
                    v.wait_ge(s["d2d"], b + 1)
                    v.tensor_scalar(safe[:, b, :], d2[:, b, :], 1e-18, None, ALU.max).then_inc(s["safed"], 1)
                chain = Chain(v, s["step"])
                for b in range(B):
                    v.wait_ge(s["invd"], b + 1)
                    chain.do(v.tensor_tensor(root[:, b, :], d2[:, b, :], inv[:, b, :], ALU.mult))
                    chain.do(v.tensor_tensor(err[:, b, :], root[:, b, :], root[:, b, :], ALU.mult))
                    chain.do(v.tensor_tensor(err[:, b, :], d2[:, b, :], err[:, b, :], ALU.subtract))
                    chain.do(v.tensor_tensor(err[:, b, :], err[:, b, :], inv[:, b, :], ALU.mult))
                    v.scalar_tensor_tensor(root[:, b, :], err[:, b, :], 0.5, root[:, b, :], ALU.mult, ALU.add)\
                        .then_inc(s["dist"], 1)


def accumulate_costs(chip, dist_dram, cost_dram):
    nc = chip.nc
    with ExitStack() as ctx:
        sb = lambda n, shape, dt=F32: chip.sb(ctx, "dc_" + n, shape, dt)
        dist, cost = sb("dist", [LANES, STEPS, CW]), sb("cost", [LANES, STEPS, CW])
        ring, least = sb("ring", [LANES, RING, CW + 1]), sb("least", [LANES, 2, CW])
        first = sb("first", [LANES, 1])
        names = ("set", "dist_set", "dist_here", "least", "row", "passed", "kept", "border", "stored")
        s = {n: chip.sem("dc_" + n) for n in names}
        shift = [(p - B) % LANES for p in range(LANES)]

        def above(v, j):
            v.tensor_tensor(least[:, (j + 1) % 2, :], ring[:, j, 1:CW + 1], ring[:, j, 0:CW], ALU.min)\
                .then_inc(s["least"], 1)

        def row_step(v, k, j, initial=None, last=False):
            at = k * RING + j
            v.wait_ge(s["least"], at + 1)
            if initial is None:
                v.wait_ge(s["passed"], at)
            if not isinstance(k, int) or k > 0:
                v.wait_ge(s["kept"], at - RING + 1)
            v.tensor_tensor_scan(ring[:, j, 1:CW + 1], least[:, j % 2, :], dist[:, at, :],
                                 ring[:, j, 0:1] if initial is None else initial, ALU.min, ALU.add)\
                .then_inc(s["row"], 1)
            v.wait_ge(s["row"], at + 1)
            if not last:
                above(v, j)
                v.stream_shuffle(ring[:, (j + 1) % RING, 0:1], ring[:, j, CW:CW + 1], shift).then_inc(s["passed"], 1)

        def keep_row(a, k, j):
            at = k * RING + j
            a.wait_ge(s["row"], at + 1)
            a.activation(cost[:, at, :], ring[:, j, 1:CW + 1], ACT.Copy).then_inc(s["kept"], 1)

        FULL = STEPS // RING
        with nc.Block() as block:
            @block.sync
            def _(sp):
                sp.wait_ge(s["dist_set"], 1)
                for c in range(NC):
                    w = CW if c < NC - 1 else LAST_CW
                    sp.dma_start(dist[c * B:(c + 1) * B, c:c + CTX, 0:w],
                                 dist_dram[:, :, c * CW:c * CW + w].rearrange("i b j -> b i j"))\
                        .then_inc(s["dist_here"], 16)
                sp.wait_ge(s["kept"], STEPS)
                for c in range(NC):
                    w = CW if c < NC - 1 else LAST_CW
                    sp.dma_start(cost_dram[1:CTX + 1, :, 1 + c * CW:1 + c * CW + w].rearrange("i b j -> b i j"),
                                 cost[c * B:(c + 1) * B, c:c + CTX, 0:w]).then_inc(s["stored"], 16)
                sp.wait_ge(s["stored"], 16 * NC)

            @block.gpsimd
            def _(g):
                g.memset(dist[:], BIG).then_inc(s["dist_set"], 1)

            @block.vector
            def _(v):
                v.memset(ring[:], BIG).then_inc(s["set"], 1)
                v.memset(first[:], BIG).then_inc(s["set"], 1)
                v.wait_ge(s["set"], 2)
                v.memset(first[0:B, :], 0.0).then_inc(s["set"], 1)
                v.wait_ge(s["set"], 3)
                v.wait_ge(s["dist_here"], 16 * NC)
                above(v, RING - 1)
                for j in range(RING):
                    row_step(v, 0, j, initial=first[:] if j == 0 else None)
                with v.Fori(1, FULL) as k:
                    for j in range(RING):
                        row_step(v, k, j)
                for j in range(STEPS - FULL * RING):
                    row_step(v, FULL, j, last=(FULL * RING + j == STEPS - 1))

            @block.scalar
            def _(a):
                with a.Fori(0, FULL) as k:
                    for j in range(RING):
                        keep_row(a, k, j)
                for j in range(STEPS - FULL * RING):
                    keep_row(a, FULL, j)


def trace_back(chip, c, cost_dram):
    nc, dram, bank = chip.nc, chip.dram, chip.bank
    UNROLL = 19
    assert (CTX - 1) % UNROLL == 0
    with ExitStack() as ctx:
        sb = lambda n, shape, dt=F32: chip.sb(ctx, "db_" + n, shape, dt)
        here_cost, above = sb("cur", [CTX, B, S + 1]), sb("above", [CTX, B, S + 1])
        leave, diag = sb("leave", [CTX, B, S]), sb("diag", [CTX, B, S])
        start = sb("start", [CTX, B, S])
        follow16 = sb("follow16", [CTX, B, S], F16)
        column = sb("column", [P, S])
        table = sb("table", [B, CTX, S], F16)
        end, hit = sb("end", [B, CTX]), sb("hit", [B, 2, S])
        endt, startt, picked = sb("endt", [CTX, B]), sb("startt", [CTX, B]), sb("picked", [CTX, B, S])
        names = ("here", "colh", "step", "table_ready", "table_here", "end_set", "hop", "end_done", "onpath", "spread", "pick",
                 "scanned")
        s = {n: chip.sem("db_" + n) for n in names}
        with nc.Block() as block:
            @block.sync
            def _(sp):
                sp.dma_start(here_cost[:], cost_dram[1:CTX + 1, :, :]).then_inc(s["here"], 16)
                sp.dma_start(above[:], cost_dram[0:CTX, :, :]).then_inc(s["here"], 16)
                sp.dma_start(column[:], dram["column"][0:1, :].broadcast_to([P, S])).then_inc(s["here"], 16)
                for b in range(B):
                    sp.wait_ge(s["table_ready"], b + 1)
                    sp.dma_start(table[b:b + 1, :, :], follow16[:, b, :]).then_inc(s["table_here"], 16)

            @block.vector
            def _(v):
                chain = Chain(v, s["step"])
                col = column[0:CTX, :].unsqueeze(1).broadcast_to([CTX, B, S])
                up, up_left, left = above[:, :, 1:S + 1], above[:, :, 0:S], here_cost[:, :, 0:S]
                v.wait_ge(s["here"], 48)
                chain.do(v.tensor_tensor(leave[:], up, up_left, ALU.min))
                v.tensor_tensor(leave[:], leave[:], left, ALU.is_le).then_inc(s["step"], 1)
                v.tensor_tensor(diag[:], up_left, up, ALU.is_le).then_inc(s["step"], 1)
                chain.at += 2
                v.wait_ge(s["step"], chain.at)
                v.tensor_tensor(picked[:], col, diag[:], ALU.subtract).then_inc(s["step"], 1)
                chain.at += 1
                v.wait_ge(s["step"], chain.at)
                v.tensor_tensor(diag[:], picked[:], leave[:], ALU.mult).then_inc(s["step"], 1)
                chain.at += 1
                v.wait_ge(s["step"], chain.at)
                for b in range(B):
                    v.tensor_tensor_scan(follow16[:, b, :], diag[:, b, :], diag[:, b, :], 0.0, ALU.max, ALU.max)\
                        .then_inc(s["table_ready"], 1)
                v.tensor_tensor(leave[:], col, leave[:], ALU.mult).then_inc(s["step"], 1)
                chain.at += 1
                v.memset(end[:, CTX - 1:CTX], float(S)).then_inc(s["end_set"], 1)
                v.wait_ge(s["step"], chain.at)
                for b in range(B):
                    v.tensor_tensor_scan(start[:, b, :], leave[:, b, :], leave[:, b, :], 0.0, ALU.max, ALU.max)\
                        .then_inc(s["scanned"], 1)
                v.wait_ge(s["end_set"], 1)
                v.wait_ge(s["table_here"], 16 * B)
                with v.Fori(0, (CTX - 1) // UNROLL) as k:
                    for j in range(UNROLL):
                        i = (CTX - 1 - j) - k * UNROLL
                        v.scalar_tensor_tensor(hit[:, j % 2, :], column[0:B, :], end[:, bass.ds(i, 1)], table[:, i, :],
                                               ALU.is_equal, ALU.mult, accum_out=end[:, bass.ds(i - 1, 1)])\
                            .then_inc(s["hop"], 1)
                        v.wait_ge(s["hop"], k * UNROLL + j + 1)
                v.wait_ge(s["end_done"], 1)
                v.tensor_copy(endt[:], bank[0:CTX, 0, 0:B]).then_inc(s["step"], 1)
                chain.at += 1
                v.wait_ge(s["step"], chain.at)
                v.wait_ge(s["scanned"], B)
                for b in range(B):
                    v.scalar_tensor_tensor(picked[:, b, :], column[0:CTX, :], endt[:, b:b + 1], start[:, b, :],
                                           ALU.is_equal, ALU.mult, accum_out=startt[:, b:b + 1]).then_inc(s["step"], 1)
                    v.tensor_scalar(diag[:, b, :], column[0:CTX, :], endt[:, b:b + 1], None, ALU.is_le)\
                        .then_inc(s["step"], 1)
                chain.at += 2 * B
                v.wait_ge(s["step"], chain.at)
                for b in range(B):
                    v.scalar_tensor_tensor(picked[:, b, :], column[0:CTX, :], startt[:, b:b + 1], diag[:, b, :],
                                           ALU.is_ge, ALU.mult).then_inc(s["onpath"], 1)
                for b in range(B):
                    v.wait_ge(s["spread"], b + 1)
                    xb = chip.x[:, b * ST:(b + 1) * ST, :].rearrange("p t d -> p (t d)")
                    v.tensor_tensor(xb, xb, bank[:, 4 + b, :], ALU.add).then_inc(s["pick"], 1)

            @block.tensor
            def _(pe):
                pe.wait_ge(s["hop"], CTX - 1)
                pe.wait_ge(s["end_set"], 1)
                pe.transpose(bank[0:CTX, 0, 0:B], end[:], chip.ident[0:B, 0:B]).then_inc(s["end_done"], 1)
                for b in range(B):
                    pe.wait_ge(s["onpath"], b + 1)
                    for j in range(ST):
                        last = pe.matmul(bank[:, 4 + b, j * D:(j + 1) * D], picked[:, b, j * P:(j + 1) * P], c[:, b, :],
                                         start=True, stop=True)
                    last.then_inc(s["spread"], 1)


def more_alignment(r, a):
    r["column"] = np.arange(1, S + 1, dtype=np.float32).reshape(1, -1)


INNER = 512
NI = INNER // P
ROUND = 1.5 * 2.0 ** 23


def ternary_feed_forward(chip):
    with ExitStack() as stage:
        wg = chip.sb(stage, "t_wg", [P, INNER], BF16)
        wu = chip.sb(stage, "t_wu", [P, INNER], BF16)
        wd = chip.sb(stage, "t_wd", [P, NI, D], BF16)
        unit = chip.sb(stage, "t_unit", [P, 3])
        identb = chip.sb(stage, "t_identb", [P, P], BF16)
        xq = chip.sb(stage, "t_xq", [P, NT, D], BF16)
        step_x = chip.sb(stage, "t_step_x", [P, NT])
        quantize_inputs(chip, (wg, wu, wd), unit, identb, xq, step_x)
        feed_forward(chip, (wg, wu, wd), unit, identb, xq, step_x)


def quantize_inputs(chip, weights, unit, identb, xq, step_x):
    nc, dram, bank = chip.nc, chip.dram, chip.bank
    names = ("t_wg", "t_wu", "t_wd")
    with ExitStack() as ctx:
        sb = lambda n, shape, dt=F32: chip.sb(ctx, "q_" + n, shape, dt)
        xn, scaled = sb("xn", [P, NT, D]), sb("scaled", [P, NT, D])
        raw = [sb("raw" + n, [P, INNER]) for n in names]
        absum, ones, mean, scale = sb("absum", [P, 3]), sb("ones", [P, P]), sb("mean", [P, 3]), sb("scale", [P, 3])
        peak, rpeak, scale_x = sb("peak", [P, NT]), sb("rpeak", [P, NT]), sb("scale_x", [P, NT])
        ln = LayerNorm(chip, ctx, "q_ln", chip.x, xn)
        here, ones_set, summed, step = (chip.sem("q_" + n) for n in ("here", "ones_set", "summed", "step"))
        idb = chip.sem("q_idb")
        with nc.Block() as block:
            @block.sync
            def _(sp):
                for n, t in zip(names, raw):
                    sp.dma_start(t[:], dram[n][:, :]).then_inc(here, 16)

            @block.gpsimd
            def _(g):
                g.memset(ones[:], 1.0).then_inc(ones_set, 1)
                g.tensor_copy(identb[:], chip.ident[:]).then_inc(idb, 1)

            @block.tensor
            def _(pe):
                pe.wait_ge(ones_set, 1)
                pe.wait_ge(step, 3)
                pe.matmul(bank[:, 0, 0:3], ones[:], absum[:], start=True, stop=True).then_inc(summed, 1)

            @block.scalar
            def _(a):
                ln.scalar(a)

            @block.vector
            def _(v):
                chain = Chain(v, step)
                v.wait_ge(here, 48)
                for n in range(3):
                    v.tensor_reduce(absum[:, n:n + 1], raw[n][:], AX.X, ALU.add, apply_absolute_value=True)\
                        .then_inc(step, 1)
                chain.at = 3
                ln.vector(v)
                v.wait_ge(summed, 1)
                chain.do(v.tensor_scalar(mean[:], bank[:, 0, 0:3], 1.0 / (INNER * D), 1e-5, ALU.mult, ALU.max))
                chain.do(v.reciprocal(scale[:], mean[:]))
                v.reciprocal(unit[:], scale[:]).then_inc(step, 1)
                chain.at += 1
                for n in range(3):
                    v.tensor_scalar(raw[n][:], raw[n][:], scale[:, n:n + 1], ROUND, ALU.mult, ALU.add).then_inc(step, 1)
                chain.at += 3
                v.wait_ge(step, chain.at)
                for n in range(3):
                    v.tensor_scalar(raw[n][:], raw[n][:], ROUND, 1.0, ALU.subtract, ALU.min).then_inc(step, 1)
                chain.at += 3
                v.wait_ge(step, chain.at)
                for n in range(3):
                    w = weights[n][:] if n < 2 else weights[n][:].rearrange("p i o -> p (i o)")
                    v.tensor_scalar(w, raw[n][:], -1.0, None, ALU.max).then_inc(step, 1)
                chain.at += 3
                v.wait_ge(ln.ready, 1)
                chain.do(v.tensor_reduce(peak[:], xn[:], AX.X, ALU.max, apply_absolute_value=True))
                chain.do(v.tensor_scalar(peak[:], peak[:], 1e-5, None, ALU.max))
                chain.do(v.reciprocal(rpeak[:], peak[:]))
                chain.do(v.tensor_scalar(scale_x[:], rpeak[:], 127.0, None, ALU.mult))
                v.reciprocal(step_x[:], scale_x[:]).then_inc(step, 1)
                chain.at += 1
                chain.do(v.tensor_tensor(scaled[:], xn[:], scale_x[:].unsqueeze(2).broadcast_to([P, NT, D]), ALU.mult))
                chain.do(v.tensor_scalar(scaled[:], scaled[:], ROUND, -ROUND, ALU.add, ALU.add))
                chain.do(v.tensor_scalar(xq[:], scaled[:], 127.0, -128.0, ALU.min, ALU.max))


def feed_forward(chip, weights, unit, identb, xq, step_x):
    nc, bank = chip.nc, chip.bank
    wg, wu, wd = weights
    with ExitStack() as ctx:
        sb = lambda n, shape, dt=F32: chip.sb(ctx, "f_" + n, shape, dt)
        per_gate, per_up = sb("per_gate", [P, NT]), sb("per_up", [P, NT])
        xt, hqt = sb("xt", [P, 2, P], BF16), sb("hqt", [P, 2, NI, P], BF16)
        act, h, hs = sb("act", [P, 2, INNER]), sb("h", [P, 2, INNER]), sb("hs", [P, 2, INNER])
        hq = sb("hq", [P, 2, INNER], BF16)
        peak, rpeak, scale = sb("peak", [P, NT]), sb("rpeak", [P, NT]), sb("scale", [P, NT])
        per_down = sb("per_down", [P, NT])
        names = ("per", "xt_done", "xt_out", "gated", "acted", "joined", "hq_ready", "hqt_done", "hqt_out", "down",
                 "added", "peaked", "clipped", "recip", "scaled", "rounded", "stepd")
        s = {n: chip.sem("f_" + n) for n in names}
        xt_ps = lambda t: bank[:, 4, :].bitcast(BF16)[:, (t % 2) * 512:(t % 2) * 512 + P]
        hqt_ps = lambda t: bank[:, 5, :].bitcast(BF16)[:, (t % 2) * 512:(t % 2) * 512 + INNER]
        with nc.Block() as block:
            @block.tensor
            def _(pe):
                for n in range(NT + 2):
                    if n < NT:
                        t = n
                        if t >= 2:
                            pe.wait_ge(s["xt_out"], t - 1)
                        pe.transpose(xt_ps(t), xq[:, t, :], identb[:]).then_inc(s["xt_done"], 1)
                        pe.wait_ge(s["xt_out"], t + 1)
                        if t >= 2:
                            pe.wait_ge(s["joined"], t - 1)
                        pe.matmul(bank[:, 2 * (t % 2), :], xt[:, t % 2, :], wg[:], start=True, stop=True)
                        pe.matmul(bank[:, 2 * (t % 2) + 1, :], xt[:, t % 2, :], wu[:], start=True, stop=True)\
                            .then_inc(s["gated"], 1)
                    if n >= 2:
                        t = n - 2
                        pe.wait_ge(s["hq_ready"], t + 1)
                        if t >= 2:
                            pe.wait_ge(s["hqt_out"], t - 1)
                        for i in range(NI):
                            last = pe.transpose(hqt_ps(t)[:, i * P:(i + 1) * P], hq[:, t % 2, i * P:(i + 1) * P], identb[:])
                        last.then_inc(s["hqt_done"], 1)
                        pe.wait_ge(s["hqt_out"], t + 1)
                        if t >= 2:
                            pe.wait_ge(s["added"], t - 1)
                        for i in range(NI):
                            last = pe.matmul(bank[:, 6 + t % 2, 0:D], hqt[:, t % 2, i, :], wd[:, i, :],
                                             start=(i == 0), stop=(i == NI - 1))
                        last.then_inc(s["down"], 1)

            @block.scalar
            def _(a):
                a.wait_ge(s["per"], 2)
                for n in range(NT + 2):
                    if n < NT:
                        t = n
                        a.wait_ge(s["xt_done"], t + 1)
                        if t >= 2:
                            a.wait_ge(s["gated"], t - 1)
                        a.activation(xt[:, t % 2, :], xt_ps(t), ACT.Copy).then_inc(s["xt_out"], 1)
                        a.wait_ge(s["gated"], t + 1)
                        if t >= 2:
                            a.wait_ge(s["joined"], t - 1)
                        a.activation(act[:, t % 2, :], bank[:, 2 * (t % 2), :], ACT.Silu, scale=per_gate[:, t:t + 1])\
                            .then_inc(s["acted"], 1)
                    if n >= 2:
                        t = n - 2
                        a.wait_ge(s["hqt_done"], t + 1)
                        if t >= 2:
                            a.wait_ge(s["down"], t - 1)
                        a.activation(hqt[:, t % 2].rearrange("p i q -> p (i q)"), hqt_ps(t), ACT.Copy)\
                            .then_inc(s["hqt_out"], 1)

            @block.vector
            def _(v):
                v.tensor_scalar(per_gate[:], step_x[:], unit[:, 0:1], None, ALU.mult).then_inc(s["per"], 1)
                v.tensor_scalar(per_up[:], step_x[:], unit[:, 1:2], None, ALU.mult).then_inc(s["per"], 1)
                v.wait_ge(s["per"], 2)
                for n in range(NT + 3):
                    if n < NT:
                        t = n
                        v.wait_ge(s["acted"], t + 1)
                        if t >= 2:
                            v.wait_ge(s["scaled"], t - 1)
                        v.scalar_tensor_tensor(h[:, t % 2, :], bank[:, 2 * (t % 2) + 1, :], per_up[:, t:t + 1],
                                               act[:, t % 2, :], ALU.mult, ALU.mult).then_inc(s["joined"], 1)
                        v.wait_ge(s["joined"], t + 1)
                        v.tensor_reduce(peak[:, t:t + 1], h[:, t % 2, :], AX.X, ALU.max, apply_absolute_value=True)\
                            .then_inc(s["peaked"], 1)
                        v.wait_ge(s["peaked"], t + 1)
                        v.tensor_scalar(peak[:, t:t + 1], peak[:, t:t + 1], 1e-5, 1.0 / 127.0, ALU.max, ALU.mult)\
                            .then_inc(s["clipped"], 1)
                        v.wait_ge(s["clipped"], t + 1)
                        v.reciprocal(rpeak[:, t:t + 1], peak[:, t:t + 1]).then_inc(s["recip"], 1)
                        v.tensor_scalar(per_down[:, t:t + 1], peak[:, t:t + 1], unit[:, 2:3], None, ALU.mult)\
                            .then_inc(s["stepd"], 1)
                        v.wait_ge(s["recip"], t + 1)
                        if t >= 2:
                            v.wait_ge(s["rounded"], t - 1)
                        v.tensor_scalar(hs[:, t % 2, :], h[:, t % 2, :], rpeak[:, t:t + 1], ROUND, ALU.mult, ALU.add)\
                            .then_inc(s["scaled"], 1)
                        v.wait_ge(s["scaled"], t + 1)
                        v.tensor_scalar(hs[:, t % 2, :], hs[:, t % 2, :], ROUND, 127.0, ALU.subtract, ALU.min)\
                            .then_inc(s["rounded"], 1)
                        v.wait_ge(s["rounded"], t + 1)
                        if t >= 2:
                            v.wait_ge(s["hqt_done"], t - 1)
                        v.tensor_scalar(hq[:, t % 2, :], hs[:, t % 2, :], -128.0, None, ALU.max)\
                            .then_inc(s["hq_ready"], 1)
                    if n >= 3:
                        t = n - 3
                        v.wait_ge(s["down"], t + 1)
                        v.scalar_tensor_tensor(chip.x[:, t, :], bank[:, 6 + t % 2, 0:D], per_down[:, t:t + 1],
                                               chip.x[:, t, :], ALU.mult, ALU.add).then_inc(s["added"], 1)


def more_ternary(r, a):
    r.update(t_wg=a["L1_ffn_w_gate"].T, t_wu=a["L1_ffn_w_up"].T,
             t_wd=a["L1_ffn_w_down"].T.reshape(NI, P, D).transpose(1, 0, 2).reshape(P, INNER))


def self_attention_stage(chip):
    with ExitStack() as stage:
        mixed = chip.sb(stage, "mixed", [P, NT, D])
        with ExitStack() as inner:
            values = chip.sb(inner, "values", [P, NT, D])
            qparts = chip.sb(inner, "qparts", [P, 3, TOK], BF16)
            kparts = chip.sb(inner, "kparts", [P, 3, TOK], BF16)
            self_attention_inputs(chip, qparts, kparts, values)
            self_attention(chip, qparts, kparts, values, mixed)
        project_and_add(chip, "a_out", mixed, "wo")


STAGES = (self_attention_stage, cross_attention, experts, mamba, alignment, ternary_feed_forward)


def build(nc, dram, out, stages=STAGES):
    with ExitStack() as ctx:
        chip = Chip(nc, ctx, dram)
        for stage in stages:
            chip.run(stage)
        with nc.semaphore("stored") as stored, nc.Block() as block:
            @block.sync
            def _(sp):
                sp.dma_start(out.rearrange("b (t p) d -> p (b t) d", p=P), chip.x[:]).then_inc(stored, 16)
                sp.wait_ge(stored, 16)


def laid_out(a):
    c = np.ascontiguousarray
    f = np.float32
    by_d = np.arange(D).reshape(H, HD).T.reshape(-1)
    swap = by_d.reshape(HD, H)[np.arange(HD) ^ 1].reshape(-1)
    half = np.arange(HD // 2, dtype=f)
    inv_freq = (f(10000.0) ** (-(half * f(2.0) / f(HD)))).astype(f)
    ang = np.arange(S, dtype=f)[:, None] * inv_freq[None, :]
    of_row = np.arange(D) // H
    cos, sin = np.cos(ang).astype(f).T[of_row // 2], np.sin(ang).astype(f).T[of_row // 2]
    sin = np.where((of_row % 2 == 0)[:, None], -sin, sin)
    k = np.arange(P)
    r = {
        "x": a["x"], "ctx": a["ctx_1024"],
        "ident": np.eye(P, dtype=f),
        "keep": np.concatenate([np.ones((P, 2 * P), f)] + 2 * [(k[:, None] <= k[None, :]).astype(f)], 1),
        "rope_cos": cos, "rope_sin": sin,
        "wq": a["L0_attn_w_q"][by_d].T, "wq_swap": a["L0_attn_w_q"][swap].T,
        "wk": a["L0_attn_w_k"][by_d].T, "wk_swap": a["L0_attn_w_k"][swap].T,
        "wv": a["L0_attn_w_v"].T, "wo": a["L0_attn_w_o"].T,
    }
    for part in (more, more_experts, more_mamba, more_alignment, more_ternary):
        part(r, a)
    return {n: c(v) for n, v in r.items()}


def kernel(**inputs):
    import concourse.bacc as bacc
    from concourse.bass_utils import run_bass_kernel_spmd

    arrays = laid_out({n: np.asarray(v) for n, v in inputs.items()})
    nc = bacc.Bacc("TRN2", target_bir_lowering=False, num_devices=1)
    dram = {n: nc.dram_tensor("in_" + n, a.shape, mybir.dt.from_np(a.dtype), kind="ExternalInput").ap()
            for n, a in arrays.items()}
    out = nc.dram_tensor("out", (B, S, D), F32, kind="ExternalOutput").ap()
    build(nc, dram, out)
    return run_bass_kernel_spmd(nc, [{"in_" + n: a for n, a in arrays.items()}], core_ids=[0]).results[0]["out"]
```

```python
from contextlib import ExitStack

import numpy as np
import concourse.bass as bass
from concourse import mybir

F32 = mybir.dt.float32
BF16 = mybir.dt.bfloat16
F16 = mybir.dt.float16
U32 = mybir.dt.uint32
ALU = mybir.AluOpType
ACT = mybir.ActivationFunctionType
AX = mybir.AxisListType

P = 128
D = 128
B, S = 4, 512
TOK = B * S
NT = TOK // P
ST = S // P
H, HD = 16, 8
CTX = 77
LN_EPS = 1e-5


class Chip:

    def __init__(self, nc, ctx, dram):
        self.nc, self.ctx, self.dram = nc, ctx, dram
        nc.disable_value_cache = True
        self.sem_ctx, self.stage_sems = ctx, []
        self.x = self.sb(ctx, "x_resid", [P, NT, D])
        self.ident = self.sb(ctx, "ident", [P, P])
        self.eps = self.sb(ctx, "eps_col", [P, 1])
        self.bank = ctx.enter_context(nc.psum_tensor("bank", [P, 8, 512], F32))

    def sb(self, ctx, name, shape, dt=F32):
        return ctx.enter_context(self.nc.sbuf_tensor(name, shape, dt))

    def sem(self, name):
        sem = self.sem_ctx.enter_context(self.nc.semaphore(name))
        self.stage_sems.append(sem)
        return sem

    def clear(self, sems):
        with self.nc.Block() as block:
            for n, engine in enumerate((block.vector, block.scalar, block.gpsimd, block.sync, block.tensor)):
                @engine
                def _(e, n=n):
                    for sem in sems[n::5]:
                        e.sem_clear(sem)

    def run(self, stage, *args):
        with ExitStack() as self.sem_ctx:
            self.stage_sems = []
            stage(self, *args)
            self.clear(self.stage_sems)


class Chain:

    def __init__(self, engine, done, at=0):
        self.engine, self.done, self.at = engine, done, at

    def do(self, instruction):
        self.at += 1
        instruction.then_inc(self.done, 1)
        self.engine.wait_ge(self.done, self.at)


class LayerNorm:

    def __init__(self, chip, ctx, name, src, dst):
        self.src, self.dst, self.chip, self.tiles = src, dst, chip, src.shape[1]
        sb = lambda n, shape: chip.sb(ctx, f"{name}_{n}", shape)
        n = self.tiles
        self.stats, self.mean = sb("stats", [P, n, 6]), sb("mean", [P, n])
        self.var, self.tmp = sb("var", [P, n]), sb("tmp", [P, n])
        self.log, self.rstd = sb("log", [P, n]), sb("rstd", [P, n])
        self.stats_done = chip.sem(f"{name}_stats_done")
        self.step_done = chip.sem(f"{name}_step_done")
        self.var_ready = chip.sem(f"{name}_var_ready")
        self.log_ready = chip.sem(f"{name}_log_ready")
        self.rough_ready = chip.sem(f"{name}_rough_ready")
        self.ready = chip.sem(f"{name}_ready")

    def sems(self):
        return [self.stats_done, self.step_done, self.var_ready, self.log_ready, self.rough_ready, self.ready]

    def vector(self, v):
        self.statistics(v)
        self.normalise(v)

    def statistics(self, v):
        st, mean, var, tmp = self.stats, self.mean, self.var, self.tmp
        for t in range(self.tiles):
            v.bn_stats(st[:, t, :], self.src[:, t, :]).then_inc(self.stats_done, 1)
        v.wait_ge(self.stats_done, self.tiles)
        v.tensor_tensor(mean[:], st[:, :, 1], st[:, :, 4], ALU.add).then_inc(self.step_done, 1)
        v.tensor_tensor(tmp[:], st[:, :, 1], st[:, :, 4], ALU.subtract).then_inc(self.step_done, 1)
        v.tensor_tensor(var[:], st[:, :, 2], st[:, :, 5], ALU.add).then_inc(self.step_done, 1)
        v.wait_ge(self.step_done, 3)
        v.tensor_scalar(mean[:], mean[:], 0.5, None, ALU.mult).then_inc(self.step_done, 1)
        v.scalar_tensor_tensor(tmp[:], tmp[:], 0.25, tmp[:], ALU.mult, ALU.mult).then_inc(self.step_done, 1)
        v.tensor_scalar(var[:], var[:], 1.0 / D, LN_EPS, ALU.mult, ALU.add).then_inc(self.step_done, 1)
        v.wait_ge(self.step_done, 6)
        v.tensor_tensor(var[:], var[:], tmp[:], ALU.add).then_inc(self.var_ready, 1)
        v.tensor_tensor(self.dst[:], self.src[:], mean[:].unsqueeze(2).broadcast_to([P, self.tiles, D]),
                        ALU.subtract).then_inc(self.step_done, 1)

    def normalise(self, v):
        var, tmp, rstd = self.var, self.tmp, self.rstd
        chain = Chain(v, self.step_done, at=7)
        v.wait_ge(self.rough_ready, 1)
        chain.do(v.tensor_tensor(tmp[:], rstd[:], rstd[:], ALU.mult))
        chain.do(v.scalar_tensor_tensor(tmp[:], tmp[:], -0.5, var[:], ALU.mult, ALU.mult))
        chain.do(v.scalar_tensor_tensor(rstd[:], tmp[:], 1.5, rstd[:], ALU.add, ALU.mult))
        v.tensor_tensor(self.dst[:], self.dst[:], rstd[:].unsqueeze(2).broadcast_to([P, self.tiles, D]),
                        ALU.mult).then_inc(self.ready, 1)

    def scalar(self, a):
        a.wait_ge(self.var_ready, 1)
        a.activation(self.log[:], self.var[:], ACT.Ln).then_inc(self.log_ready, 1)
        a.wait_ge(self.log_ready, 1)
        a.activation(self.rstd[:], self.log[:], ACT.Exp, scale=-0.5).then_inc(self.rough_ready, 1)


def feature_major(eng, chip, src, per_bank_done, banks=range(4)):
    for g, bank in enumerate(banks):
        for j in range(ST):
            last = eng.transpose(chip.bank[:, bank, j * P:(j + 1) * P], src[:, g * ST + j, :], chip.ident[:])
        last.then_inc(per_bank_done, 1)


def self_attention_inputs(chip, qstack_src, kstack_src, values):
    nc, dram, bank = chip.nc, chip.dram, chip.bank
    with ExitStack() as ctx:
        xn = chip.sb(ctx, "a_xn", [P, NT, D])
        xnt = chip.sb(ctx, "a_xnt", [P, TOK])
        names = ("wq", "wq_swap", "wk", "wk_swap", "wv")
        w = {n: chip.sb(ctx, "a_" + n, [D, D]) for n in names}
        cos, sin = chip.sb(ctx, "a_cos", [P, S]), chip.sb(ctx, "a_sin", [P, S])
        prod_cos, prod_sin = chip.sb(ctx, "a_pc", [P, 2, S]), chip.sb(ctx, "a_ps", [P, 2, S])
        turned, rest = chip.sb(ctx, "a_turned", [P, 2, S]), chip.sb(ctx, "a_rest", [P, 2, S])
        ln = LayerNorm(chip, ctx, "a_ln", chip.x, xn)
        x_here, w_here = chip.sem("a_x_here"), chip.sem("a_w_here")
        t_done, xnt_ready = chip.sem("a_t_done"), chip.sem("a_xnt_ready")
        qk_done, qk_read = chip.sem("a_qk_done"), chip.sem("a_qk_read")
        v_done = chip.sem("a_v_done")
        prods, turned_ready = chip.sem("a_prods"), chip.sem("a_turned_ready")
        part1, rest_ready = chip.sem("a_part1"), chip.sem("a_rest_ready")
        part2, part3 = chip.sem("a_part2"), chip.sem("a_part3")
        v_out = chip.sem("a_v_out")
        items = [(b, which) for b in range(B) for which in range(2)]
        def remainder(v, n):
            b, which = items[n]
            parts = kstack_src if which else qstack_src
            v.wait_ge(part1, n + 1)
            v.wait_ge(turned_ready, n + 1)
            if n >= 2:
                v.wait_ge(part2, n - 1)
                v.wait_ge(part3, n - 1)
            v.tensor_tensor(rest[:, n % 2, :], turned[:, n % 2, :], parts[:, 0, b * S:(b + 1) * S],
                            ALU.subtract).then_inc(rest_ready, 1)

        with nc.Block() as block:
            @block.sync
            def _(sp):
                sp.dma_start(chip.x[:], dram["x"].rearrange("b (t p) d -> p (b t) d", p=P)).then_inc(x_here, 16)
                sp.dma_start(chip.ident[:], dram["ident"][:, :]).then_inc(w_here, 16)
                for n in names:
                    sp.dma_start(w[n][:], dram[n][:, :]).then_inc(w_here, 16)
                sp.dma_start(cos[:], dram["rope_cos"][:, :]).then_inc(w_here, 16)
                sp.dma_start(sin[:], dram["rope_sin"][:, :]).then_inc(w_here, 16)

            @block.vector
            def _(v):
                v.wait_ge(x_here, 16)
                ln.vector(v)
                v.wait_ge(w_here, 16 * 8)
                for n, (b, which) in enumerate(items):
                    v.wait_ge(qk_done, n + 1)
                    s = n % 2
                    if n >= 2:
                        v.wait_ge(turned_ready, n - 1)
                    v.tensor_tensor(prod_cos[:, s, :], bank[:, 4 + 2 * which, :], cos[:], ALU.mult).then_inc(prods, 1)
                    v.tensor_tensor(prod_sin[:, s, :], bank[:, 5 + 2 * which, :], sin[:], ALU.mult)\
                        .then_inc(qk_read, 1)
                    v.wait_ge(prods, n + 1)
                    v.wait_ge(qk_read, n + 1)
                    if n >= 2:
                        v.wait_ge(part1, n - 1)
                        v.wait_ge(rest_ready, n - 1)
                    v.tensor_tensor(turned[:, s, :], prod_cos[:, s, :], prod_sin[:, s, :], ALU.add)\
                        .then_inc(turned_ready, 1)
                    if n >= 1:
                        remainder(v, n - 1)
                remainder(v, len(items) - 1)

            @block.scalar
            def _(a):
                ln.scalar(a)
                for g in range(B):
                    a.wait_ge(t_done, g + 1)
                    a.activation(xnt[:, g * S:(g + 1) * S], bank[:, g, :], ACT.Copy).then_inc(xnt_ready, 1)
                for n, (b, which) in enumerate(items):
                    parts = kstack_src if which else qstack_src
                    cols = slice(b * S, (b + 1) * S)
                    a.wait_ge(turned_ready, n + 1)
                    a.activation(parts[:, 0, cols], turned[:, n % 2, :], ACT.Copy).then_inc(part1, 1)
                    if which:
                        a.wait_ge(v_done, b + 1)
                        a.activation(values[:, b * ST:(b + 1) * ST, :].rearrange("p t d -> p (t d)"),
                                     bank[:, b, :], ACT.Copy).then_inc(v_out, 1)
                    a.wait_ge(rest_ready, n + 1)
                    a.activation(parts[:, 1, cols], rest[:, n % 2, :], ACT.Copy).then_inc(part2, 1)

            @block.gpsimd
            def _(g):
                for n, (b, which) in enumerate(items):
                    parts = kstack_src if which else qstack_src
                    cols = slice(b * S, (b + 1) * S)
                    g.wait_ge(part2, n + 1)
                    g.wait_ge(rest_ready, n + 1)
                    g.tensor_tensor(parts[:, 2, cols], rest[:, n % 2, :], parts[:, 1, cols], ALU.subtract)\
                        .then_inc(part3, 1)

            @block.tensor
            def _(pe):
                pe.wait_ge(w_here, 16 * 8)
                pe.wait_ge(ln.ready, 1)
                feature_major(pe, chip, xn, t_done)
                for b in range(B):
                    pe.wait_ge(xnt_ready, b + 1)
                    cols = xnt[:, b * S:(b + 1) * S]
                    for which in range(2):
                        n = 2 * b + which
                        if n >= 2:
                            pe.wait_ge(qk_read, n - 1)
                        name = ("wq", "wk")[which]
                        pe.matmul(bank[:, 4 + 2 * which, :], w[name][:], cols, start=True, stop=True)
                        pe.matmul(bank[:, 5 + 2 * which, :], w[name + "_swap"][:], cols, start=True, stop=True)\
                            .then_inc(qk_done, 1)
                    for j in range(ST):
                        last = pe.matmul(bank[:, b, j * P:(j + 1) * P], xnt[:, (b * ST + j) * P:(b * ST + j + 1) * P],
                                         w["wv"][:], start=True, stop=True)
                    last.then_inc(v_done, 1)


QPART = (0, 0, 1, 1, 0, 2)
KPART = (0, 1, 0, 1, 2, 0)


def self_attention(chip, qparts, kparts, values, mixt):
    nc, bank = chip.nc, chip.bank
    SCALE = float(HD) ** -0.5
    SLOTS = len(QPART)
    units = [(qt, hp) for qt in range(ST) for hp in range(H // 2)]
    NU = len(units)
    with ExitStack() as ctx:
        qs = chip.sb(ctx, "s_q", [P, 2, H, S], BF16)
        ks = chip.sb(ctx, "s_k", [P, 2, H, S], BF16)
        keep = chip.sb(ctx, "s_keep", [P, 4, P])
        prob = chip.sb(ctx, "s_prob", [P, 2, 2, S])
        probt = chip.sb(ctx, "s_probt", [P, 2, 2 * ST, P])
        top = chip.sb(ctx, "s_top", [P, 2, 2])
        shift = chip.sb(ctx, "s_shift", [P, 2, 2])
        total = chip.sb(ctx, "s_total", [P, 2, H])
        rtotal, rwide = chip.sb(ctx, "s_rtotal", [P, H]), chip.sb(ctx, "s_rwide", [P, H, HD])
        rturned, rt_out = chip.sb(ctx, "s_rturned", [P, P]), chip.sem("s_rt_out")
        vpad = chip.sb(ctx, "s_vpad", [P, ST, H * (D + HD)])
        zeroed, keep_here = chip.sem("s_zeroed"), chip.sem("s_keep_here")
        stacked, scored, topped = chip.sem("s_stacked"), chip.sem("s_scored"), chip.sem("s_topped")
        shifted, expd = chip.sem("s_shifted"), chip.sem("s_expd")
        turned, below_out, diag_out = chip.sem("s_turned"), chip.sem("s_below_out"), chip.sem("s_diag_out")
        weighed, rt_ready, mixed_out = chip.sem("s_weighed"), chip.sem("s_rt_ready"), chip.sem("s_mixed_out")
        recip, rt_turned, v_placed = chip.sem("s_recip"), chip.sem("s_rt_turned"), chip.sem("s_v_placed")

        def ptb(hh, kb):
            i = 2 * kb + hh
            return bank[:, 4 + i // 4, (i % 4) * P:(i % 4 + 1) * P]

        def stack(sp, b, slot):
            for n in range(SLOTS):
                for parts, st, which in ((qparts, qs, QPART), (kparts, ks, KPART)):
                    src = parts[:, which[n], :].rearrange("p (b s) -> p b s", b=B)
                    sp.dma_start(st[n * HD:(n + 1) * HD, slot, :, :], src[:, b, :]).then_inc(stacked, 16)

        def place_values(g, b):
            for kb in range(ST):
                g.tensor_copy(vpad[:, kb, :].rearrange("p (h c) -> p h c", h=H)[:, :, 0:HD],
                              values[:, bass.ds(b * ST + kb, 1), :].rearrange("p t (h d) -> p (t h) d", h=H))\
                    .then_inc(v_placed, 1)

        with nc.Block() as block:
            @block.sync
            def _(sp):
                sp.dma_start(keep[:].rearrange("p k q -> p (k q)"), chip.dram["keep"][:, :]).then_inc(keep_here, 16)
                sp.wait_ge(zeroed, 2)
                for b in range(2):
                    stack(sp, b, b)
                    sp.wait_ge(stacked, 16 * 2 * SLOTS * (b + 1))
                for b in range(2, B):
                    sp.wait_ge(scored, NU * (b - 1))
                    stack(sp, b, b % 2)
                    sp.wait_ge(stacked, 16 * 2 * SLOTS * (b + 1))

            @block.gpsimd
            def _(g):
                g.memset(qs[:], 0.0).then_inc(zeroed, 1)
                g.memset(ks[:], 0.0).then_inc(zeroed, 1)
                g.memset(vpad[:], 0.0).then_inc(zeroed, 1)
                g.wait_ge(zeroed, 3)
                place_values(g, 0)
                with g.Fori(1, B) as b:
                    g.wait_ge(weighed, NU * b)
                    place_values(g, b)

            @block.tensor
            def _(pe):
                with pe.Fori(0, B) as b:
                    pe.wait_ge(stacked, 16 * 2 * SLOTS * (b + 1))
                    for n in range(NU + 2):
                        if n < NU:
                            qt, hp = units[n]
                            if n >= 2:
                                pe.wait_ge(expd, 2 * (NU * b + n - 1))
                            for hh in range(2):
                                h = 2 * hp + hh
                                last = pe.matmul(bank[:, 2 * (n % 2) + hh, :], qs[:, b % 2, h, qt * P:(qt + 1) * P],
                                                 ks[:, b % 2, h, :], start=True, stop=True)
                            last.then_inc(scored, 1)
                        if 1 <= n <= NU:
                            qt, hp = units[n - 1]
                            pe.wait_ge(expd, 2 * (NU * b + n))
                            if n >= 2:
                                pe.wait_ge(diag_out, NU * b + n - 1)
                                pe.wait_ge(below_out, NU * b + n - 1)
                            for kb in range(qt + 1):
                                for hh in range(2):
                                    last = pe.transpose(ptb(hh, kb), prob[:, (n - 1) % 2, hh, kb * P:(kb + 1) * P],
                                                        chip.ident[:])
                            last.then_inc(turned, 1)
                        if n >= 2:
                            qt, hp = units[n - 2]
                            pe.wait_ge(diag_out, NU * b + n - 1)
                            pe.wait_ge(below_out, NU * b + n - 1)
                            if n == 2:
                                pe.wait_ge(v_placed, ST * (b + 1))
                            if hp == 0 and qt >= 2:
                                pe.wait_ge(mixed_out, ST * b + qt - 1)
                            for hh in range(2):
                                h = 2 * hp + hh
                                for kb in range(qt + 1):
                                    last = pe.matmul(bank[:, 6 + qt % 2, 0:P], vpad[:, kb, h * D:(h + 1) * D],
                                                     probt[:, (n - 2) % 2, 2 * kb + hh, :],
                                                     start=(h == 0 and kb == 0), stop=(h == H - 1 and kb == qt))
                            last.then_inc(weighed, 1)
                            if hp == H // 2 - 1:
                                pe.wait_ge(rt_ready, ST * b + qt + 1)
                                pe.transpose(bank[:, 6 + qt % 2, P:2 * P], rwide[:].rearrange("p h d -> p (h d)"),
                                             chip.ident[:]).then_inc(rt_turned, 1)
                    pe.wait_ge(mixed_out, ST * (b + 1))

            @block.vector
            def _(v):
                v.wait_ge(keep_here, 16)
                with v.Fori(0, B) as b:
                    for n in range(NU + 3):
                        if n < NU:
                            qt, hp = units[n]
                            v.wait_ge(scored, NU * b + n + 1)
                            v.tensor_reduce(top[:, n % 2, :], bank[:, 2 * (n % 2):2 * (n % 2) + 2, :], AX.X, ALU.max)\
                                .then_inc(topped, 1)
                            v.wait_ge(topped, NU * b + n + 1)
                            if n >= 2:
                                v.wait_ge(expd, 2 * (NU * b + n - 1))
                            v.tensor_scalar(shift[:, n % 2, :], top[:, n % 2, :], -SCALE, None, ALU.mult)\
                                .then_inc(shifted, 1)
                        if 1 <= n <= NU:
                            qt, hp = units[n - 1]
                            v.wait_ge(turned, NU * b + n)
                            if n >= 3:
                                v.wait_ge(weighed, NU * b + n - 2)
                            odd = qt % 2
                            v.tensor_tensor(probt[:, (n - 1) % 2, 2 * (qt - odd):2 * qt + 2, :],
                                            bank[:, 4 + qt // 2, 0:(2 + 2 * odd) * P].rearrange("p (k q) -> p k q", q=P),
                                            keep[:, 2 - 2 * odd:4, :], ALU.mult)\
                                .then_inc(diag_out, 1)
                        if 1 <= n <= NU and units[n - 1][1] == H // 2 - 1:
                            qt = units[n - 1][0]
                            v.reciprocal(rtotal[:], total[:, qt % 2, :]).then_inc(recip, 1)
                            v.wait_ge(recip, ST * b + qt + 1)
                            v.tensor_copy(rwide[:], rtotal[:].unsqueeze(2).broadcast_to([P, H, HD]))\
                                .then_inc(rt_ready, 1)
                        if n >= 3 and units[n - 3][1] == H // 2 - 1:
                            qt = units[n - 3][0]
                            v.wait_ge(rt_turned, ST * b + qt + 1)
                            v.tensor_copy(rturned[:], bank[:, 6 + qt % 2, P:2 * P]).then_inc(rt_out, 1)
                            v.wait_ge(rt_out, ST * b + qt + 1)
                            v.tensor_tensor(mixt[:, bass.ds((b * ST + qt) * P, P)], bank[:, 6 + qt % 2, 0:P],
                                            rturned[:], ALU.mult).then_inc(mixed_out, 1)

            @block.scalar
            def _(a):
                with a.Fori(0, B) as b:
                    for n in range(NU + 1):
                        if n < NU:
                            qt, hp = units[n]
                            a.wait_ge(shifted, NU * b + n + 1)
                            if n >= 2:
                                a.wait_ge(turned, NU * b + n - 1)
                            if hp == 0 and qt >= 2:
                                a.wait_ge(recip, ST * b + qt - 1)
                            for hh in range(2):
                                h = 2 * hp + hh
                                a.activation(prob[:, n % 2, hh, :], bank[:, 2 * (n % 2) + hh, :], ACT.Exp,
                                             bias=shift[:, n % 2, hh:hh + 1], scale=SCALE,
                                             accum_out=total[:, qt % 2, h:h + 1]).then_inc(expd, 1)
                        if n >= 1:
                            qt, hp = units[n - 1]
                            a.wait_ge(turned, NU * b + n)
                            if n >= 3:
                                a.wait_ge(weighed, NU * b + n - 2)
                            if qt < 2:
                                a.sem_inc(below_out, 1)
                                continue
                            a.activation(probt[:, (n - 1) % 2, 0:4, :].rearrange("p t q -> p (t q)"),
                                         bank[:, 4, :], ACT.Copy).then_inc(below_out, 1)


def project_and_add(chip, name, mixt, w_name, bias_name=None):
    nc, bank = chip.nc, chip.bank
    with ExitStack() as ctx:
        w = chip.sb(ctx, name + "_w", [D, D])
        bias = chip.sb(ctx, name + "_bias", [P, D])
        here, o_done = chip.sem(name + "_here"), chip.sem(name + "_o_done")
        added = chip.sem(name + "_added")
        with nc.Block() as block:
            @block.sync
            def _(sp):
                sp.dma_start(w[:], chip.dram[w_name][:, :]).then_inc(here, 16)
                if bias_name:
                    sp.dma_start(bias[:], chip.dram[bias_name][0:1, :].broadcast_to([P, D])).then_inc(here, 16)

            @block.tensor
            def _(pe):
                pe.wait_ge(here, 32 if bias_name else 16)
                for g in range(B):
                    for j in range(ST):
                        t = g * ST + j
                        last = pe.matmul(bank[:, 4 + g, j * D:(j + 1) * D], mixt[:, t * P:(t + 1) * P], w[:],
                                         start=True, stop=True)
                    last.then_inc(o_done, 1)

            @block.vector
            def _(v):
                if bias_name:
                    v.wait_ge(here, 32)
                    v.tensor_tensor(chip.x[:], chip.x[:], bias[:].unsqueeze(1).broadcast_to([P, NT, D]), ALU.add)\
                        .then_inc(added, 1)
                    v.wait_ge(added, 1)
                for g in range(B):
                    v.wait_ge(o_done, g + 1)
                    xg = chip.x[:, g * ST:(g + 1) * ST, :].rearrange("p t d -> p (t d)")
                    v.tensor_tensor(xg, xg, bank[:, 4 + g, :], ALU.add).then_inc(added, 1)


XG, XH = 3, 6
XW = XH * CTX


def cross_attention(chip):
    nc, dram, bank = chip.nc, chip.dram, chip.bank
    with ExitStack() as stage:
        mixt = chip.sb(stage, "x_mixt", [P, TOK])
        qt_ = chip.sb(stage, "x_qt", [P, TOK])
        kblk = chip.sb(stage, "x_kblk", [P, B, XG * XH, CTX])
        vpad = chip.sb(stage, "x_vpad", [CTX, B, H * (D + HD)])
        cross_inputs(chip, qt_, kblk, vpad)
        cross_core(chip, qt_, kblk, vpad, mixt)
        project_and_add(chip, "x_out", mixt, "x_wo", "x_bo")


def cross_inputs(chip, q_t, kblk, vpad):
    nc, dram, bank = chip.nc, chip.dram, chip.bank
    with ExitStack() as ctx:
        xn = chip.sb(ctx, "xi_xn", [P, NT, D])
        xnt = chip.sb(ctx, "xi_xnt", [P, TOK])
        w = {n: chip.sb(ctx, "xi_" + n, [D, D]) for n in ("x_wq", "x_wk", "x_wv")}
        bq, bk = chip.sb(ctx, "xi_bq", [D, 1]), chip.sb(ctx, "xi_bk", [D, 1])
        bv = chip.sb(ctx, "xi_bv", [CTX, D])
        own = chip.sb(ctx, "xi_own", [P, XG * XH])
        c = chip.sb(ctx, "xi_c", [CTX, B, D])
        ct, kt = chip.sb(ctx, "xi_ct", [D, B * CTX]), chip.sb(ctx, "xi_kt", [D, B * CTX])
        ln = LayerNorm(chip, ctx, "xi_ln", chip.x, xn)
        here, t_done, xnt_ready = chip.sem("xi_here"), chip.sem("xi_t_done"), chip.sem("xi_xnt_ready")
        ct_done, ct_ready, k_done, v_done = (chip.sem("xi_" + n) for n in ("ct_done", "ct_ready", "k_done", "v_done"))
        kt_ready, q_done, zeroed, out = (chip.sem("xi_" + n) for n in ("kt_ready", "q_done", "zeroed", "out"))
        with nc.Block() as block:
            @block.sync
            def _(sp):
                sp.dma_start(c[:], dram["ctx"].rearrange("b k d -> k b d")).then_inc(here, 16)
                for n in w:
                    sp.dma_start(w[n][:], dram[n][:, :]).then_inc(here, 16)
                sp.dma_start(bq[:], dram["x_bq"][:, :]).then_inc(here, 16)
                sp.dma_start(bk[:], dram["x_bk"][:, :]).then_inc(here, 16)
                sp.dma_start(bv[:], dram["x_bv"][0:1, :].broadcast_to([CTX, D])).then_inc(here, 16)
                sp.dma_start(own[:], dram["own_head"][:, :]).then_inc(here, 16)

            @block.tensor
            def _(pe):
                pe.wait_ge(here, 16 * 8)
                for b in range(B):
                    last = pe.transpose(bank[:, 4, b * CTX:(b + 1) * CTX], c[:, b, :], chip.ident[0:CTX, 0:CTX])
                last.then_inc(ct_done, 1)
                pe.wait_ge(ct_ready, 1)
                pe.matmul(bank[:, 5, 0:B * CTX], w["x_wk"][:], ct[:], start=True, stop=True).then_inc(k_done, 1)
                for b in range(B):
                    last = pe.matmul(bank[0:CTX, 6, b * D:(b + 1) * D], ct[:, b * CTX:(b + 1) * CTX], w["x_wv"][:],
                                     start=True, stop=True)
                last.then_inc(v_done, 1)
                pe.wait_ge(ln.ready, 1)
                feature_major(pe, chip, xn, t_done)
                for b in range(B):
                    pe.wait_ge(xnt_ready, b + 1)
                    pe.matmul(bank[:, b, :], w["x_wq"][:], xnt[:, b * S:(b + 1) * S], start=True, stop=True)\
                        .then_inc(q_done, 1)

            @block.scalar
            def _(a):
                a.wait_ge(here, 16 * 8)
                a.wait_ge(ct_done, 1)
                a.activation(ct[:], bank[:, 4, 0:B * CTX], ACT.Copy).then_inc(ct_ready, 1)
                a.wait_ge(k_done, 1)
                a.activation(kt[:], bank[:, 5, 0:B * CTX], ACT.Identity, bias=bk[:, 0:1]).then_inc(kt_ready, 1)
                ln.scalar(a)
                for b in range(B):
                    a.wait_ge(t_done, b + 1)
                    a.activation(xnt[:, b * S:(b + 1) * S], bank[:, b, :], ACT.Copy).then_inc(xnt_ready, 1)
                for b in range(B):
                    a.wait_ge(q_done, b + 1)
                    a.activation(q_t[:, b * S:(b + 1) * S], bank[:, b, :], ACT.Identity, bias=bq[:, 0:1])\
                        .then_inc(out, 1)

            @block.gpsimd
            def _(g):
                g.memset(vpad[:], 0.0).then_inc(zeroed, 1)
                g.wait_ge(kt_ready, 1)
                for b in range(B):
                    g.tensor_tensor(kblk[:, b, :, :],
                                    kt[:, b * CTX:(b + 1) * CTX].unsqueeze(1).broadcast_to([P, XG * XH, CTX]),
                                    own[:].unsqueeze(2).broadcast_to([P, XG * XH, CTX]), ALU.mult).then_inc(out, 1)

            @block.vector
            def _(v):
                ln.vector(v)
                v.wait_ge(v_done, 1)
                v.wait_ge(here, 16 * 8)
                v.wait_ge(zeroed, 1)
                own_columns = vpad[:].rearrange("k b (h c) -> k b h c", h=H)[:, :, :, 0:HD]
                v.tensor_tensor(own_columns, bank[0:CTX, 6, :].rearrange("k (b h d) -> k b h d", b=B, h=H),
                                bv[:].rearrange("k (h d) -> k h d", h=H).unsqueeze(1).broadcast_to([CTX, B, H, HD]),
                                ALU.add).then_inc(out, 1)


def cross_core(chip, q_t, kblk, vpad, mixt):
    nc, bank = chip.nc, chip.bank
    HALF = H // 2
    with ExitStack() as ctx:
        sb = lambda n, shape: chip.sb(ctx, "xc_" + n, shape)
        top, total, rtotal = sb("top", [P, XG, XH]), sb("total", [P, XG, XH]), sb("rtotal", [P, XG, XH])
        rwide, rturned = sb("rwide", [P, H, HD]), sb("rturned", [P, P])
        low = sb("low", [P, 2, XG, XH, CTX])
        probt = sb("probt", [CTX, 2, HALF, P])
        names = ("scored", "topped", "lowered", "expd", "turned", "turned_out", "weighed", "totalled", "recip",
                 "rt_ready", "rt_turned", "rt_out", "mixed_out")
        s = {n: chip.sem("xc_" + n) for n in names}
        scores = bank[:, 0:XG, 0:XW].rearrange("p g (h k) -> p g h k", h=XH)

        def tile_scores(pe, t):
            for g in range(XG):
                last = pe.matmul(bank[:, g, 0:XW], q_t[:, t * P:(t + 1) * P],
                                 kblk[:, t // ST, g * XH:(g + 1) * XH, :].rearrange("p h k -> p (h k)"),
                                 start=True, stop=True)
            last.then_inc(s["scored"], 1)

        def turn_totals(pe, t):
            pe.wait_ge(s["rt_ready"], t + 1)
            pe.transpose(bank[:, 7, P:2 * P], rwide[:].rearrange("p h d -> p (h d)"), chip.ident[:])\
                .then_inc(s["rt_turned"], 1)

        def add_up(v, t):
            v.wait_ge(s["expd"], t + 1)
            v.tensor_reduce(total[:], low[:, t % 2], AX.X, ALU.add).then_inc(s["totalled"], 1)
            v.wait_ge(s["totalled"], t + 1)
            v.reciprocal(rtotal[:], total[:]).then_inc(s["recip"], 1)
            v.wait_ge(s["recip"], t + 1)
            if t >= 1:
                v.wait_ge(s["rt_turned"], t)
            flat = rtotal[:].rearrange("p g h -> p (g h)")
            v.tensor_copy(rwide[:], flat[:, 0:H].unsqueeze(2).broadcast_to([P, H, HD])).then_inc(s["rt_ready"], 1)

        def divide(v, t):
            v.wait_ge(s["rt_turned"], t + 1)
            v.tensor_copy(rturned[:], bank[:, 7, P:2 * P]).then_inc(s["rt_out"], 1)
            v.wait_ge(s["rt_out"], t + 1)
            v.wait_ge(s["weighed"], t + 1)
            v.tensor_tensor(mixt[:, t * P:(t + 1) * P], bank[:, 7, 0:P], rturned[:], ALU.mult)\
                .then_inc(s["mixed_out"], 1)

        with nc.Block() as block:
            @block.tensor
            def _(pe):
                tile_scores(pe, 0)
                for t in range(NT):
                    for half in range(2):
                        n = 2 * t + half
                        if half == 0:
                            pe.wait_ge(s["expd"], t + 1)
                        if n >= 2:
                            pe.wait_ge(s["turned_out"], n - 1)
                        for j in range(HALF):
                            h = half * HALF + j
                            last = pe.transpose(bank[0:CTX, 3 + 2 * half + j // 4, (j % 4) * P:(j % 4 + 1) * P],
                                                low[:, t % 2, h // XH, h % XH, :], chip.ident[:])
                        last.then_inc(s["turned"], 1)
                        if half == 0:
                            if t >= 1:
                                turn_totals(pe, t - 1)
                            if t + 1 < NT:
                                pe.wait_ge(s["lowered"], t + 1)
                                tile_scores(pe, t + 1)
                    if t >= 1:
                        pe.wait_ge(s["mixed_out"], t)
                    for half in range(2):
                        pe.wait_ge(s["turned_out"], 2 * t + half + 1)
                        for j in range(HALF):
                            h = half * HALF + j
                            last = pe.matmul(bank[:, 7, 0:P], vpad[:, t // ST, h * D:(h + 1) * D], probt[:, half, j, :],
                                             start=(h == 0), stop=(h == H - 1))
                    last.then_inc(s["weighed"], 1)
                turn_totals(pe, NT - 1)

            @block.vector
            def _(v):
                for t in range(NT):
                    v.wait_ge(s["scored"], t + 1)
                    v.tensor_reduce(top[:], scores, AX.X, ALU.max).then_inc(s["topped"], 1)
                    v.wait_ge(s["topped"], t + 1)
                    if t >= 2:
                        v.wait_ge(s["turned"], 2 * (t - 1))
                        v.wait_ge(s["totalled"], t - 1)
                    v.tensor_tensor(low[:, t % 2], scores, top[:].unsqueeze(3).broadcast_to([P, XG, XH, CTX]),
                                    ALU.subtract).then_inc(s["lowered"], 1)
                    if t >= 1:
                        divide(v, t - 1)
                    add_up(v, t)
                divide(v, NT - 1)

            @block.scalar
            def _(a):
                for t in range(NT):
                    a.wait_ge(s["lowered"], t + 1)
                    flat = low[:, t % 2].rearrange("p g h k -> p (g h k)")
                    a.activation(flat, flat, ACT.Exp).then_inc(s["expd"], 1)
                    for half in range(2):
                        a.wait_ge(s["turned"], 2 * t + half + 1)
                        if t >= 1:
                            a.wait_ge(s["weighed"], t)
                        a.activation(probt[:, half].rearrange("k h q -> k (h q)"),
                                     bank[0:CTX, 3 + 2 * half:5 + 2 * half, :].rearrange("k b q -> k (b q)"),
                                     ACT.Copy).then_inc(s["turned_out"], 1)


def more(r, a):
    f = np.float32
    col = lambda n: a[n].reshape(-1, 1)
    row = lambda n: a[n].reshape(1, -1)
    own = (np.arange(P)[:, None] // HD == np.arange(XG * XH)[None, :]).astype(f)
    r.update(x_wq=a["L0_xattn_Wq"].T, x_wk=a["L0_xattn_Wk"].T, x_wv=a["L0_xattn_Wv"].T, x_wo=a["L0_xattn_Wo"].T,
             x_bq=col("L0_xattn_bq"), x_bk=col("L0_xattn_bk"), x_bv=row("L0_xattn_bv"), x_bo=row("L0_xattn_bo"),
             own_head=own)


NE, NSH, TOPK = 16, 2, 2
QE = 4
ACT_E = 1


def experts(chip):
    with ExitStack() as stage:
        u = chip.sb(stage, "e_u", [P, NT, D])
        ut = chip.sb(stage, "e_ut", [P, TOK])
        gates = chip.sb(stage, "e_gates", [P, NT, NE + NSH])
        wr = chip.sb(stage, "e_wr", [D, NE, D])
        ws = chip.sb(stage, "e_ws", [D, NSH, D])
        brs = chip.sb(stage, "e_brs", [NE + NSH, D])
        weights_here = chip.sem("e_weights_here")
        route(chip, u, ut, gates, wr, ws, brs, weights_here)
        mix_experts(chip, u, ut, gates, wr, ws, brs, weights_here)


def route(chip, u, ut, gates, wr, ws, brs, weights_here):
    nc, dram, bank = chip.nc, chip.dram, chip.bank
    with ExitStack() as ctx:
        sb = lambda n, shape, dt=F32: chip.sb(ctx, "r_" + n, shape, dt)
        cent, bias, iota = sb("cent", [D, NE]), sb("bias", [P, NE]), sb("iota", [P, NE])
        score, hit = sb("score", [P, NT, NE]), sb("hit", [P, NT, NE])
        top, tot, rtot = sb("top", [P, NT]), sb("tot", [P, NT]), sb("rtot", [P, NT])
        best, where, wheref = sb("best", [P, NT, 8]), sb("where", [P, NT, 8], U32), sb("wheref", [P, NT, 8])
        ln = LayerNorm(chip, ctx, "r_ln", chip.x, u)
        here, t_done, ut_ready, raw_done = (chip.sem("r_" + n) for n in ("here", "t_done", "ut_ready", "raw_done"))
        step, centred, expd = chip.sem("r_step"), chip.sem("r_centred"), chip.sem("r_expd")
        summed = chip.sem("r_summed")
        with nc.Block() as block:
            @block.sync
            def _(sp):
                sp.dma_start(cent[:], dram["e_cent"][:, :]).then_inc(here, 16)
                sp.dma_start(bias[:], dram["e_bias"][0:1, :].broadcast_to([P, NE])).then_inc(here, 16)
                sp.dma_start(iota[:], dram["iota"][0:1, 0:NE].broadcast_to([P, NE])).then_inc(here, 16)
                sp.dma_start(wr[:], dram["e_wr"].rearrange("e d o -> d e o")).then_inc(weights_here, 16)
                sp.dma_start(ws[:], dram["e_ws"].rearrange("e d o -> d e o")).then_inc(weights_here, 16)
                sp.dma_start(brs[0:NE, :], dram["e_br"][:, :]).then_inc(weights_here, 16)
                sp.dma_start(brs[NE:NE + NSH, :], dram["e_bs"][:, :]).then_inc(weights_here, 16)

            @block.tensor
            def _(pe):
                pe.wait_ge(ln.ready, 1)
                feature_major(pe, chip, u, t_done)
                pe.wait_ge(here, 48)
                pe.wait_ge(ut_ready, B)
                for t in range(NT):
                    last = pe.matmul(bank[:, 4, t * NE:(t + 1) * NE], ut[:, t * P:(t + 1) * P], cent[:],
                                     start=True, stop=True)
                last.then_inc(raw_done, 1)

            @block.scalar
            def _(a):
                ln.scalar(a)
                for g in range(B):
                    a.wait_ge(t_done, g + 1)
                    a.activation(ut[:, g * S:(g + 1) * S], bank[:, g, :], ACT.Copy).then_inc(ut_ready, 1)
                a.wait_ge(centred, 1)
                a.activation(score[:], score[:], ACT.Exp).then_inc(expd, 1)

            @block.gpsimd
            def _(g):
                g.memset(gates[:, :, NE:NE + NSH], 1.0 / NSH).then_inc(summed, 1)
                g.wait_ge(weights_here, 64)
                g.tensor_tensor(ws[:, 0, :], ws[:, 0, :], ws[:, 1, :], ALU.add).then_inc(summed, 1)
                g.wait_ge(summed, 2)
                g.tensor_scalar(ws[:, 0, :], ws[:, 0, :], 1.0 / NSH, None, ALU.mult).then_inc(summed, 1)

            @block.vector
            def _(v):
                over_e = lambda col: col.unsqueeze(2).broadcast_to([P, NT, NE])
                over_t = lambda row: row.unsqueeze(1).broadcast_to([P, NT, NE])
                ln.vector(v)
                v.wait_ge(here, 48)
                v.wait_ge(raw_done, 1)
                chain = Chain(v, step)
                chain.do(v.tensor_tensor(score[:], bank[:, 4, 0:NT * NE].rearrange("p (t e) -> p t e", t=NT),
                                         over_t(bias[:]), ALU.add))
                chain.do(v.tensor_reduce(top[:], score[:], AX.X, ALU.max))
                v.tensor_tensor(score[:], score[:], over_e(top[:]), ALU.subtract).then_inc(centred, 1)
                v.wait_ge(expd, 1)
                chain.do(v.tensor_reduce(tot[:], score[:], AX.X, ALU.add))
                chain.do(v.reciprocal(rtot[:], tot[:]))
                chain.do(v.tensor_tensor(score[:], score[:], over_e(rtot[:]), ALU.mult))
                for t in range(NT):
                    v.max(best[:, t, :], score[:, t, :]).then_inc(step, 1)
                chain.at += NT
                v.wait_ge(step, chain.at)
                for t in range(NT):
                    v.max_index(where[:, t, :], best[:, t, :], score[:, t, :]).then_inc(step, 1)
                chain.at += NT
                v.wait_ge(step, chain.at)
                chain.do(v.tensor_copy(wheref[:], where[:]))
                routed = gates[:, :, 0:NE]
                chain.do(v.tensor_tensor(routed, over_t(iota[:]), over_e(wheref[:, :, 0]), ALU.is_equal))
                chain.do(v.tensor_tensor(routed, routed, over_e(best[:, :, 0]), ALU.mult))
                for k in range(1, TOPK):
                    chain.do(v.tensor_tensor(hit[:], over_t(iota[:]), over_e(wheref[:, :, k]), ALU.is_equal))
                    chain.do(v.tensor_tensor(hit[:], hit[:], over_e(best[:, :, k]), ALU.mult))
                    chain.do(v.tensor_tensor(routed, routed, hit[:], ALU.add))


def mix_experts(chip, u, ut, gates, wr, ws, brs, weights_here):
    nc, bank = chip.nc, chip.bank
    NQ = NE // QE
    DVE_E = QE - ACT_E
    with ExitStack() as ctx:
        gatest = chip.sb(ctx, "m_gatest", [NE + NSH, TOK])
        gated = chip.sb(ctx, "m_gated", [P, 2, NE, D])
        routed = chip.sb(ctx, "m_routed", [P, 2, D])
        gt_done, gt_out = chip.sem("m_gt_done"), chip.sem("m_gt_out")
        made, by_vector, by_scalar = chip.sem("m_made"), chip.sem("m_by_vector"), chip.sem("m_by_scalar")
        shared, reduced, joined, plus_u = (chip.sem("m_" + n) for n in ("shared", "reduced", "joined", "plus_u"))
        with nc.Block() as block:
            @block.gpsimd
            def _(g):
                g.tensor_tensor(chip.x[:], chip.x[:], u[:], ALU.add).then_inc(plus_u, 1)

            @block.tensor
            def _(pe):
                for g in range(4):
                    for j in range(ST):
                        t = g * ST + j
                        last = pe.transpose(bank[0:NE + NSH, g, j * P:(j + 1) * P], gates[:, t, :], chip.ident[:])
                    last.then_inc(gt_done, 1)
                pe.wait_ge(weights_here, 64)
                for t in range(NT):
                    for q in range(NQ):
                        n = t * NQ + q
                        if n < 4:
                            pe.wait_ge(gt_out, n + 1)
                        if n >= 6:
                            pe.wait_ge(by_vector, n - 5)
                            pe.wait_ge(by_scalar, n - 5)
                        pe.matmul(bank[:, n % 6, :], ut[:, t * P:(t + 1) * P],
                                  wr[:, q * QE:(q + 1) * QE, :].rearrange("d e o -> d (e o)"), start=True, stop=True)\
                            .then_inc(made, 1)
                    if t == 0:
                        pe.wait_ge(gt_out, 4)
                    if t >= 2:
                        pe.wait_ge(joined, t - 1)
                    s = bank[:, 6 + t % 2, 0:D]
                    pe.matmul(s, ut[:, t * P:(t + 1) * P], ws[:, 0, :], start=True, stop=False)
                    pe.matmul(s, gatest[:, t * P:(t + 1) * P], brs[:], start=False, stop=True).then_inc(shared, 1)

            @block.scalar
            def _(a):
                for g in range(4):
                    a.wait_ge(gt_done, g + 1)
                    a.activation(gatest[:, g * S:(g + 1) * S], bank[0:NE + NSH, g, :], ACT.Copy).then_inc(gt_out, 1)
                for n in range(NT * NQ):
                    t, q = n // NQ, n % NQ
                    a.wait_ge(by_vector, n + 1)
                    if q == 0 and t >= 2:
                        a.wait_ge(reduced, t - 1)
                    for e in range(DVE_E, QE):
                        last = a.activation(gated[:, t % 2, q * QE + e, :], bank[:, n % 6, e * D:(e + 1) * D],
                                            ACT.Copy, scale=gates[:, t, q * QE + e:q * QE + e + 1])
                    last.then_inc(by_scalar, 1)

            @block.vector
            def _(v):
                v.wait_ge(plus_u, 1)
                for t in range(NT + 1):
                    if t < NT:
                        for q in range(NQ):
                            n = t * NQ + q
                            v.wait_ge(made, n + 1)
                            e = slice(q * QE, q * QE + DVE_E)
                            v.tensor_tensor(gated[:, t % 2, e, :],
                                            bank[:, n % 6, 0:DVE_E * D].rearrange("p (e o) -> p e o", o=D),
                                            gates[:, t, e].unsqueeze(2).broadcast_to([P, DVE_E, D]), ALU.mult)\
                                .then_inc(by_vector, 1)
                    if t >= 1:
                        v.wait_ge(by_scalar, NQ * t)
                        s = (t - 1) % 2
                        v.tensor_reduce(routed[:, s, :], gated[:, s].rearrange("p e o -> p o e"), AX.X, ALU.add)\
                            .then_inc(reduced, 1)
                        v.wait_ge(shared, t)
                        v.tensor_tensor(chip.x[:, t - 1, :], chip.x[:, t - 1, :], bank[:, 6 + s, 0:D], ALU.add)\
                            .then_inc(joined, 1)
                        v.wait_ge(joined, t)
                        v.wait_ge(reduced, t)
                        v.tensor_tensor(chip.x[:, t - 1, :], chip.x[:, t - 1, :], routed[:, s, :], ALU.add)


def more_experts(r, a):
    T = lambda n: a[n].transpose(0, 2, 1)
    r.update(e_cent=a["L0_ffn_centroids"].T, e_bias=a["L0_ffn_expert_biases"].reshape(1, -1),
             e_wr=T("L0_ffn_Wr"), e_ws=T("L0_ffn_Ws"), e_br=a["L0_ffn_br"], e_bs=a["L0_ffn_bs"],
             iota=np.arange(S, dtype=np.float32).reshape(1, -1))


NL = 4
DI, DS, DR, DC = 256, 16, 64, 4
NCH = DI // P
PAD = DC - 1
HB = B // 2
HT = HB * S
HTT = HT // P
NU = DS * NCH
SMALL = 1 / 16
SERIES = (1.0, -0.49999176, 0.33253264, -0.22751441)
REP = 96
RA = 3
EXP_AND_LN = "natural_log_exp_and_others"
NR = 3
LAG = 3
ITEMS = [("turn", b, 0) for b in range(HB)] + [("conv", b, c) for b in range(HB) for c in range(NCH)]
ITEMS += [("gate", 0, c) for c in range(NCH)]
for b in range(HB):
    ITEMS += [("rank", b, 0), ("bc", b, 0)] + [("dt", b, c) for c in range(NCH)]
ITEMS += [("gate", 1, c) for c in range(NCH)]
SLOT = [3, 4] + [5, 7, 9, 11] + [13, 14] + [15, 16, 17, 18] + [19, 20, 21, 22] + [23, 24]
EVAC = 2
SILU_AT = 14
SERIES_AT = [20, 24]
SERIES_STEPS = 8


def after(kind, b, c=0):
    return ITEMS.index((kind, b, c)) + 1


class MambaTiles:
    def __init__(self, chip, ctx):
        sb = lambda n, shape, dt=F32: chip.sb(ctx, "m_" + n, shape, dt)
        self.res = sb("res", [P, NT, D])
        self.xs, self.zs = sb("xs", [P, NCH, TOK]), sb("zs", [P, NCH, TOK])
        self.dt, self.u = sb("dt", [P, NCH, TOK]), sb("u", [P, NCH, TOK])
        self.bc = sb("bc", [REP, TOK], BF16)
        self.pick = sb("pick", [REP, 2 * DS, P], BF16)
        self.in_w, self.taps = sb("in_w", [D, 2 * DI]), sb("taps", [D, DC, DI])
        self.xp_w, self.dtp_w = sb("xp_w", [P, NCH, DR + 2 * DS]), sb("dtp_w", [DR, DI])
        self.col = sb("col", [P, 2, 2 + 3 * NCH])
        self.a = sb("a", [P, 2, NCH, DS])
        self.out_w = sb("out_w", [P, 2, NCH, D])
        self.xn = sb("xn", [P, HTT, D])
        self.h_t = sb("h_t", [P, HB, PAD + S])
        self.rank = sb("rank", [DR, HB, S])
        self.rest, self.mid = sb("rest", [2 * DS, HB, S]), sb("mid", [2 * DS, HB, S], BF16)
        self.mag, self.big = sb("mag", [P, HB, NCH, S]), sb("big", [P, HB, NCH, S])
        self.series = sb("series", [P, HB, NCH, S])
        self.one, self.log_small = sb("one", [P, 1]), sb("log_small", [P, 1])
        self.decay, self.inp = sb("decay", [P, RA, HB, S]), sb("inp", [P, RA, HT])
        self.state, self.read = sb("state", [P, RA, HT]), sb("read", [P, NR, HT])
        self.c_rep = sb("c_rep", [P, 2, HB, S])


def mamba(chip):
    nc, dram = chip.nc, chip.dram
    with ExitStack() as stage:
        m = MambaTiles(chip, stage)
        with ExitStack() as ctx:
            first = LayerNorm(chip, ctx, "m_first", chip.x, m.res)
            here, zero, cast = chip.sem("m_here"), chip.sem("m_zero"), chip.sem("m_cast")
            small = chip.sem("m_small")
            pick32 = m.xs[0:REP].rearrange("p c t -> p (c t)")
            with nc.Block() as block:
                @block.sync
                def _(sp):
                    sp.dma_start(pick32, dram["pick"][:, :]).then_inc(here, 16)

                @block.gpsimd
                def _(g):
                    g.memset(m.h_t[:], 0.0).then_inc(zero, 1)
                    g.memset(m.decay[:], 0.0).then_inc(zero, 1)
                    g.memset(m.one[:], 1.0).then_inc(small, 1)
                    g.memset(m.log_small[:], SMALL).then_inc(small, 1)

                @block.vector
                def _(v):
                    first.vector(v)

                @block.scalar
                def _(a):
                    first.scalar(a)
                    a.wait_ge(small, 2)
                    a.activation(m.log_small[:], m.log_small[:], ACT.Ln, bias=m.one[:]).then_inc(small, 1)
                    a.wait_ge(here, 16)
                    a.activation(m.pick[:].rearrange("r n p -> r (n p)"), pick32, ACT.Copy).then_inc(cast, 1)
        work = MambaStage(chip, m, stage)
        work.block(core=None, front=0, layer=0)
        with nc.Fori(0, NL - 1) as layer:
            work.block(core=0, front=1, layer=layer)
            work.block(core=1, front=0, layer=layer + 1)
        work.block(core=0, front=1, layer=NL - 1)
        work.block(core=1, front=None)
        mamba_out(chip, m)


class MambaStage:

    def __init__(self, chip, m, ctx):
        self.chip, self.m = chip, m
        names = ("w_here", "tapped", "a_exp", "a_neg", "filled", "emptied", "x_silu", "z_silu", "bc_hi", "bc_mid",
                 "bc_midcopy", "bc_lo", "u_ready")
        names += tuple(n + str(b) for n in ("abs_ready", "exp_ready", "step", "log_ready", "dt_ready") for b in range(HB))
        self.f = {n: chip.sem("mf_" + n) for n in names}
        names = ("reps_b", "reps_c", "decay", "c_out", "input", "state", "read", "summed", "direct", "gated",
                 "projected", "added")
        self.s = {n: chip.sem("mc_" + n) for n in names}
        self.ln = LayerNorm(chip, ctx, "mf_ln", m.res[:, 0:HTT, :], m.xn)

    def block(self, core, front, layer=0):
        self.core, self.front = core, front
        if front is not None:
            self.ln.src = self.m.res[:, front * HTT:(front + 1) * HTT, :]
        self.new = front == 0
        self.loads = 7 if self.new else 3
        with self.chip.nc.Block() as block:
            @block.sync
            def _(sp):
                if front is not None:
                    self.load(sp, layer)

            @block.tensor
            def _(pe):
                for u in range(NU + LAG):
                    if core is not None:
                        self.core_tensor(pe, u)
                    if front is not None:
                        self.front_tensor(pe, u)
                if core is not None:
                    self.project(pe)

            @block.scalar
            def _(a):
                a.preload_act_table_set(EXP_AND_LN)
                for u in range(NU + LAG):
                    if core is not None:
                        self.core_scalar(a, u)
                    if front is not None:
                        self.front_scalar(a, u)

            @block.vector
            def _(v):
                for u in range(NU):
                    if core is not None:
                        self.core_vector(v, u)
                    if front is not None:
                        self.front_vector(v, u)
                if core is not None:
                    self.join(v)
                    self.add_to_residual(v)

            @block.gpsimd
            def _(g):
                for u in range(NU):
                    if core is not None:
                        self.core_pool(g, u)
                    if front is not None:
                        self.front_pool(g, u)
                if front is not None:
                    self.inputs(g, 1)
        self.chip.clear(list(self.s.values()) + list(self.f.values()) + self.ln.sems())


    def wide(self, i):
        return self.chip.bank[:, i:i + 2, :].rearrange("p k q -> p (k q)")

    def half(self, tile, c, core):
        return tile[:, c, core * HT:(core + 1) * HT]

    def core_tensor(self, pe, u):
        m, s, bank = self.m, self.s, self.chip.bank
        n, c = u // NCH, u % NCH
        cols = lambda bb: m.bc[:, self.core * HT + bb * S:self.core * HT + (bb + 1) * S]
        if u < NU:
            if u >= 1:
                pe.wait_ge(s["c_out"], u)
            pe.matmul(bank[:, 6, :], m.pick[:, DS + n, :], cols(c), start=True, stop=True).then_inc(s["reps_c"], 1)
            if c == 0:
                if n >= 1:
                    pe.wait_ge(s["input"], u)
                for bb in range(HB):
                    last = pe.matmul(bank[:, 4 + bb, :], m.pick[:, n, :], cols(bb), start=True, stop=True)
                last.then_inc(s["reps_b"], 1)
        if u >= LAG:
            n, c = (u - LAG) // NCH, (u - LAG) % NCH
            pe.wait_ge(s["read"], u - LAG + 1)
            for bb in range(HB):
                last = pe.matmul(bank[:, 2 * c + bb, :], self.chip.ident[:],
                                 m.read[:, (u - LAG) % NR, bb * S:(bb + 1) * S], start=(n == 0), stop=(n == DS - 1))
            last.then_inc(s["summed"], 1)

    def project(self, pe):
        m, s, bank = self.m, self.s, self.chip.bank
        for c in range(NCH):
            pe.wait_ge(s["gated"], c + 1)
            for t in range(HTT):
                last = pe.matmul(bank[:, 4 + t // ST, (t % ST) * D:(t % ST + 1) * D], self.half(m.xs, c, self.core)[:, t * P:(t + 1) * P],
                                 m.out_w[:, self.core, c, :], start=(c == 0 and t % ST == 0),
                                 stop=(c == NCH - 1 and t % ST == ST - 1))
        last.then_inc(s["projected"], 1)

    def core_scalar(self, a, u):
        m, s = self.m, self.s
        n, c = u // NCH, u % NCH
        if u < NU:
            if u >= RA:
                a.wait_ge(s["state"], u - RA + 1)
            dt = self.half(m.dt, c, self.core).rearrange("p (b t) -> p b t", b=HB)
            a.activation(m.decay[:, u % RA, :, 1:], dt[:, :, 1:], ACT.Exp, scale=m.a[:, self.core, c, n:n + 1])\
                .then_inc(s["decay"], 1)
        if 1 <= u <= NU:
            n, bb = (u - 1) // NCH, (u - 1) % NCH
            a.wait_ge(s["reps_c"], u)
            if n >= 2:
                a.wait_ge(s["read"], NCH * (n - 1))
            a.activation(m.c_rep[:, n % 2, bb, :], self.chip.bank[:, 6, :], ACT.Copy).then_inc(s["c_out"], 1)

    def core_vector(self, v, u):
        m, s = self.m, self.s
        if u % NCH == 0:
            v.wait_ge(s["reps_b"], u // NCH + 1)
            for c in range(NCH):
                i = u + c
                if i >= RA:
                    v.wait_ge(s["state"], i - RA + 1)
                v.tensor_tensor(m.inp[:, i % RA, :], self.half(m.u, c, self.core), self.wide(4), ALU.mult)\
                    .then_inc(s["input"], 1)
        v.wait_ge(s["input"], u + 1)
        v.wait_ge(s["decay"], u + 1)
        if u >= RA:
            v.wait_ge(s["read"], u - RA + 1)
        v.tensor_tensor_scan(m.state[:, u % RA, :], m.decay[:, u % RA].rearrange("p b t -> p (b t)"),
                             m.inp[:, u % RA, :], 0.0, ALU.mult, ALU.add).then_inc(s["state"], 1)

    def core_pool(self, g, u):
        m, s = self.m, self.s
        n = u // NCH
        g.wait_ge(s["c_out"], HB * (n + 1))
        g.wait_ge(s["state"], u + 1)
        if u >= NR:
            g.wait_ge(s["summed"], u - NR + 1)
        g.tensor_tensor(m.read[:, u % NR, :], m.state[:, u % RA, :], m.c_rep[:, n % 2].rearrange("p b t -> p (b t)"),
                        ALU.mult).then_inc(s["read"], 1)

    def join(self, v):
        m, s, core = self.m, self.s, self.core
        for c in range(NCH):
            v.wait_ge(s["summed"], NU - NCH + c + 1)
            x = self.half(m.xs, c, core)
            v.scalar_tensor_tensor(x, x,
                                   m.col[:, core, 2 + 2 * NCH + c:3 + 2 * NCH + c], self.wide(2 * c),
                                   ALU.mult, ALU.add).then_inc(s["direct"], 1)
            v.wait_ge(s["direct"], c + 1)
            v.tensor_tensor(x, x, self.half(m.zs, c, core), ALU.mult).then_inc(s["gated"], 1)

    def add_to_residual(self, v):
        m, s = self.m, self.s
        v.wait_ge(s["projected"], 1)
        r = m.res[:, self.core * HTT:(self.core + 1) * HTT, :].rearrange("p t d -> p (t d)")
        v.tensor_tensor(r, r, self.wide(4), ALU.add).then_inc(s["added"], 1)


    def load(self, sp, layer):
        m, here, dram, front = self.m, self.f["w_here"], self.chip.dram, self.front
        flat = lambda t: t.rearrange("p a b -> p (a b)")

        def load(dst, name):
            sp.dma_start(dst, dram[name][bass.ds(layer, 1)].rearrange("l p n -> (l p) n")).then_inc(here, 16)
        load(m.col[:, front, :], "mb_col")
        load(flat(m.a[:, front]), "mb_a")
        load(flat(m.out_w[:, front]), "mb_out")
        if self.new:
            load(m.in_w[:], "mb_in")
            sp.dma_start(flat(m.taps[:]), dram["mb_conv"][bass.ds(layer, 1), :].broadcast_to([D, DC * DI]))\
                .then_inc(here, 16)
            load(flat(m.xp_w[:]), "mb_xp")
            load(m.dtp_w[:], "mb_dtp")

    def cols(self, b):
        return slice(self.front * HT + b * S, self.front * HT + (b + 1) * S)

    def front_tensor(self, pe, u):
        m, f, bank = self.m, self.f, self.chip.bank[:, 7, :]
        for k, (kind, b, c) in enumerate(ITEMS):
            if u == SLOT[k]:
                pe.wait_ge(f["filled"], k) if k else pe.wait_ge(self.ln.ready, 1)
                if k:
                    pe.wait_ge(f["emptied"], k)
                if kind == "turn":
                    for j in range(ST):
                        last = pe.transpose(bank[:, j * P:(j + 1) * P], m.xn[:, b * ST + j, :], self.chip.ident[:])
                elif kind == "conv":
                    pe.wait_ge(f["w_here"], 16 * self.loads)
                    if self.new:
                        pe.wait_ge(f["tapped"], 1)
                    self.convolve(pe, b, c, range(DC // 2))
                    continue
                elif kind == "gate":
                    last = pe.matmul(bank, m.in_w[:, DI + c * P:DI + (c + 1) * P], m.h_t[:, b, PAD:],
                                     start=True, stop=True)
                elif kind == "dt":
                    last = pe.matmul(bank, m.dtp_w[:, c * P:(c + 1) * P], m.rank[:, b, :], start=True, stop=True)
                else:
                    pe.wait_ge(f["x_silu"], 1)
                    which = slice(0, DR) if kind == "rank" else slice(DR, DR + 2 * DS)
                    for c in range(NCH):
                        last = pe.matmul(bank[0:which.stop - which.start], m.xp_w[:, c, which], m.xs[:, c, self.cols(b)],
                                         start=(c == 0), stop=(c == NCH - 1))
                last.then_inc(f["filled"], 1)
            elif kind == "conv" and u == SLOT[k] + 1:
                self.convolve(pe, b, c, range(DC // 2, DC)).then_inc(f["filled"], 1)

    def convolve(self, pe, b, c, taps):
        m = self.m
        for k in taps:
            last = pe.matmul(self.chip.bank[:, 7, :], m.taps[:, k, c * P:(c + 1) * P], m.h_t[:, b, k:k + S],
                             start=(k == 0), stop=(k == DC - 1))
        return last

    def front_scalar(self, a, u):
        m, f, front = self.m, self.f, self.front
        bank, col = self.chip.bank[:, 7, :], m.col[:, front, :]
        if u == 1:
            a.wait_ge(f["w_here"], 16 * self.loads)
            a.activation(m.a[:, front], m.a[:, front], ACT.Exp).then_inc(f["a_exp"], 1)
        if u == 3:
            self.ln.scalar(a)
        for k, (kind, b, c) in enumerate(ITEMS):
            if u != SLOT[k] + EVAC + (kind == "conv"):
                continue
            a.wait_ge(f["filled"], k + 1)
            done = f["emptied"]
            if kind == "turn":
                last = a.activation(m.h_t[:, b, PAD:], bank, ACT.Identity, scale=col[:, 0:1], bias=col[:, 1:2])
            elif kind == "conv":
                last = a.activation(m.xs[:, c, self.cols(b)], bank, ACT.Identity, bias=col[:, 2 + c:3 + c])
            elif kind == "gate":
                last = a.activation(m.zs[:, c, self.cols(b)], bank, ACT.Copy)
            elif kind == "rank":
                last = a.activation(m.rank[:, b, :], bank[0:DR], ACT.Copy)
            elif kind == "dt":
                last = a.activation(m.dt[:, c, self.cols(b)], bank, ACT.Identity, bias=col[:, 2 + NCH + c:3 + NCH + c])
            else:
                last, done = a.activation(m.bc[0:2 * DS, self.cols(b)], bank[0:2 * DS], ACT.Copy), f["bc_hi"]
            last.then_inc(done, 1)
            if kind == "dt" and c == 0:
                a.wait_ge(f["emptied"], after("bc", b))
                a.activation(m.mid[:, b, :], m.rest[:, b, :], ACT.Copy).then_inc(f["bc_mid"], 1)
                a.activation(m.bc[2 * DS:4 * DS, self.cols(b)], m.rest[:, b, :], ACT.Copy).then_inc(f["bc_midcopy"], 1)
        if u == SILU_AT:
            self.silu(a, m.xs, after("conv", HB - 1, NCH - 1), f["x_silu"])
            a.preload_act_table_set(EXP_AND_LN)
        if u == NU + LAG - 1:
            self.silu(a, m.zs, after("gate", HB - 1, NCH - 1), f["z_silu"])
        for b in range(HB):
            if u == SERIES_AT[b]:
                self.exponential(a, b)
            if u == SERIES_AT[b] + 5:
                self.logarithm(a, b)

    def silu(self, a, tile, count, done):
        part = tile[:, :, self.front * HT:(self.front + 1) * HT]
        a.wait_ge(self.f["emptied"], count)
        a.activation(part, part, ACT.Silu).then_inc(done, 1)


    def exponential(self, a, b):
        m, f = self.m, self.f
        a.wait_ge(f["emptied"], after("dt", b, NCH - 1))
        a.activation(m.mag[:, b], m.dt[:, :, self.cols(b)], ACT.Abs).then_inc(f[f"abs_ready{b}"], 1)
        a.wait_ge(f[f"abs_ready{b}"], 1)
        a.activation(m.mag[:, b], m.mag[:, b], ACT.Exp, scale=-1.0).then_inc(f[f"exp_ready{b}"], 1)

    def logarithm(self, a, b):
        m, f = self.m, self.f
        a.wait_ge(f[f"step{b}"], 1)
        a.activation(m.big[:, b], m.big[:, b], ACT.Ln, bias=m.one[:]).then_inc(f[f"log_ready{b}"], 1)

    def soft_plus(self, v, b, i):
        m, f = self.m, self.f
        e, p, big, dt = m.mag[:, b], m.series[:, b], m.big[:, b], m.dt[:, :, self.cols(b)]
        step = f[f"step{b}"]
        if i == 0:
            v.wait_ge(f[f"exp_ready{b}"], 1)
            v.tensor_scalar(big, e, SMALL, None, ALU.max).then_inc(step, 1)
            return
        v.wait_ge(step, i)
        if i == 1:
            v.tensor_scalar(e, e, SMALL, None, ALU.min).then_inc(step, 1)
        if i == 2:
            v.tensor_scalar(p, e, SERIES[3], SERIES[2], ALU.mult, ALU.add).then_inc(step, 1)
        if i == 3:
            v.tensor_tensor(p, p, e, ALU.mult).then_inc(step, 1)
        if i == 4:
            v.scalar_tensor_tensor(p, p, SERIES[1], e, ALU.add, ALU.mult).then_inc(step, 1)
        if i == 5:
            v.scalar_tensor_tensor(p, p, SERIES[0], e, ALU.add, ALU.mult).then_inc(step, 1)
        if i == 6:
            v.scalar_tensor_tensor(p, dt, 0.0, p, ALU.max, ALU.add).then_inc(step, 1)
        if i == 7:
            v.wait_ge(f[f"log_ready{b}"], 1)
            v.scalar_tensor_tensor(dt, big, m.log_small[:], p, ALU.subtract, ALU.add)\
                .then_inc(f[f"dt_ready{b}"], 1)

    def front_vector(self, v, u):
        m, f = self.m, self.f
        if u == 0:
            self.ln.statistics(v)
        if u == 2:
            self.ln.normalise(v)
        for b in range(HB):
            if u == SLOT[after("bc", b) - 1] + 1:
                v.wait_ge(f["bc_hi"], b + 1)
                v.tensor_tensor(m.rest[:, b, :], self.chip.bank[0:2 * DS, 7, :], m.bc[0:2 * DS, self.cols(b)],
                                ALU.subtract).then_inc(f["emptied"], 1)
            if u == SLOT[after("bc", b) - 1] + 4:
                v.wait_ge(f["bc_mid"], b + 1)
                v.wait_ge(f["emptied"], after("bc", b))
                v.tensor_tensor(m.bc[4 * DS:6 * DS, self.cols(b)], m.rest[:, b, :], m.mid[:, b, :],
                                ALU.subtract).then_inc(f["bc_lo"], 1)
        for b in range(HB):
            if SERIES_AT[b] <= u < SERIES_AT[b] + SERIES_STEPS:
                self.soft_plus(v, b, u - SERIES_AT[b])

    def front_pool(self, g, u):
        m, f, front = self.m, self.f, self.front
        if u == 0 and self.new:
            g.wait_ge(f["w_here"], 16 * self.loads)
            g.tensor_tensor(m.taps[:], m.in_w[:, 0:DI].unsqueeze(1).broadcast_to([D, DC, DI]), m.taps[:],
                            ALU.mult).then_inc(f["tapped"], 1)
        if u == 1:
            g.wait_ge(f["a_exp"], 1)
            g.tensor_scalar(m.a[:, front], m.a[:, front], -1.0, None, ALU.mult).then_inc(f["a_neg"], 1)
        if u == NU - 1:
            self.inputs(g, 0)

    def inputs(self, g, b):
        m, f = self.m, self.f
        g.wait_ge(f[f"dt_ready{b}"], 1)
        g.wait_ge(f["x_silu"], 1)
        g.tensor_tensor(m.u[:, :, self.cols(b)], m.dt[:, :, self.cols(b)], m.xs[:, :, self.cols(b)], ALU.mult)\
            .then_inc(f["u_ready"], 1)


def mamba_out(chip, m):
    nc, dram = chip.nc, chip.dram
    with ExitStack() as ctx:
        w, b = chip.sb(ctx, "mo_w", [P, D]), chip.sb(ctx, "mo_b", [P, D])
        xn = m.u[:, 0, :].rearrange("p (t d) -> p t d", d=D)
        ln = LayerNorm(chip, ctx, "mo_ln", m.res, xn)
        here, step = chip.sem("mo_here"), chip.sem("mo_step")
        over_t = lambda row: row[:].unsqueeze(1).broadcast_to([P, NT, D])
        with nc.Block() as block:
            @block.sync
            def _(sp):
                sp.dma_start(w[:], dram["mb_fw"][0:1, :].broadcast_to([P, D])).then_inc(here, 16)
                sp.dma_start(b[:], dram["mb_fb"][0:1, :].broadcast_to([P, D])).then_inc(here, 16)

            @block.scalar
            def _(a):
                ln.scalar(a)

            @block.gpsimd
            def _(g):
                g.wait_ge(here, 32)
                g.tensor_tensor(chip.x[:], chip.x[:], over_t(b), ALU.add).then_inc(step, 1)

            @block.vector
            def _(v):
                ln.vector(v)
                v.wait_ge(here, 32)
                v.wait_ge(ln.ready, 1)
                v.wait_ge(step, 1)
                v.tensor_tensor(xn[:], xn[:], over_t(w), ALU.mult).then_inc(step, 1)
                v.wait_ge(step, 2)
                v.tensor_tensor(chip.x[:], chip.x[:], xn[:], ALU.add).then_inc(step, 1)


def more_mamba(r, a):
    g = lambda n: a["L1_attn_" + n]
    f = np.float32
    by_chunk = lambda v: v.reshape(NL, NCH, P, -1).transpose(0, 2, 1, 3).reshape(NL, P, -1)
    rows, n = np.arange(REP), np.arange(2 * DS)
    pick = np.repeat((rows[:, None] % (2 * DS) == n[None, :]).astype(f)[:, :, None], P, axis=2)
    r.update(
        mb_in=g("in_proj_w").transpose(0, 2, 1), mb_xp=by_chunk(g("x_proj_w").transpose(0, 2, 1)),
        mb_dtp=g("dt_proj_w").transpose(0, 2, 1), mb_out=by_chunk(g("out_proj_w").transpose(0, 2, 1)),
        mb_col=np.concatenate([g("norm_w")[:, :, None], g("norm_b")[:, :, None], by_chunk(g("conv_b")),
                               by_chunk(g("dt_proj_b")), by_chunk(g("D_param"))], axis=2),
        mb_a=by_chunk(g("A_log")), mb_conv=g("conv_w").transpose(0, 2, 1).reshape(NL, -1),
        mb_fw=g("fnorm_w").reshape(1, -1), mb_fb=g("fnorm_b").reshape(1, -1), pick=pick.reshape(REP, -1))


NC = 7
CW = 74
LAST_CW = S - (NC - 1) * CW
LANES = 32
STEPS = CTX + NC - 1
RING = 8
BIG = 1e30


def alignment(chip):
    nc = chip.nc
    dist_dram = nc.dram_tensor("dist_scratch", (CTX, B, S), F32, kind="Internal").ap()
    cost_dram = nc.dram_tensor("cost_scratch", (CTX + 1, B, S + 1), F32, kind="Internal").ap()
    with ExitStack() as stage:
        c = chip.sb(stage, "d_c", [CTX, B, D])
        big_row = chip.sb(stage, "d_big", [CTX + 1, B, S + 1])
        distances(chip, c, dist_dram, cost_dram, big_row)
        accumulate_costs(chip, dist_dram, cost_dram)
        trace_back(chip, c, cost_dram)


def distances(chip, c, dist_dram, cost_dram, big):
    nc, dram, bank = chip.nc, chip.dram, chip.bank
    with ExitStack() as ctx:
        sb = lambda n, shape, dt=F32: chip.sb(ctx, "dd_" + n, shape, dt)
        xn, xnt, sq = sb("xn", [P, NT, D]), sb("xnt", [P, TOK]), sb("sq", [P, TOK])
        ct, ones = sb("ct", [D, B * CTX]), sb("ones", [D, CTX])
        csq, cc = sb("csq", [CTX, B, D]), sb("cc", [CTX, B])
        d2, safe = sb("d2", [CTX, B, S]), sb("safe", [CTX, B, S])
        log, inv = sb("log", [CTX, B, S]), sb("inv", [CTX, B, S])
        root, err = sb("root", [CTX, B, S]), sb("err", [CTX, B, S])
        ln = LayerNorm(chip, ctx, "dd_ln", chip.x, xn)
        names = ("here", "ct_done", "ct_ready", "t_done", "xnt_ready", "sq_ready", "ones_set", "prod", "csqd", "ccd",
                 "d2d", "safed", "logd", "invd", "step", "dist", "stored", "big_set", "border")
        s = {n: chip.sem("dd_" + n) for n in names}
        with nc.Block() as block:
            @block.sync
            def _(sp):
                sp.dma_start(c[:], dram["ctx"].rearrange("b k d -> k b d")).then_inc(s["here"], 16)
                sp.wait_ge(s["big_set"], 1)
                sp.dma_start(cost_dram[:, :, :], big[:]).then_inc(s["border"], 16)
                sp.wait_ge(s["border"], 16)
                for b in range(B):
                    sp.wait_ge(s["dist"], b + 1)
                    sp.dma_start(dist_dram[:, b, :], root[:, b, :]).then_inc(s["stored"], 16)
                sp.wait_ge(s["stored"], 16 * B)

            @block.gpsimd
            def _(g):
                g.memset(big[:], BIG).then_inc(s["big_set"], 1)
                g.memset(ones[:], 1.0).then_inc(s["ones_set"], 1)

            @block.tensor
            def _(pe):
                pe.wait_ge(s["here"], 16)
                for b in range(B):
                    last = pe.transpose(bank[:, 4, b * CTX:(b + 1) * CTX], c[:, b, :], chip.ident[0:CTX, 0:CTX])
                last.then_inc(s["ct_done"], 1)
                pe.wait_ge(ln.ready, 1)
                feature_major(pe, chip, xn, s["t_done"])
                pe.wait_ge(s["ones_set"], 1)
                pe.wait_ge(s["ct_ready"], 1)
                for b in range(B):
                    cols = slice(b * S, (b + 1) * S)
                    pe.wait_ge(s["xnt_ready"], b + 1)
                    pe.wait_ge(s["sq_ready"], b + 1)
                    pe.matmul(bank[0:CTX, b, :], ones[:], sq[:, cols], start=True, stop=False)
                    pe.matmul(bank[0:CTX, b, :], ct[:, b * CTX:(b + 1) * CTX], xnt[:, cols], start=False, stop=True)\
                        .then_inc(s["prod"], 1)

            @block.scalar
            def _(a):
                a.wait_ge(s["ct_done"], 1)
                a.activation(ct[:], bank[:, 4, 0:B * CTX], ACT.Copy, scale=-2.0).then_inc(s["ct_ready"], 1)
                ln.scalar(a)
                for b in range(B):
                    cols = slice(b * S, (b + 1) * S)
                    a.wait_ge(s["t_done"], b + 1)
                    a.activation(xnt[:, cols], bank[:, b, :], ACT.Copy).then_inc(s["xnt_ready"], 1)
                    a.activation(sq[:, cols], bank[:, b, :], ACT.Square).then_inc(s["sq_ready"], 1)
                for b in range(B):
                    a.wait_ge(s["safed"], b + 1)
                    a.activation(log[:, b, :], safe[:, b, :], ACT.Ln).then_inc(s["logd"], 1)
                    a.wait_ge(s["logd"], b + 1)
                    a.activation(inv[:, b, :], log[:, b, :], ACT.Exp, scale=-0.5).then_inc(s["invd"], 1)

            @block.vector
            def _(v):
                v.wait_ge(s["here"], 16)
                v.tensor_tensor(csq[:], c[:], c[:], ALU.mult).then_inc(s["csqd"], 1)
                v.wait_ge(s["csqd"], 1)
                v.tensor_reduce(cc[:], csq[:], AX.X, ALU.add).then_inc(s["ccd"], 1)
                ln.vector(v)
                v.wait_ge(s["ccd"], 1)
                for b in range(B):
                    v.wait_ge(s["prod"], b + 1)
                    v.tensor_scalar(d2[:, b, :], bank[0:CTX, b, :], cc[:, b:b + 1], 0.0, ALU.add, ALU.max)\
                        .then_inc(s["d2d"], 1)
                    v.wait_ge(s["d2d"], b + 1)
                    v.tensor_scalar(safe[:, b, :], d2[:, b, :], 1e-18, None, ALU.max).then_inc(s["safed"], 1)
                chain = Chain(v, s["step"])
                for b in range(B):
                    v.wait_ge(s["invd"], b + 1)
                    chain.do(v.tensor_tensor(root[:, b, :], d2[:, b, :], inv[:, b, :], ALU.mult))
                    chain.do(v.tensor_tensor(err[:, b, :], root[:, b, :], root[:, b, :], ALU.mult))
                    chain.do(v.tensor_tensor(err[:, b, :], d2[:, b, :], err[:, b, :], ALU.subtract))
                    chain.do(v.tensor_tensor(err[:, b, :], err[:, b, :], inv[:, b, :], ALU.mult))
                    v.scalar_tensor_tensor(root[:, b, :], err[:, b, :], 0.5, root[:, b, :], ALU.mult, ALU.add)\
                        .then_inc(s["dist"], 1)


def accumulate_costs(chip, dist_dram, cost_dram):
    nc = chip.nc
    with ExitStack() as ctx:
        sb = lambda n, shape, dt=F32: chip.sb(ctx, "dc_" + n, shape, dt)
        dist, cost = sb("dist", [LANES, STEPS, CW]), sb("cost", [LANES, STEPS, CW])
        ring, least = sb("ring", [LANES, RING, CW + 1]), sb("least", [LANES, 2, CW])
        first = sb("first", [LANES, 1])
        names = ("set", "dist_set", "dist_here", "least", "row", "passed", "kept", "border", "stored")
        s = {n: chip.sem("dc_" + n) for n in names}
        shift = [(p - B) % LANES for p in range(LANES)]

        def above(v, j):
            v.tensor_tensor(least[:, (j + 1) % 2, :], ring[:, j, 1:CW + 1], ring[:, j, 0:CW], ALU.min)\
                .then_inc(s["least"], 1)

        def row_step(v, k, j, initial=None, last=False):
            at = k * RING + j
            v.wait_ge(s["least"], at + 1)
            if initial is None:
                v.wait_ge(s["passed"], at)
            if not isinstance(k, int) or k > 0:
                v.wait_ge(s["kept"], at - RING + 1)
            v.tensor_tensor_scan(ring[:, j, 1:CW + 1], least[:, j % 2, :], dist[:, at, :],
                                 ring[:, j, 0:1] if initial is None else initial, ALU.min, ALU.add)\
                .then_inc(s["row"], 1)
            v.wait_ge(s["row"], at + 1)
            if not last:
                above(v, j)
                v.stream_shuffle(ring[:, (j + 1) % RING, 0:1], ring[:, j, CW:CW + 1], shift).then_inc(s["passed"], 1)

        def keep_row(a, k, j):
            at = k * RING + j
            a.wait_ge(s["row"], at + 1)
            a.activation(cost[:, at, :], ring[:, j, 1:CW + 1], ACT.Copy).then_inc(s["kept"], 1)

        FULL = STEPS // RING
        with nc.Block() as block:
            @block.sync
            def _(sp):
                sp.wait_ge(s["dist_set"], 1)
                for c in range(NC):
                    w = CW if c < NC - 1 else LAST_CW
                    sp.dma_start(dist[c * B:(c + 1) * B, c:c + CTX, 0:w],
                                 dist_dram[:, :, c * CW:c * CW + w].rearrange("i b j -> b i j"))\
                        .then_inc(s["dist_here"], 16)
                sp.wait_ge(s["kept"], STEPS)
                for c in range(NC):
                    w = CW if c < NC - 1 else LAST_CW
                    sp.dma_start(cost_dram[1:CTX + 1, :, 1 + c * CW:1 + c * CW + w].rearrange("i b j -> b i j"),
                                 cost[c * B:(c + 1) * B, c:c + CTX, 0:w]).then_inc(s["stored"], 16)
                sp.wait_ge(s["stored"], 16 * NC)

            @block.gpsimd
            def _(g):
                g.memset(dist[:], BIG).then_inc(s["dist_set"], 1)

            @block.vector
            def _(v):
                v.memset(ring[:], BIG).then_inc(s["set"], 1)
                v.memset(first[:], BIG).then_inc(s["set"], 1)
                v.wait_ge(s["set"], 2)
                v.memset(first[0:B, :], 0.0).then_inc(s["set"], 1)
                v.wait_ge(s["set"], 3)
                v.wait_ge(s["dist_here"], 16 * NC)
                above(v, RING - 1)
                for j in range(RING):
                    row_step(v, 0, j, initial=first[:] if j == 0 else None)
                with v.Fori(1, FULL) as k:
                    for j in range(RING):
                        row_step(v, k, j)
                for j in range(STEPS - FULL * RING):
                    row_step(v, FULL, j, last=(FULL * RING + j == STEPS - 1))

            @block.scalar
            def _(a):
                with a.Fori(0, FULL) as k:
                    for j in range(RING):
                        keep_row(a, k, j)
                for j in range(STEPS - FULL * RING):
                    keep_row(a, FULL, j)


def trace_back(chip, c, cost_dram):
    nc, dram, bank = chip.nc, chip.dram, chip.bank
    UNROLL = 19
    assert (CTX - 1) % UNROLL == 0
    with ExitStack() as ctx:
        sb = lambda n, shape, dt=F32: chip.sb(ctx, "db_" + n, shape, dt)
        here_cost, above = sb("cur", [CTX, B, S + 1]), sb("above", [CTX, B, S + 1])
        leave, diag = sb("leave", [CTX, B, S]), sb("diag", [CTX, B, S])
        start = sb("start", [CTX, B, S])
        follow16 = sb("follow16", [CTX, B, S], F16)
        column = sb("column", [P, S])
        table = sb("table", [B, CTX, S], F16)
        end, hit = sb("end", [B, CTX]), sb("hit", [B, 2, S])
        endt, startt, picked = sb("endt", [CTX, B]), sb("startt", [CTX, B]), sb("picked", [CTX, B, S])
        names = ("here", "colh", "step", "table_ready", "table_here", "end_set", "hop", "end_done", "onpath", "spread", "pick",
                 "scanned")
        s = {n: chip.sem("db_" + n) for n in names}
        with nc.Block() as block:
            @block.sync
            def _(sp):
                sp.dma_start(here_cost[:], cost_dram[1:CTX + 1, :, :]).then_inc(s["here"], 16)
                sp.dma_start(above[:], cost_dram[0:CTX, :, :]).then_inc(s["here"], 16)
                sp.dma_start(column[:], dram["column"][0:1, :].broadcast_to([P, S])).then_inc(s["here"], 16)
                for b in range(B):
                    sp.wait_ge(s["table_ready"], b + 1)
                    sp.dma_start(table[b:b + 1, :, :], follow16[:, b, :]).then_inc(s["table_here"], 16)

            @block.vector
            def _(v):
                chain = Chain(v, s["step"])
                col = column[0:CTX, :].unsqueeze(1).broadcast_to([CTX, B, S])
                up, up_left, left = above[:, :, 1:S + 1], above[:, :, 0:S], here_cost[:, :, 0:S]
                v.wait_ge(s["here"], 48)
                chain.do(v.tensor_tensor(leave[:], up, up_left, ALU.min))
                v.tensor_tensor(leave[:], leave[:], left, ALU.is_le).then_inc(s["step"], 1)
                v.tensor_tensor(diag[:], up_left, up, ALU.is_le).then_inc(s["step"], 1)
                chain.at += 2
                v.wait_ge(s["step"], chain.at)
                v.tensor_tensor(picked[:], col, diag[:], ALU.subtract).then_inc(s["step"], 1)
                chain.at += 1
                v.wait_ge(s["step"], chain.at)
                v.tensor_tensor(diag[:], picked[:], leave[:], ALU.mult).then_inc(s["step"], 1)
                chain.at += 1
                v.wait_ge(s["step"], chain.at)
                for b in range(B):
                    v.tensor_tensor_scan(follow16[:, b, :], diag[:, b, :], diag[:, b, :], 0.0, ALU.max, ALU.max)\
                        .then_inc(s["table_ready"], 1)
                v.tensor_tensor(leave[:], col, leave[:], ALU.mult).then_inc(s["step"], 1)
                chain.at += 1
                v.memset(end[:, CTX - 1:CTX], float(S)).then_inc(s["end_set"], 1)
                v.wait_ge(s["step"], chain.at)
                for b in range(B):
                    v.tensor_tensor_scan(start[:, b, :], leave[:, b, :], leave[:, b, :], 0.0, ALU.max, ALU.max)\
                        .then_inc(s["scanned"], 1)
                v.wait_ge(s["end_set"], 1)
                v.wait_ge(s["table_here"], 16 * B)
                with v.Fori(0, (CTX - 1) // UNROLL) as k:
                    for j in range(UNROLL):
                        i = (CTX - 1 - j) - k * UNROLL
                        v.scalar_tensor_tensor(hit[:, j % 2, :], column[0:B, :], end[:, bass.ds(i, 1)], table[:, i, :],
                                               ALU.is_equal, ALU.mult, accum_out=end[:, bass.ds(i - 1, 1)])\
                            .then_inc(s["hop"], 1)
                        v.wait_ge(s["hop"], k * UNROLL + j + 1)
                v.wait_ge(s["end_done"], 1)
                v.tensor_copy(endt[:], bank[0:CTX, 0, 0:B]).then_inc(s["step"], 1)
                chain.at += 1
                v.wait_ge(s["step"], chain.at)
                v.wait_ge(s["scanned"], B)
                for b in range(B):
                    v.scalar_tensor_tensor(picked[:, b, :], column[0:CTX, :], endt[:, b:b + 1], start[:, b, :],
                                           ALU.is_equal, ALU.mult, accum_out=startt[:, b:b + 1]).then_inc(s["step"], 1)
                    v.tensor_scalar(diag[:, b, :], column[0:CTX, :], endt[:, b:b + 1], None, ALU.is_le)\
                        .then_inc(s["step"], 1)
                chain.at += 2 * B
                v.wait_ge(s["step"], chain.at)
                for b in range(B):
                    v.scalar_tensor_tensor(picked[:, b, :], column[0:CTX, :], startt[:, b:b + 1], diag[:, b, :],
                                           ALU.is_ge, ALU.mult).then_inc(s["onpath"], 1)
                for b in range(B):
                    v.wait_ge(s["spread"], b + 1)
                    xb = chip.x[:, b * ST:(b + 1) * ST, :].rearrange("p t d -> p (t d)")
                    v.tensor_tensor(xb, xb, bank[:, 4 + b, :], ALU.add).then_inc(s["pick"], 1)

            @block.tensor
            def _(pe):
                pe.wait_ge(s["hop"], CTX - 1)
                pe.wait_ge(s["end_set"], 1)
                pe.transpose(bank[0:CTX, 0, 0:B], end[:], chip.ident[0:B, 0:B]).then_inc(s["end_done"], 1)
                for b in range(B):
                    pe.wait_ge(s["onpath"], b + 1)
                    for j in range(ST):
                        last = pe.matmul(bank[:, 4 + b, j * D:(j + 1) * D], picked[:, b, j * P:(j + 1) * P], c[:, b, :],
                                         start=True, stop=True)
                    last.then_inc(s["spread"], 1)


def more_alignment(r, a):
    r["column"] = np.arange(1, S + 1, dtype=np.float32).reshape(1, -1)


INNER = 512
NI = INNER // P
ROUND = 1.5 * 2.0 ** 23


def ternary_feed_forward(chip):
    with ExitStack() as stage:
        wg = chip.sb(stage, "t_wg", [P, INNER], BF16)
        wu = chip.sb(stage, "t_wu", [P, INNER], BF16)
        wd = chip.sb(stage, "t_wd", [P, NI, D], BF16)
        unit = chip.sb(stage, "t_unit", [P, 3])
        identb = chip.sb(stage, "t_identb", [P, P], BF16)
        xq = chip.sb(stage, "t_xq", [P, NT, D], BF16)
        step_x = chip.sb(stage, "t_step_x", [P, NT])
        quantize_inputs(chip, (wg, wu, wd), unit, identb, xq, step_x)
        feed_forward(chip, (wg, wu, wd), unit, identb, xq, step_x)


def quantize_inputs(chip, weights, unit, identb, xq, step_x):
    nc, dram, bank = chip.nc, chip.dram, chip.bank
    names = ("t_wg", "t_wu", "t_wd")
    with ExitStack() as ctx:
        sb = lambda n, shape, dt=F32: chip.sb(ctx, "q_" + n, shape, dt)
        xn, scaled = sb("xn", [P, NT, D]), sb("scaled", [P, NT, D])
        raw = [sb("raw" + n, [P, INNER]) for n in names]
        absum, ones, mean, scale = sb("absum", [P, 3]), sb("ones", [P, P]), sb("mean", [P, 3]), sb("scale", [P, 3])
        peak, rpeak, scale_x = sb("peak", [P, NT]), sb("rpeak", [P, NT]), sb("scale_x", [P, NT])
        ln = LayerNorm(chip, ctx, "q_ln", chip.x, xn)
        here, ones_set, summed, step = (chip.sem("q_" + n) for n in ("here", "ones_set", "summed", "step"))
        idb = chip.sem("q_idb")
        with nc.Block() as block:
            @block.sync
            def _(sp):
                for n, t in zip(names, raw):
                    sp.dma_start(t[:], dram[n][:, :]).then_inc(here, 16)

            @block.gpsimd
            def _(g):
                g.memset(ones[:], 1.0).then_inc(ones_set, 1)
                g.tensor_copy(identb[:], chip.ident[:]).then_inc(idb, 1)

            @block.tensor
            def _(pe):
                pe.wait_ge(ones_set, 1)
                pe.wait_ge(step, 3)
                pe.matmul(bank[:, 0, 0:3], ones[:], absum[:], start=True, stop=True).then_inc(summed, 1)

            @block.scalar
            def _(a):
                ln.scalar(a)

            @block.vector
            def _(v):
                chain = Chain(v, step)
                v.wait_ge(here, 48)
                for n in range(3):
                    v.tensor_reduce(absum[:, n:n + 1], raw[n][:], AX.X, ALU.add, apply_absolute_value=True)\
                        .then_inc(step, 1)
                chain.at = 3
                ln.vector(v)
                v.wait_ge(summed, 1)
                chain.do(v.tensor_scalar(mean[:], bank[:, 0, 0:3], 1.0 / (INNER * D), 1e-5, ALU.mult, ALU.max))
                chain.do(v.reciprocal(scale[:], mean[:]))
                v.reciprocal(unit[:], scale[:]).then_inc(step, 1)
                chain.at += 1
                for n in range(3):
                    v.tensor_scalar(raw[n][:], raw[n][:], scale[:, n:n + 1], ROUND, ALU.mult, ALU.add).then_inc(step, 1)
                chain.at += 3
                v.wait_ge(step, chain.at)
                for n in range(3):
                    v.tensor_scalar(raw[n][:], raw[n][:], ROUND, 1.0, ALU.subtract, ALU.min).then_inc(step, 1)
                chain.at += 3
                v.wait_ge(step, chain.at)
                for n in range(3):
                    w = weights[n][:] if n < 2 else weights[n][:].rearrange("p i o -> p (i o)")
                    v.tensor_scalar(w, raw[n][:], -1.0, None, ALU.max).then_inc(step, 1)
                chain.at += 3
                v.wait_ge(ln.ready, 1)
                chain.do(v.tensor_reduce(peak[:], xn[:], AX.X, ALU.max, apply_absolute_value=True))
                chain.do(v.tensor_scalar(peak[:], peak[:], 1e-5, None, ALU.max))
                chain.do(v.reciprocal(rpeak[:], peak[:]))
                chain.do(v.tensor_scalar(scale_x[:], rpeak[:], 127.0, None, ALU.mult))
                v.reciprocal(step_x[:], scale_x[:]).then_inc(step, 1)
                chain.at += 1
                chain.do(v.tensor_tensor(scaled[:], xn[:], scale_x[:].unsqueeze(2).broadcast_to([P, NT, D]), ALU.mult))
                chain.do(v.tensor_scalar(scaled[:], scaled[:], ROUND, -ROUND, ALU.add, ALU.add))
                chain.do(v.tensor_scalar(xq[:], scaled[:], 127.0, -128.0, ALU.min, ALU.max))


def feed_forward(chip, weights, unit, identb, xq, step_x):
    nc, bank = chip.nc, chip.bank
    wg, wu, wd = weights
    with ExitStack() as ctx:
        sb = lambda n, shape, dt=F32: chip.sb(ctx, "f_" + n, shape, dt)
        per_gate, per_up = sb("per_gate", [P, NT]), sb("per_up", [P, NT])
        xt, hqt = sb("xt", [P, 2, P], BF16), sb("hqt", [P, 2, NI, P], BF16)
        act, h, hs = sb("act", [P, 2, INNER]), sb("h", [P, 2, INNER]), sb("hs", [P, 2, INNER])
        hq = sb("hq", [P, 2, INNER], BF16)
        peak, rpeak, scale = sb("peak", [P, NT]), sb("rpeak", [P, NT]), sb("scale", [P, NT])
        per_down = sb("per_down", [P, NT])
        names = ("per", "xt_done", "xt_out", "gated", "acted", "joined", "hq_ready", "hqt_done", "hqt_out", "down",
                 "added", "peaked", "clipped", "recip", "scaled", "rounded", "stepd")
        s = {n: chip.sem("f_" + n) for n in names}
        xt_ps = lambda t: bank[:, 4, :].bitcast(BF16)[:, (t % 2) * 512:(t % 2) * 512 + P]
        hqt_ps = lambda t: bank[:, 5, :].bitcast(BF16)[:, (t % 2) * 512:(t % 2) * 512 + INNER]
        with nc.Block() as block:
            @block.tensor
            def _(pe):
                for n in range(NT + 2):
                    if n < NT:
                        t = n
                        if t >= 2:
                            pe.wait_ge(s["xt_out"], t - 1)
                        pe.transpose(xt_ps(t), xq[:, t, :], identb[:]).then_inc(s["xt_done"], 1)
                        pe.wait_ge(s["xt_out"], t + 1)
                        if t >= 2:
                            pe.wait_ge(s["joined"], t - 1)
                        pe.matmul(bank[:, 2 * (t % 2), :], xt[:, t % 2, :], wg[:], start=True, stop=True)
                        pe.matmul(bank[:, 2 * (t % 2) + 1, :], xt[:, t % 2, :], wu[:], start=True, stop=True)\
                            .then_inc(s["gated"], 1)
                    if n >= 2:
                        t = n - 2
                        pe.wait_ge(s["hq_ready"], t + 1)
                        if t >= 2:
                            pe.wait_ge(s["hqt_out"], t - 1)
                        for i in range(NI):
                            last = pe.transpose(hqt_ps(t)[:, i * P:(i + 1) * P], hq[:, t % 2, i * P:(i + 1) * P], identb[:])
                        last.then_inc(s["hqt_done"], 1)
                        pe.wait_ge(s["hqt_out"], t + 1)
                        if t >= 2:
                            pe.wait_ge(s["added"], t - 1)
                        for i in range(NI):
                            last = pe.matmul(bank[:, 6 + t % 2, 0:D], hqt[:, t % 2, i, :], wd[:, i, :],
                                             start=(i == 0), stop=(i == NI - 1))
                        last.then_inc(s["down"], 1)

            @block.scalar
            def _(a):
                a.wait_ge(s["per"], 2)
                for n in range(NT + 2):
                    if n < NT:
                        t = n
                        a.wait_ge(s["xt_done"], t + 1)
                        if t >= 2:
                            a.wait_ge(s["gated"], t - 1)
                        a.activation(xt[:, t % 2, :], xt_ps(t), ACT.Copy).then_inc(s["xt_out"], 1)
                        a.wait_ge(s["gated"], t + 1)
                        if t >= 2:
                            a.wait_ge(s["joined"], t - 1)
                        a.activation(act[:, t % 2, :], bank[:, 2 * (t % 2), :], ACT.Silu, scale=per_gate[:, t:t + 1])\
                            .then_inc(s["acted"], 1)
                    if n >= 2:
                        t = n - 2
                        a.wait_ge(s["hqt_done"], t + 1)
                        if t >= 2:
                            a.wait_ge(s["down"], t - 1)
                        a.activation(hqt[:, t % 2].rearrange("p i q -> p (i q)"), hqt_ps(t), ACT.Copy)\
                            .then_inc(s["hqt_out"], 1)

            @block.vector
            def _(v):
                v.tensor_scalar(per_gate[:], step_x[:], unit[:, 0:1], None, ALU.mult).then_inc(s["per"], 1)
                v.tensor_scalar(per_up[:], step_x[:], unit[:, 1:2], None, ALU.mult).then_inc(s["per"], 1)
                v.wait_ge(s["per"], 2)
                for n in range(NT + 3):
                    if n < NT:
                        t = n
                        v.wait_ge(s["acted"], t + 1)
                        if t >= 2:
                            v.wait_ge(s["scaled"], t - 1)
                        v.scalar_tensor_tensor(h[:, t % 2, :], bank[:, 2 * (t % 2) + 1, :], per_up[:, t:t + 1],
                                               act[:, t % 2, :], ALU.mult, ALU.mult).then_inc(s["joined"], 1)
                        v.wait_ge(s["joined"], t + 1)
                        v.tensor_reduce(peak[:, t:t + 1], h[:, t % 2, :], AX.X, ALU.max, apply_absolute_value=True)\
                            .then_inc(s["peaked"], 1)
                        v.wait_ge(s["peaked"], t + 1)
                        v.tensor_scalar(peak[:, t:t + 1], peak[:, t:t + 1], 1e-5, 1.0 / 127.0, ALU.max, ALU.mult)\
                            .then_inc(s["clipped"], 1)
                        v.wait_ge(s["clipped"], t + 1)
                        v.reciprocal(rpeak[:, t:t + 1], peak[:, t:t + 1]).then_inc(s["recip"], 1)
                        v.tensor_scalar(per_down[:, t:t + 1], peak[:, t:t + 1], unit[:, 2:3], None, ALU.mult)\
                            .then_inc(s["stepd"], 1)
                        v.wait_ge(s["recip"], t + 1)
                        if t >= 2:
                            v.wait_ge(s["rounded"], t - 1)
                        v.tensor_scalar(hs[:, t % 2, :], h[:, t % 2, :], rpeak[:, t:t + 1], ROUND, ALU.mult, ALU.add)\
                            .then_inc(s["scaled"], 1)
                        v.wait_ge(s["scaled"], t + 1)
                        v.tensor_scalar(hs[:, t % 2, :], hs[:, t % 2, :], ROUND, 127.0, ALU.subtract, ALU.min)\
                            .then_inc(s["rounded"], 1)
                        v.wait_ge(s["rounded"], t + 1)
                        if t >= 2:
                            v.wait_ge(s["hqt_done"], t - 1)
                        v.tensor_scalar(hq[:, t % 2, :], hs[:, t % 2, :], -128.0, None, ALU.max)\
                            .then_inc(s["hq_ready"], 1)
                    if n >= 3:
                        t = n - 3
                        v.wait_ge(s["down"], t + 1)
                        v.scalar_tensor_tensor(chip.x[:, t, :], bank[:, 6 + t % 2, 0:D], per_down[:, t:t + 1],
                                               chip.x[:, t, :], ALU.mult, ALU.add).then_inc(s["added"], 1)


def more_ternary(r, a):
    r.update(t_wg=a["L1_ffn_w_gate"].T, t_wu=a["L1_ffn_w_up"].T,
             t_wd=a["L1_ffn_w_down"].T.reshape(NI, P, D).transpose(1, 0, 2).reshape(P, INNER))


def self_attention_stage(chip):
    with ExitStack() as stage:
        mixt = chip.sb(stage, "mixt", [P, TOK])
        with ExitStack() as inner:
            values = chip.sb(inner, "values", [P, NT, D])
            qparts = chip.sb(inner, "qparts", [P, 3, TOK], BF16)
            kparts = chip.sb(inner, "kparts", [P, 3, TOK], BF16)
            self_attention_inputs(chip, qparts, kparts, values)
            self_attention(chip, qparts, kparts, values, mixt)
        project_and_add(chip, "a_out", mixt, "wo")


STAGES = (self_attention_stage, cross_attention, experts, mamba, alignment, ternary_feed_forward)


def build(nc, dram, out, stages=STAGES):
    with ExitStack() as ctx:
        chip = Chip(nc, ctx, dram)
        for stage in stages:
            chip.run(stage)
        with nc.semaphore("stored") as stored, nc.Block() as block:
            @block.sync
            def _(sp):
                sp.dma_start(out.rearrange("b (t p) d -> p (b t) d", p=P), chip.x[:]).then_inc(stored, 16)
                sp.wait_ge(stored, 16)


def laid_out(a):
    c = np.ascontiguousarray
    f = np.float32
    by_d = np.arange(D).reshape(H, HD).T.reshape(-1)
    swap = by_d.reshape(HD, H)[np.arange(HD) ^ 1].reshape(-1)
    half = np.arange(HD // 2, dtype=f)
    inv_freq = (f(10000.0) ** (-(half * f(2.0) / f(HD)))).astype(f)
    ang = np.arange(S, dtype=f)[:, None] * inv_freq[None, :]
    of_row = np.arange(D) // H
    cos, sin = np.cos(ang).astype(f).T[of_row // 2], np.sin(ang).astype(f).T[of_row // 2]
    sin = np.where((of_row % 2 == 0)[:, None], -sin, sin)
    k = np.arange(P)
    r = {
        "x": a["x"], "ctx": a["ctx_1024"],
        "ident": np.eye(P, dtype=f),
        "keep": np.concatenate([np.ones((P, 2 * P), f)] + 2 * [(k[:, None] <= k[None, :]).astype(f)], 1),
        "rope_cos": cos, "rope_sin": sin,
        "wq": a["L0_attn_w_q"][by_d].T, "wq_swap": a["L0_attn_w_q"][swap].T,
        "wk": a["L0_attn_w_k"][by_d].T, "wk_swap": a["L0_attn_w_k"][swap].T,
        "wv": a["L0_attn_w_v"].T, "wo": a["L0_attn_w_o"].T,
    }
    for part in (more, more_experts, more_mamba, more_alignment, more_ternary):
        part(r, a)
    return {n: c(v) for n, v in r.items()}


def kernel(**inputs):
    import concourse.bacc as bacc
    from concourse.bass_utils import run_bass_kernel_spmd

    arrays = laid_out({n: np.asarray(v) for n, v in inputs.items()})
    nc = bacc.Bacc("TRN2", target_bir_lowering=False, num_devices=1)
    dram = {n: nc.dram_tensor("in_" + n, a.shape, mybir.dt.from_np(a.dtype), kind="ExternalInput").ap()
            for n, a in arrays.items()}
    out = nc.dram_tensor("out", (B, S, D), F32, kind="ExternalOutput").ap()
    build(nc, dram, out)
    return run_bass_kernel_spmd(nc, [{"in_" + n: a for n, a in arrays.items()}], core_ids=[0]).results[0]["out"]
```

```python
from contextlib import ExitStack

import numpy as np
import concourse.bass as bass
from concourse import mybir

F32 = mybir.dt.float32
BF16 = mybir.dt.bfloat16
F16 = mybir.dt.float16
U32 = mybir.dt.uint32
ALU = mybir.AluOpType
ACT = mybir.ActivationFunctionType
AX = mybir.AxisListType

P = 128
D = 128
B, S = 4, 512
TOK = B * S
NT = TOK // P
ST = S // P
H, HD = 16, 8
CTX = 77
LN_EPS = 1e-5
EXP_AND_LN = "natural_log_exp_and_others"


class Chip:

    def __init__(self, nc, ctx, dram):
        self.nc, self.ctx, self.dram = nc, ctx, dram
        nc.disable_value_cache = True
        self.sem_ctx, self.stage_sems = ctx, []
        self.x = self.sb(ctx, "x_resid", [P, NT, D])
        self.ident = self.sb(ctx, "ident", [P, P])
        self.eps = self.sb(ctx, "eps_col", [P, 1])
        self.bank = ctx.enter_context(nc.psum_tensor("bank", [P, 8, 512], F32))

    def sb(self, ctx, name, shape, dt=F32):
        return ctx.enter_context(self.nc.sbuf_tensor(name, shape, dt))

    def sem(self, name):
        sem = self.sem_ctx.enter_context(self.nc.semaphore(name))
        self.stage_sems.append(sem)
        return sem

    def clear(self, sems):
        with self.nc.Block() as block:
            for n, engine in enumerate((block.vector, block.scalar, block.gpsimd, block.sync, block.tensor)):
                @engine
                def _(e, n=n):
                    for sem in sems[n::5]:
                        e.sem_clear(sem)

    def run(self, stage, *args):
        with ExitStack() as self.sem_ctx:
            self.stage_sems = []
            stage(self, *args)
            self.clear(self.stage_sems)


class Chain:

    def __init__(self, engine, done, at=0):
        self.engine, self.done, self.at = engine, done, at

    def do(self, instruction):
        self.at += 1
        instruction.then_inc(self.done, 1)
        self.engine.wait_ge(self.done, self.at)


class LayerNorm:

    def __init__(self, chip, ctx, name, src, dst):
        self.src, self.dst, self.chip, self.tiles = src, dst, chip, src.shape[1]
        sb = lambda n, shape: chip.sb(ctx, f"{name}_{n}", shape)
        n = self.tiles
        self.stats, self.mean = sb("stats", [P, n, 6]), sb("mean", [P, n])
        self.var, self.tmp = sb("var", [P, n]), sb("tmp", [P, n])
        self.log, self.rstd = sb("log", [P, n]), sb("rstd", [P, n])
        self.stats_done = chip.sem(f"{name}_stats_done")
        self.step_done = chip.sem(f"{name}_step_done")
        self.var_ready = chip.sem(f"{name}_var_ready")
        self.log_ready = chip.sem(f"{name}_log_ready")
        self.rough_ready = chip.sem(f"{name}_rough_ready")
        self.ready = chip.sem(f"{name}_ready")

    def sems(self):
        return [self.stats_done, self.step_done, self.var_ready, self.log_ready, self.rough_ready, self.ready]

    def vector(self, v):
        self.statistics(v)
        self.normalise(v)

    def statistics(self, v):
        st, mean, var, tmp = self.stats, self.mean, self.var, self.tmp
        for t in range(self.tiles):
            v.bn_stats(st[:, t, :], self.src[:, t, :]).then_inc(self.stats_done, 1)
        v.wait_ge(self.stats_done, self.tiles)
        v.tensor_tensor(mean[:], st[:, :, 1], st[:, :, 4], ALU.add).then_inc(self.step_done, 1)
        v.tensor_tensor(tmp[:], st[:, :, 1], st[:, :, 4], ALU.subtract).then_inc(self.step_done, 1)
        v.tensor_tensor(var[:], st[:, :, 2], st[:, :, 5], ALU.add).then_inc(self.step_done, 1)
        v.wait_ge(self.step_done, 3)
        v.tensor_scalar(mean[:], mean[:], 0.5, None, ALU.mult).then_inc(self.step_done, 1)
        v.scalar_tensor_tensor(tmp[:], tmp[:], 0.25, tmp[:], ALU.mult, ALU.mult).then_inc(self.step_done, 1)
        v.tensor_scalar(var[:], var[:], 1.0 / D, LN_EPS, ALU.mult, ALU.add).then_inc(self.step_done, 1)
        v.wait_ge(self.step_done, 6)
        v.tensor_tensor(var[:], var[:], tmp[:], ALU.add).then_inc(self.var_ready, 1)
        v.tensor_tensor(self.dst[:], self.src[:], mean[:].unsqueeze(2).broadcast_to([P, self.tiles, D]),
                        ALU.subtract).then_inc(self.step_done, 1)

    def normalise(self, v):
        var, tmp, rstd = self.var, self.tmp, self.rstd
        chain = Chain(v, self.step_done, at=7)
        v.wait_ge(self.rough_ready, 1)
        chain.do(v.tensor_tensor(tmp[:], rstd[:], rstd[:], ALU.mult))
        chain.do(v.scalar_tensor_tensor(tmp[:], tmp[:], -0.5, var[:], ALU.mult, ALU.mult))
        chain.do(v.scalar_tensor_tensor(rstd[:], tmp[:], 1.5, rstd[:], ALU.add, ALU.mult))
        v.tensor_tensor(self.dst[:], self.dst[:], rstd[:].unsqueeze(2).broadcast_to([P, self.tiles, D]),
                        ALU.mult).then_inc(self.ready, 1)

    def scalar(self, a, load=True):
        if load:
            a.preload_act_table_set(EXP_AND_LN)
        a.wait_ge(self.var_ready, 1)
        a.activation(self.log[:], self.var[:], ACT.Ln).then_inc(self.log_ready, 1)
        a.wait_ge(self.log_ready, 1)
        a.activation(self.rstd[:], self.log[:], ACT.Exp, scale=-0.5).then_inc(self.rough_ready, 1)


def feature_major(eng, chip, src, per_bank_done, banks=range(4)):
    for g, bank in enumerate(banks):
        for j in range(ST):
            last = eng.transpose(chip.bank[:, bank, j * P:(j + 1) * P], src[:, g * ST + j, :], chip.ident[:])
        last.then_inc(per_bank_done, 1)


QPART = (0, 0, 1, 1, 0, 2)
KPART = (0, 1, 0, 1, 2, 0)
SLOTS = len(QPART)


class Stacks:

    def __init__(self, chip, ctx, qparts, kparts):
        self.qparts, self.kparts = qparts, kparts
        self.qs = chip.sb(ctx, "s_q", [P, 2, H, S], BF16)
        self.ks = chip.sb(ctx, "s_k", [P, 2, H, S], BF16)
        self.vpad = chip.sb(ctx, "s_vpad", [P, ST, H * (D + HD)])
        self.stacked = chip.sem("s_stacked")

    def stack(self, sp, b):
        for n in range(SLOTS):
            for parts, st, which in ((self.qparts, self.qs, QPART), (self.kparts, self.ks, KPART)):
                sp.dma_start(st[n * HD:(n + 1) * HD, b % 2, :, :], parts[:, which[n], b * S:(b + 1) * S])\
                    .then_inc(self.stacked, 16)
        sp.wait_ge(self.stacked, 16 * 2 * SLOTS * (b + 1))


def self_attention_inputs(chip, stacks, qstack_src, kstack_src, values):
    nc, dram, bank = chip.nc, chip.dram, chip.bank
    with ExitStack() as ctx:
        xn = chip.sb(ctx, "a_xn", [P, NT, D])
        xnt = chip.sb(ctx, "a_xnt", [P, TOK])
        names = ("wq", "wq_swap", "wk", "wk_swap", "wv")
        w = {n: chip.sb(ctx, "a_" + n, [D, D]) for n in names}
        cos, sin = chip.sb(ctx, "a_cos", [P, S]), chip.sb(ctx, "a_sin", [P, S])
        prod_cos, prod_sin = chip.sb(ctx, "a_pc", [P, 2, S]), chip.sb(ctx, "a_ps", [P, 2, S])
        turned, rest = chip.sb(ctx, "a_turned", [P, 2, S]), chip.sb(ctx, "a_rest", [P, 2, S])
        ln = LayerNorm(chip, ctx, "a_ln", chip.x, xn)
        x_here, w_here = chip.sem("a_x_here"), chip.sem("a_w_here")
        t_done, xnt_ready = chip.sem("a_t_done"), chip.sem("a_xnt_ready")
        qk_done, qk_read = chip.sem("a_qk_done"), chip.sem("a_qk_read")
        v_done = chip.sem("a_v_done")
        prods, turned_ready = chip.sem("a_prods"), chip.sem("a_turned_ready")
        part1, rest_ready = chip.sem("a_part1"), chip.sem("a_rest_ready")
        part2, part3 = chip.sem("a_part2"), chip.sem("a_part3")
        v_out, zeroed = chip.sem("a_v_out"), chip.sem("a_zeroed")
        items = [(b, which) for b in range(B) for which in range(2)]
        def remainder(v, n):
            b, which = items[n]
            parts = kstack_src if which else qstack_src
            v.wait_ge(part1, n + 1)
            v.wait_ge(turned_ready, n + 1)
            if n >= 2:
                v.wait_ge(part2, n - 1)
                v.wait_ge(part3, n - 1)
            v.tensor_tensor(rest[:, n % 2, :], turned[:, n % 2, :], parts[:, 0, b * S:(b + 1) * S],
                            ALU.subtract).then_inc(rest_ready, 1)

        with nc.Block() as block:
            @block.sync
            def _(sp):
                sp.dma_start(chip.x[:], dram["x"].rearrange("b (t p) d -> p (b t) d", p=P)).then_inc(x_here, 16)
                sp.dma_start(chip.ident[:], dram["ident"][:, :]).then_inc(w_here, 16)
                for n in names:
                    sp.dma_start(w[n][:], dram[n][:, :]).then_inc(w_here, 16)
                sp.dma_start(cos[:], dram["rope_cos"][:, :]).then_inc(w_here, 16)
                sp.dma_start(sin[:], dram["rope_sin"][:, :]).then_inc(w_here, 16)
                sp.wait_ge(zeroed, 3)
                for b in range(2):
                    for part in (part1, part2, part3):
                        sp.wait_ge(part, 2 * (b + 1))
                    stacks.stack(sp, b)

            @block.vector
            def _(v):
                v.wait_ge(x_here, 16)
                ln.vector(v)
                v.wait_ge(w_here, 16 * 8)
                for n, (b, which) in enumerate(items):
                    v.wait_ge(qk_done, n + 1)
                    s = n % 2
                    if n >= 2:
                        v.wait_ge(turned_ready, n - 1)
                    v.tensor_tensor(prod_cos[:, s, :], bank[:, 4 + 2 * which, :], cos[:], ALU.mult).then_inc(prods, 1)
                    v.tensor_tensor(prod_sin[:, s, :], bank[:, 5 + 2 * which, :], sin[:], ALU.mult)\
                        .then_inc(qk_read, 1)
                    v.wait_ge(prods, n + 1)
                    v.wait_ge(qk_read, n + 1)
                    if n >= 2:
                        v.wait_ge(part1, n - 1)
                        v.wait_ge(rest_ready, n - 1)
                    v.tensor_tensor(turned[:, s, :], prod_cos[:, s, :], prod_sin[:, s, :], ALU.add)\
                        .then_inc(turned_ready, 1)
                    if n >= 1:
                        remainder(v, n - 1)
                remainder(v, len(items) - 1)

            @block.scalar
            def _(a):
                ln.scalar(a)
                for g in range(B):
                    a.wait_ge(t_done, g + 1)
                    a.activation(xnt[:, g * S:(g + 1) * S], bank[:, g, :], ACT.Copy).then_inc(xnt_ready, 1)
                for n, (b, which) in enumerate(items):
                    parts = kstack_src if which else qstack_src
                    cols = slice(b * S, (b + 1) * S)
                    a.wait_ge(turned_ready, n + 1)
                    a.activation(parts[:, 0, cols], turned[:, n % 2, :], ACT.Copy).then_inc(part1, 1)
                    if which:
                        a.wait_ge(v_done, b + 1)
                        a.activation(values[:, b * ST:(b + 1) * ST, :].rearrange("p t d -> p (t d)"),
                                     bank[:, b, :], ACT.Copy).then_inc(v_out, 1)
                    a.wait_ge(rest_ready, n + 1)
                    a.activation(parts[:, 1, cols], rest[:, n % 2, :], ACT.Copy).then_inc(part2, 1)

            @block.gpsimd
            def _(g):
                for tile in (stacks.qs, stacks.ks):
                    g.memset(tile[:].bitcast(F32), 0.0).then_inc(zeroed, 1)
                g.memset(stacks.vpad[:], 0.0).then_inc(zeroed, 1)
                for n, (b, which) in enumerate(items):
                    parts = kstack_src if which else qstack_src
                    cols = slice(b * S, (b + 1) * S)
                    g.wait_ge(part2, n + 1)
                    g.wait_ge(rest_ready, n + 1)
                    g.tensor_tensor(parts[:, 2, cols], rest[:, n % 2, :], parts[:, 1, cols], ALU.subtract)\
                        .then_inc(part3, 1)

            @block.tensor
            def _(pe):
                pe.wait_ge(w_here, 16 * 8)
                pe.wait_ge(ln.ready, 1)
                feature_major(pe, chip, xn, t_done)
                for b in range(B):
                    pe.wait_ge(xnt_ready, b + 1)
                    cols = xnt[:, b * S:(b + 1) * S]
                    for which in range(2):
                        n = 2 * b + which
                        if n >= 2:
                            pe.wait_ge(qk_read, n - 1)
                        name = ("wq", "wk")[which]
                        pe.matmul(bank[:, 4 + 2 * which, :], w[name][:], cols, start=True, stop=True)
                        pe.matmul(bank[:, 5 + 2 * which, :], w[name + "_swap"][:], cols, start=True, stop=True)\
                            .then_inc(qk_done, 1)
                    for j in range(ST):
                        last = pe.matmul(bank[:, b, j * P:(j + 1) * P], xnt[:, (b * ST + j) * P:(b * ST + j + 1) * P],
                                         w["wv"][:], start=True, stop=True)
                    last.then_inc(v_done, 1)


def self_attention(chip, stacks, values, mixt):
    nc, bank = chip.nc, chip.bank
    SCALE = float(HD) ** -0.5
    qs, ks, vpad, stacked = stacks.qs, stacks.ks, stacks.vpad, stacks.stacked
    units = [(qt, hp) for qt in range(ST) for hp in range(H // 2)]
    NU = len(units)
    DEPTH = 3
    with ExitStack() as ctx:
        keep = chip.sb(ctx, "s_keep", [P, 4, P])
        prob = chip.sb(ctx, "s_prob", [P, 2, 2, S])
        probt = chip.sb(ctx, "s_probt", [P, 2, 2 * ST, P])
        top = chip.sb(ctx, "s_top", [P, 2, 2])
        shift = chip.sb(ctx, "s_shift", [P, 2, 2])
        total = chip.sb(ctx, "s_total", [P, 2, H])
        rtotal, rwide = chip.sb(ctx, "s_rtotal", [P, H]), chip.sb(ctx, "s_rwide", [P, H, HD])
        rturned, rt_out = chip.sb(ctx, "s_rturned", [P, P]), chip.sem("s_rt_out")
        keep_here = chip.sem("s_keep_here")
        scored, topped = chip.sem("s_scored"), chip.sem("s_topped")
        shifted, expd = chip.sem("s_shifted"), chip.sem("s_expd")
        turned, below_out, diag_out = chip.sem("s_turned"), chip.sem("s_below_out"), chip.sem("s_diag_out")
        weighed, rt_ready, mixed_out = chip.sem("s_weighed"), chip.sem("s_rt_ready"), chip.sem("s_mixed_out")
        recip, rt_turned, v_placed = chip.sem("s_recip"), chip.sem("s_rt_turned"), chip.sem("s_v_placed")

        def ptb(hh, kb):
            i = 2 * kb + hh
            return bank[:, 4 + i // 4, (i % 4) * P:(i % 4 + 1) * P]

        def at(b, u):
            qt, hp = units[u % NU]
            return qt, hp, ST * b + u // (H // 2), b + u // NU

        def pipeline(engine, step):
            for n in range(DEPTH):
                step(0, n, True)
            with engine.Fori(0, B - 1) as b:
                for n in range(DEPTH, NU + DEPTH):
                    step(b, n, True)
            for n in range(DEPTH, NU + DEPTH):
                step(B - 1, n, n < NU)

        def place_values(g, b):
            for kb in range(ST):
                g.tensor_copy(vpad[:, kb, :].rearrange("p (h c) -> p h c", h=H)[:, :, 0:HD],
                              values[:, bass.ds(b * ST + kb, 1), :].rearrange("p t (h d) -> p (t h) d", h=H))\
                    .then_inc(v_placed, 1)

        with nc.Block() as block:
            @block.sync
            def _(sp):
                sp.dma_start(keep[:].rearrange("p k q -> p (k q)"), chip.dram["keep"][:, :]).then_inc(keep_here, 16)
                for b in range(2, B):
                    sp.wait_ge(scored, NU * (b - 1))
                    stacks.stack(sp, b)

            @block.gpsimd
            def _(g):
                place_values(g, 0)
                with g.Fori(1, B) as b:
                    g.wait_ge(weighed, NU * b)
                    place_values(g, b)

            @block.tensor
            def _(pe):
                def step(b, n, scores):
                    if scores:
                        qt, hp, _, batch = at(b, n)
                        if n % NU == 0:
                            pe.wait_ge(stacked, 16 * 2 * SLOTS * (batch + 1))
                        if n >= 2:
                            pe.wait_ge(expd, 2 * (NU * b + n - 1))
                        for hh in range(2):
                            h = 2 * hp + hh
                            last = pe.matmul(bank[:, 2 * (n % 2) + hh, :], qs[:, batch % 2, h, qt * P:(qt + 1) * P],
                                             ks[:, batch % 2, h, :], start=True, stop=True)
                        last.then_inc(scored, 1)
                    if n >= 1 and (scores or n <= NU):
                        qt, hp, _, _ = at(b, n - 1)
                        pe.wait_ge(expd, 2 * (NU * b + n))
                        if n >= 2:
                            pe.wait_ge(diag_out, NU * b + n - 1)
                            pe.wait_ge(below_out, NU * b + n - 1)
                        for kb in range(qt + 1):
                            for hh in range(2):
                                last = pe.transpose(ptb(hh, kb), prob[:, (n - 1) % 2, hh, kb * P:(kb + 1) * P],
                                                    chip.ident[:])
                        last.then_inc(turned, 1)
                    if n >= 2 and (scores or n <= NU + 1):
                        qt, hp, tile, _ = at(b, n - 2)
                        pe.wait_ge(diag_out, NU * b + n - 1)
                        pe.wait_ge(below_out, NU * b + n - 1)
                        if hp == 0:
                            pe.wait_ge(v_placed, tile + 1)
                        if hp == 0 and (n - 2) // (H // 2) >= 2:
                            pe.wait_ge(mixed_out, tile - 1)
                        for hh in range(2):
                            h = 2 * hp + hh
                            for kb in range(qt + 1):
                                last = pe.matmul(bank[:, 6 + qt % 2, 0:P], vpad[:, kb, h * D:(h + 1) * D],
                                                 probt[:, (n - 2) % 2, 2 * kb + hh, :],
                                                 start=(h == 0 and kb == 0), stop=(h == H - 1 and kb == qt))
                        last.then_inc(weighed, 1)
                        if hp == H // 2 - 1:
                            pe.wait_ge(rt_ready, tile + 1)
                            pe.transpose(bank[:, 6 + qt % 2, P:2 * P], rwide[:].rearrange("p h d -> p (h d)"),
                                         chip.ident[:]).then_inc(rt_turned, 1)
                pipeline(pe, step)

            @block.vector
            def _(v):
                v.wait_ge(keep_here, 16)

                def step(b, n, scores):
                    if scores:
                        v.wait_ge(scored, NU * b + n + 1)
                        v.tensor_reduce(top[:, n % 2, :], bank[:, 2 * (n % 2):2 * (n % 2) + 2, :], AX.X, ALU.max)\
                            .then_inc(topped, 1)
                        v.wait_ge(topped, NU * b + n + 1)
                        if n >= 2:
                            v.wait_ge(expd, 2 * (NU * b + n - 1))
                        v.tensor_scalar(shift[:, n % 2, :], top[:, n % 2, :], -SCALE, None, ALU.mult)\
                            .then_inc(shifted, 1)
                    if n >= 1 and (scores or n <= NU):
                        qt, hp, tile, _ = at(b, n - 1)
                        v.wait_ge(turned, NU * b + n)
                        if n >= 3:
                            v.wait_ge(weighed, NU * b + n - 2)
                        odd = qt % 2
                        v.tensor_tensor(probt[:, (n - 1) % 2, 2 * (qt - odd):2 * qt + 2, :],
                                        bank[:, 4 + qt // 2, 0:(2 + 2 * odd) * P].rearrange("p (k q) -> p k q", q=P),
                                        keep[:, 2 - 2 * odd:4, :], ALU.mult)\
                            .then_inc(diag_out, 1)
                        if hp == H // 2 - 1:
                            v.reciprocal(rtotal[:], total[:, qt % 2, :]).then_inc(recip, 1)
                            v.wait_ge(recip, tile + 1)
                            v.tensor_copy(rwide[:], rtotal[:].unsqueeze(2).broadcast_to([P, H, HD]))\
                                .then_inc(rt_ready, 1)
                    if n >= 3:
                        qt, hp, tile, _ = at(b, n - 3)
                        if hp == H // 2 - 1:
                            v.wait_ge(rt_turned, tile + 1)
                            v.tensor_copy(rturned[:], bank[:, 6 + qt % 2, P:2 * P]).then_inc(rt_out, 1)
                            v.wait_ge(rt_out, tile + 1)
                            v.tensor_tensor(mixt[:, bass.ds(tile * P, P)], bank[:, 6 + qt % 2, 0:P],
                                            rturned[:], ALU.mult).then_inc(mixed_out, 1)
                pipeline(v, step)

            @block.scalar
            def _(a):
                def step(b, n, scores):
                    if scores:
                        qt, hp, tile, _ = at(b, n)
                        a.wait_ge(shifted, NU * b + n + 1)
                        if n >= 2:
                            a.wait_ge(turned, NU * b + n - 1)
                        if hp == 0 and n // (H // 2) >= 2:
                            a.wait_ge(recip, tile - 1)
                        for hh in range(2):
                            h = 2 * hp + hh
                            a.activation(prob[:, n % 2, hh, :], bank[:, 2 * (n % 2) + hh, :], ACT.Exp,
                                         bias=shift[:, n % 2, hh:hh + 1], scale=SCALE,
                                         accum_out=total[:, qt % 2, h:h + 1]).then_inc(expd, 1)
                    if n >= 1 and (scores or n <= NU):
                        qt, _, _, _ = at(b, n - 1)
                        a.wait_ge(turned, NU * b + n)
                        if n >= 3:
                            a.wait_ge(weighed, NU * b + n - 2)
                        if qt < 2:
                            a.sem_inc(below_out, 1)
                            return
                        a.activation(probt[:, (n - 1) % 2, 0:4, :].rearrange("p t q -> p (t q)"),
                                     bank[:, 4, :], ACT.Copy).then_inc(below_out, 1)
                pipeline(a, step)


def project_and_add(chip, name, mixt, w_name, bias_name=None):
    nc, bank = chip.nc, chip.bank
    with ExitStack() as ctx:
        w = chip.sb(ctx, name + "_w", [D, D])
        bias = chip.sb(ctx, name + "_bias", [P, D])
        here, o_done = chip.sem(name + "_here"), chip.sem(name + "_o_done")
        added = chip.sem(name + "_added")
        with nc.Block() as block:
            @block.sync
            def _(sp):
                sp.dma_start(w[:], chip.dram[w_name][:, :]).then_inc(here, 16)
                if bias_name:
                    sp.dma_start(bias[:], chip.dram[bias_name][0:1, :].broadcast_to([P, D])).then_inc(here, 16)

            @block.tensor
            def _(pe):
                pe.wait_ge(here, 32 if bias_name else 16)
                for g in range(B):
                    for j in range(ST):
                        t = g * ST + j
                        last = pe.matmul(bank[:, 4 + g, j * D:(j + 1) * D], mixt[:, t * P:(t + 1) * P], w[:],
                                         start=True, stop=True)
                    last.then_inc(o_done, 1)

            @block.vector
            def _(v):
                if bias_name:
                    v.wait_ge(here, 32)
                    v.tensor_tensor(chip.x[:], chip.x[:], bias[:].unsqueeze(1).broadcast_to([P, NT, D]), ALU.add)\
                        .then_inc(added, 1)
                    v.wait_ge(added, 1)
                for g in range(B):
                    v.wait_ge(o_done, g + 1)
                    xg = chip.x[:, g * ST:(g + 1) * ST, :].rearrange("p t d -> p (t d)")
                    v.tensor_tensor(xg, xg, bank[:, 4 + g, :], ALU.add).then_inc(added, 1)


XG, XH = 3, 6
XW = XH * CTX


def cross_attention(chip):
    nc, dram, bank = chip.nc, chip.dram, chip.bank
    with ExitStack() as stage:
        mixt = chip.sb(stage, "x_mixt", [P, TOK])
        qt_ = chip.sb(stage, "x_qt", [P, TOK])
        kblk = chip.sb(stage, "x_kblk", [P, B, XG * XH, CTX])
        vpad = chip.sb(stage, "x_vpad", [CTX, B, H * (D + HD)])
        cross_inputs(chip, qt_, kblk, vpad)
        cross_core(chip, qt_, kblk, vpad, mixt)
        project_and_add(chip, "x_out", mixt, "x_wo", "x_bo")


def cross_inputs(chip, q_t, kblk, vpad):
    nc, dram, bank = chip.nc, chip.dram, chip.bank
    with ExitStack() as ctx:
        xn = chip.sb(ctx, "xi_xn", [P, NT, D])
        xnt = chip.sb(ctx, "xi_xnt", [P, TOK])
        w = {n: chip.sb(ctx, "xi_" + n, [D, D]) for n in ("x_wq", "x_wk", "x_wv")}
        bq, bk = chip.sb(ctx, "xi_bq", [D, 1]), chip.sb(ctx, "xi_bk", [D, 1])
        bv = chip.sb(ctx, "xi_bv", [CTX, D])
        own = chip.sb(ctx, "xi_own", [P, XG * XH])
        c = chip.sb(ctx, "xi_c", [CTX, B, D])
        ct, kt = chip.sb(ctx, "xi_ct", [D, B * CTX]), chip.sb(ctx, "xi_kt", [D, B * CTX])
        ln = LayerNorm(chip, ctx, "xi_ln", chip.x, xn)
        here, t_done, xnt_ready = chip.sem("xi_here"), chip.sem("xi_t_done"), chip.sem("xi_xnt_ready")
        ct_done, ct_ready, k_done, v_done = (chip.sem("xi_" + n) for n in ("ct_done", "ct_ready", "k_done", "v_done"))
        kt_ready, q_done, zeroed, out = (chip.sem("xi_" + n) for n in ("kt_ready", "q_done", "zeroed", "out"))
        with nc.Block() as block:
            @block.sync
            def _(sp):
                sp.dma_start(c[:], dram["ctx"].rearrange("b k d -> k b d")).then_inc(here, 16)
                for n in w:
                    sp.dma_start(w[n][:], dram[n][:, :]).then_inc(here, 16)
                sp.dma_start(bq[:], dram["x_bq"][:, :]).then_inc(here, 16)
                sp.dma_start(bk[:], dram["x_bk"][:, :]).then_inc(here, 16)
                sp.dma_start(bv[:], dram["x_bv"][0:1, :].broadcast_to([CTX, D])).then_inc(here, 16)
                sp.dma_start(own[:], dram["own_head"][:, :]).then_inc(here, 16)

            @block.tensor
            def _(pe):
                pe.wait_ge(here, 16 * 8)
                for b in range(B):
                    last = pe.transpose(bank[:, 4, b * CTX:(b + 1) * CTX], c[:, b, :], chip.ident[0:CTX, 0:CTX])
                last.then_inc(ct_done, 1)
                pe.wait_ge(ct_ready, 1)
                pe.matmul(bank[:, 5, 0:B * CTX], w["x_wk"][:], ct[:], start=True, stop=True).then_inc(k_done, 1)
                for b in range(B):
                    last = pe.matmul(bank[0:CTX, 6, b * D:(b + 1) * D], ct[:, b * CTX:(b + 1) * CTX], w["x_wv"][:],
                                     start=True, stop=True)
                last.then_inc(v_done, 1)
                pe.wait_ge(ln.ready, 1)
                feature_major(pe, chip, xn, t_done)
                for b in range(B):
                    pe.wait_ge(xnt_ready, b + 1)
                    pe.matmul(bank[:, b, :], w["x_wq"][:], xnt[:, b * S:(b + 1) * S], start=True, stop=True)\
                        .then_inc(q_done, 1)

            @block.scalar
            def _(a):
                a.wait_ge(here, 16 * 8)
                a.wait_ge(ct_done, 1)
                a.activation(ct[:], bank[:, 4, 0:B * CTX], ACT.Copy).then_inc(ct_ready, 1)
                a.wait_ge(k_done, 1)
                a.activation(kt[:], bank[:, 5, 0:B * CTX], ACT.Identity, bias=bk[:, 0:1]).then_inc(kt_ready, 1)
                ln.scalar(a)
                for b in range(B):
                    a.wait_ge(t_done, b + 1)
                    a.activation(xnt[:, b * S:(b + 1) * S], bank[:, b, :], ACT.Copy).then_inc(xnt_ready, 1)
                for b in range(B):
                    a.wait_ge(q_done, b + 1)
                    a.activation(q_t[:, b * S:(b + 1) * S], bank[:, b, :], ACT.Identity, bias=bq[:, 0:1])\
                        .then_inc(out, 1)

            @block.gpsimd
            def _(g):
                g.memset(vpad[:], 0.0).then_inc(zeroed, 1)
                g.wait_ge(kt_ready, 1)
                for b in range(B):
                    g.tensor_tensor(kblk[:, b, :, :],
                                    kt[:, b * CTX:(b + 1) * CTX].unsqueeze(1).broadcast_to([P, XG * XH, CTX]),
                                    own[:].unsqueeze(2).broadcast_to([P, XG * XH, CTX]), ALU.mult).then_inc(out, 1)

            @block.vector
            def _(v):
                ln.vector(v)
                v.wait_ge(v_done, 1)
                v.wait_ge(here, 16 * 8)
                v.wait_ge(zeroed, 1)
                own_columns = vpad[:].rearrange("k b (h c) -> k b h c", h=H)[:, :, :, 0:HD]
                v.tensor_tensor(own_columns, bank[0:CTX, 6, :].rearrange("k (b h d) -> k b h d", b=B, h=H),
                                bv[:].rearrange("k (h d) -> k h d", h=H).unsqueeze(1).broadcast_to([CTX, B, H, HD]),
                                ALU.add).then_inc(out, 1)


def cross_core(chip, q_t, kblk, vpad, mixt):
    nc, bank = chip.nc, chip.bank
    HALF = H // 2
    with ExitStack() as ctx:
        sb = lambda n, shape: chip.sb(ctx, "xc_" + n, shape)
        top, total, rtotal = sb("top", [P, XG, XH]), sb("total", [P, XG, XH]), sb("rtotal", [P, XG, XH])
        rwide, rturned = sb("rwide", [P, H, HD]), sb("rturned", [P, P])
        low = sb("low", [P, 2, XG, XH, CTX])
        probt = sb("probt", [CTX, 2, HALF, P])
        names = ("scored", "topped", "lowered", "expd", "turned", "turned_out", "weighed", "totalled", "recip",
                 "rt_ready", "rt_turned", "rt_out", "mixed_out")
        s = {n: chip.sem("xc_" + n) for n in names}
        scores = bank[:, 0:XG, 0:XW].rearrange("p g (h k) -> p g h k", h=XH)

        def tile_scores(pe, t):
            for g in range(XG):
                last = pe.matmul(bank[:, g, 0:XW], q_t[:, t * P:(t + 1) * P],
                                 kblk[:, t // ST, g * XH:(g + 1) * XH, :].rearrange("p h k -> p (h k)"),
                                 start=True, stop=True)
            last.then_inc(s["scored"], 1)

        def turn_totals(pe, t):
            pe.wait_ge(s["rt_ready"], t + 1)
            pe.transpose(bank[:, 7, P:2 * P], rwide[:].rearrange("p h d -> p (h d)"), chip.ident[:])\
                .then_inc(s["rt_turned"], 1)

        def add_up(v, t):
            v.wait_ge(s["expd"], t + 1)
            v.tensor_reduce(total[:], low[:, t % 2], AX.X, ALU.add).then_inc(s["totalled"], 1)
            v.wait_ge(s["totalled"], t + 1)
            v.reciprocal(rtotal[:], total[:]).then_inc(s["recip"], 1)
            v.wait_ge(s["recip"], t + 1)
            if t >= 1:
                v.wait_ge(s["rt_turned"], t)
            flat = rtotal[:].rearrange("p g h -> p (g h)")
            v.tensor_copy(rwide[:], flat[:, 0:H].unsqueeze(2).broadcast_to([P, H, HD])).then_inc(s["rt_ready"], 1)

        def divide(v, t):
            v.wait_ge(s["rt_turned"], t + 1)
            v.tensor_copy(rturned[:], bank[:, 7, P:2 * P]).then_inc(s["rt_out"], 1)
            v.wait_ge(s["rt_out"], t + 1)
            v.wait_ge(s["weighed"], t + 1)
            v.tensor_tensor(mixt[:, t * P:(t + 1) * P], bank[:, 7, 0:P], rturned[:], ALU.mult)\
                .then_inc(s["mixed_out"], 1)

        with nc.Block() as block:
            @block.tensor
            def _(pe):
                tile_scores(pe, 0)
                for t in range(NT):
                    for half in range(2):
                        n = 2 * t + half
                        if half == 0:
                            pe.wait_ge(s["expd"], t + 1)
                        if n >= 2:
                            pe.wait_ge(s["turned_out"], n - 1)
                        for j in range(HALF):
                            h = half * HALF + j
                            last = pe.transpose(bank[0:CTX, 3 + 2 * half + j // 4, (j % 4) * P:(j % 4 + 1) * P],
                                                low[:, t % 2, h // XH, h % XH, :], chip.ident[:])
                        last.then_inc(s["turned"], 1)
                        if half == 0:
                            if t >= 1:
                                turn_totals(pe, t - 1)
                            if t + 1 < NT:
                                pe.wait_ge(s["lowered"], t + 1)
                                tile_scores(pe, t + 1)
                    if t >= 1:
                        pe.wait_ge(s["mixed_out"], t)
                    for half in range(2):
                        pe.wait_ge(s["turned_out"], 2 * t + half + 1)
                        for j in range(HALF):
                            h = half * HALF + j
                            last = pe.matmul(bank[:, 7, 0:P], vpad[:, t // ST, h * D:(h + 1) * D], probt[:, half, j, :],
                                             start=(h == 0), stop=(h == H - 1))
                    last.then_inc(s["weighed"], 1)
                turn_totals(pe, NT - 1)

            @block.vector
            def _(v):
                for t in range(NT):
                    v.wait_ge(s["scored"], t + 1)
                    v.tensor_reduce(top[:], scores, AX.X, ALU.max).then_inc(s["topped"], 1)
                    v.wait_ge(s["topped"], t + 1)
                    if t >= 2:
                        v.wait_ge(s["turned"], 2 * (t - 1))
                        v.wait_ge(s["totalled"], t - 1)
                    v.tensor_tensor(low[:, t % 2], scores, top[:].unsqueeze(3).broadcast_to([P, XG, XH, CTX]),
                                    ALU.subtract).then_inc(s["lowered"], 1)
                    if t >= 1:
                        divide(v, t - 1)
                    add_up(v, t)
                divide(v, NT - 1)

            @block.scalar
            def _(a):
                for t in range(NT):
                    a.wait_ge(s["lowered"], t + 1)
                    flat = low[:, t % 2].rearrange("p g h k -> p (g h k)")
                    a.activation(flat, flat, ACT.Exp).then_inc(s["expd"], 1)
                    for half in range(2):
                        a.wait_ge(s["turned"], 2 * t + half + 1)
                        if t >= 1:
                            a.wait_ge(s["weighed"], t)
                        a.activation(probt[:, half].rearrange("k h q -> k (h q)"),
                                     bank[0:CTX, 3 + 2 * half:5 + 2 * half, :].rearrange("k b q -> k (b q)"),
                                     ACT.Copy).then_inc(s["turned_out"], 1)


def more(r, a):
    f = np.float32
    col = lambda n: a[n].reshape(-1, 1)
    row = lambda n: a[n].reshape(1, -1)
    own = (np.arange(P)[:, None] // HD == np.arange(XG * XH)[None, :]).astype(f)
    r.update(x_wq=a["L0_xattn_Wq"].T, x_wk=a["L0_xattn_Wk"].T, x_wv=a["L0_xattn_Wv"].T, x_wo=a["L0_xattn_Wo"].T,
             x_bq=col("L0_xattn_bq"), x_bk=col("L0_xattn_bk"), x_bv=row("L0_xattn_bv"), x_bo=row("L0_xattn_bo"),
             own_head=own)


NE, NSH, TOPK = 16, 2, 2
QE = 4
ACT_E = 1


def experts(chip):
    with ExitStack() as stage:
        u = chip.sb(stage, "e_u", [P, NT, D])
        ut = chip.sb(stage, "e_ut", [P, TOK])
        gates = chip.sb(stage, "e_gates", [P, NT, NE + NSH])
        wr = chip.sb(stage, "e_wr", [D, NE, D])
        ws = chip.sb(stage, "e_ws", [D, NSH, D])
        brs = chip.sb(stage, "e_brs", [NE + NSH, D])
        weights_here = chip.sem("e_weights_here")
        route(chip, u, ut, gates, wr, ws, brs, weights_here)
        mix_experts(chip, u, ut, gates, wr, ws, brs, weights_here)


def route(chip, u, ut, gates, wr, ws, brs, weights_here):
    nc, dram, bank = chip.nc, chip.dram, chip.bank
    with ExitStack() as ctx:
        sb = lambda n, shape, dt=F32: chip.sb(ctx, "r_" + n, shape, dt)
        cent, bias, iota = sb("cent", [D, NE]), sb("bias", [P, NE]), sb("iota", [P, NE])
        score, hit = sb("score", [P, NT, NE]), sb("hit", [P, NT, NE])
        top, tot, rtot = sb("top", [P, NT]), sb("tot", [P, NT]), sb("rtot", [P, NT])
        best, where, wheref = sb("best", [P, NT, 8]), sb("where", [P, NT, 8], U32), sb("wheref", [P, NT, 8])
        ln = LayerNorm(chip, ctx, "r_ln", chip.x, u)
        here, t_done, ut_ready, raw_done = (chip.sem("r_" + n) for n in ("here", "t_done", "ut_ready", "raw_done"))
        step, centred, expd = chip.sem("r_step"), chip.sem("r_centred"), chip.sem("r_expd")
        summed = chip.sem("r_summed")
        with nc.Block() as block:
            @block.sync
            def _(sp):
                sp.dma_start(cent[:], dram["e_cent"][:, :]).then_inc(here, 16)
                sp.dma_start(bias[:], dram["e_bias"][0:1, :].broadcast_to([P, NE])).then_inc(here, 16)
                sp.dma_start(iota[:], dram["iota"][0:1, 0:NE].broadcast_to([P, NE])).then_inc(here, 16)
                sp.dma_start(wr[:], dram["e_wr"].rearrange("e d o -> d e o")).then_inc(weights_here, 16)
                sp.dma_start(ws[:], dram["e_ws"].rearrange("e d o -> d e o")).then_inc(weights_here, 16)
                sp.dma_start(brs[0:NE, :], dram["e_br"][:, :]).then_inc(weights_here, 16)
                sp.dma_start(brs[NE:NE + NSH, :], dram["e_bs"][:, :]).then_inc(weights_here, 16)

            @block.tensor
            def _(pe):
                pe.wait_ge(ln.ready, 1)
                feature_major(pe, chip, u, t_done)
                pe.wait_ge(here, 48)
                pe.wait_ge(ut_ready, B)
                for t in range(NT):
                    last = pe.matmul(bank[:, 4, t * NE:(t + 1) * NE], ut[:, t * P:(t + 1) * P], cent[:],
                                     start=True, stop=True)
                last.then_inc(raw_done, 1)

            @block.scalar
            def _(a):
                ln.scalar(a)
                for g in range(B):
                    a.wait_ge(t_done, g + 1)
                    a.activation(ut[:, g * S:(g + 1) * S], bank[:, g, :], ACT.Copy).then_inc(ut_ready, 1)
                a.wait_ge(centred, 1)
                a.activation(score[:], score[:], ACT.Exp).then_inc(expd, 1)

            @block.gpsimd
            def _(g):
                g.memset(gates[:, :, NE:NE + NSH], 1.0 / NSH).then_inc(summed, 1)
                g.wait_ge(weights_here, 64)
                g.tensor_tensor(ws[:, 0, :], ws[:, 0, :], ws[:, 1, :], ALU.add).then_inc(summed, 1)
                g.wait_ge(summed, 2)
                g.tensor_scalar(ws[:, 0, :], ws[:, 0, :], 1.0 / NSH, None, ALU.mult).then_inc(summed, 1)

            @block.vector
            def _(v):
                over_e = lambda col: col.unsqueeze(2).broadcast_to([P, NT, NE])
                over_t = lambda row: row.unsqueeze(1).broadcast_to([P, NT, NE])
                ln.vector(v)
                v.wait_ge(here, 48)
                v.wait_ge(raw_done, 1)
                chain = Chain(v, step)
                chain.do(v.tensor_tensor(score[:], bank[:, 4, 0:NT * NE].rearrange("p (t e) -> p t e", t=NT),
                                         over_t(bias[:]), ALU.add))
                chain.do(v.tensor_reduce(top[:], score[:], AX.X, ALU.max))
                v.tensor_tensor(score[:], score[:], over_e(top[:]), ALU.subtract).then_inc(centred, 1)
                v.wait_ge(expd, 1)
                chain.do(v.tensor_reduce(tot[:], score[:], AX.X, ALU.add))
                chain.do(v.reciprocal(rtot[:], tot[:]))
                chain.do(v.tensor_tensor(score[:], score[:], over_e(rtot[:]), ALU.mult))
                for t in range(NT):
                    v.max(best[:, t, :], score[:, t, :]).then_inc(step, 1)
                chain.at += NT
                v.wait_ge(step, chain.at)
                for t in range(NT):
                    v.max_index(where[:, t, :], best[:, t, :], score[:, t, :]).then_inc(step, 1)
                chain.at += NT
                v.wait_ge(step, chain.at)
                chain.do(v.tensor_copy(wheref[:], where[:]))
                routed = gates[:, :, 0:NE]
                chain.do(v.tensor_tensor(routed, over_t(iota[:]), over_e(wheref[:, :, 0]), ALU.is_equal))
                chain.do(v.tensor_tensor(routed, routed, over_e(best[:, :, 0]), ALU.mult))
                for k in range(1, TOPK):
                    chain.do(v.tensor_tensor(hit[:], over_t(iota[:]), over_e(wheref[:, :, k]), ALU.is_equal))
                    chain.do(v.tensor_tensor(hit[:], hit[:], over_e(best[:, :, k]), ALU.mult))
                    chain.do(v.tensor_tensor(routed, routed, hit[:], ALU.add))


def mix_experts(chip, u, ut, gates, wr, ws, brs, weights_here):
    nc, bank = chip.nc, chip.bank
    NQ = NE // QE
    DVE_E = QE - ACT_E
    with ExitStack() as ctx:
        gatest = chip.sb(ctx, "m_gatest", [NE + NSH, TOK])
        gated = chip.sb(ctx, "m_gated", [P, 2, NE, D])
        paired = chip.sb(ctx, "m_paired", [P, 2, NE // 2, D])
        routed = chip.sb(ctx, "m_routed", [P, 2, D])
        gt_done, gt_out = chip.sem("m_gt_done"), chip.sem("m_gt_out")
        made, by_vector, by_scalar = chip.sem("m_made"), chip.sem("m_by_vector"), chip.sem("m_by_scalar")
        shared, reduced, joined, plus_u = (chip.sem("m_" + n) for n in ("shared", "reduced", "joined", "plus_u"))
        pairs = chip.sem("m_pairs")
        with nc.Block() as block:
            @block.gpsimd
            def _(g):
                g.tensor_tensor(chip.x[:], chip.x[:], u[:], ALU.add).then_inc(plus_u, 1)
                for t in range(NT):
                    g.wait_ge(by_scalar, NQ * (t + 1))
                    g.wait_ge(by_vector, NQ * (t + 1))
                    if t >= 2:
                        g.wait_ge(reduced, t - 1)
                    g.tensor_tensor(paired[:, t % 2], gated[:, t % 2, 0:NE // 2, :], gated[:, t % 2, NE // 2:, :],
                                    ALU.add).then_inc(pairs, 1)

            @block.tensor
            def _(pe):
                for g in range(4):
                    for j in range(ST):
                        t = g * ST + j
                        last = pe.transpose(bank[0:NE + NSH, g, j * P:(j + 1) * P], gates[:, t, :], chip.ident[:])
                    last.then_inc(gt_done, 1)
                pe.wait_ge(weights_here, 64)
                for t in range(NT):
                    for q in range(NQ):
                        n = t * NQ + q
                        if n < 4:
                            pe.wait_ge(gt_out, n + 1)
                        if n >= 6:
                            pe.wait_ge(by_vector, n - 5)
                            pe.wait_ge(by_scalar, n - 5)
                        pe.matmul(bank[:, n % 6, :], ut[:, t * P:(t + 1) * P],
                                  wr[:, q * QE:(q + 1) * QE, :].rearrange("d e o -> d (e o)"), start=True, stop=True)\
                            .then_inc(made, 1)
                    if t == 0:
                        pe.wait_ge(gt_out, 4)
                    if t >= 2:
                        pe.wait_ge(joined, t - 1)
                    s = bank[:, 6 + t % 2, 0:D]
                    pe.matmul(s, ut[:, t * P:(t + 1) * P], ws[:, 0, :], start=True, stop=False)
                    pe.matmul(s, gatest[:, t * P:(t + 1) * P], brs[:], start=False, stop=True).then_inc(shared, 1)

            @block.scalar
            def _(a):
                for g in range(4):
                    a.wait_ge(gt_done, g + 1)
                    a.activation(gatest[:, g * S:(g + 1) * S], bank[0:NE + NSH, g, :], ACT.Copy).then_inc(gt_out, 1)
                for n in range(NT * NQ):
                    t, q = n // NQ, n % NQ
                    a.wait_ge(by_vector, n + 1)
                    if q == 0 and t >= 2:
                        a.wait_ge(pairs, t - 1)
                    for e in range(DVE_E, QE):
                        last = a.activation(gated[:, t % 2, q * QE + e, :], bank[:, n % 6, e * D:(e + 1) * D],
                                            ACT.Copy, scale=gates[:, t, q * QE + e:q * QE + e + 1])
                    last.then_inc(by_scalar, 1)

            @block.vector
            def _(v):
                v.wait_ge(plus_u, 1)
                for t in range(NT + 2):
                    if t < NT:
                        if t >= 2:
                            v.wait_ge(pairs, t - 1)
                        for q in range(NQ):
                            n = t * NQ + q
                            v.wait_ge(made, n + 1)
                            e = slice(q * QE, q * QE + DVE_E)
                            v.tensor_tensor(gated[:, t % 2, e, :],
                                            bank[:, n % 6, 0:DVE_E * D].rearrange("p (e o) -> p e o", o=D),
                                            gates[:, t, e].unsqueeze(2).broadcast_to([P, DVE_E, D]), ALU.mult)\
                                .then_inc(by_vector, 1)
                    if t >= 2:
                        s = t % 2
                        v.wait_ge(pairs, t - 1)
                        v.tensor_reduce(routed[:, s, :], paired[:, s].rearrange("p e o -> p o e"), AX.X, ALU.add)\
                            .then_inc(reduced, 1)
                    if 1 <= t <= NT:
                        v.wait_ge(shared, t)
                        v.tensor_tensor(chip.x[:, t - 1, :], chip.x[:, t - 1, :], bank[:, 6 + (t - 1) % 2, 0:D], ALU.add)\
                            .then_inc(joined, 1)
                    if t >= 2:
                        v.wait_ge(joined, t - 1)
                        v.wait_ge(reduced, t - 1)
                        v.tensor_tensor(chip.x[:, t - 2, :], chip.x[:, t - 2, :], routed[:, s, :], ALU.add)


def more_experts(r, a):
    T = lambda n: a[n].transpose(0, 2, 1)
    r.update(e_cent=a["L0_ffn_centroids"].T, e_bias=a["L0_ffn_expert_biases"].reshape(1, -1),
             e_wr=T("L0_ffn_Wr"), e_ws=T("L0_ffn_Ws"), e_br=a["L0_ffn_br"], e_bs=a["L0_ffn_bs"],
             iota=np.arange(S, dtype=np.float32).reshape(1, -1))


NL = 4
DI, DS, DR, DC = 256, 16, 64, 4
NCH = DI // P
PAD = DC - 1
HB = B // 2
HT = HB * S
HTT = HT // P
NU = DS * NCH
SMALL = 1 / 16
SERIES = (1.0, -0.49999176, 0.33253264, -0.22751441)
REP = 96
RA = 3
NR = 6
LAG = 3
ITEMS = [
    ("turn", 0, 0), ("turn", 1, 0), ("conv", 0, 0), ("conv", 0, 1), ("gate", 0, 0), ("gate", 0, 1), ("conv", 1, 0),
    ("rank", 0, 0), ("bc", 0, 0), ("dt", 0, 0), ("dt", 0, 1), ("conv", 1, 1), ("gate", 1, 0), ("gate", 1, 1),
    ("rank", 1, 0), ("bc", 1, 0), ("dt", 1, 0), ("dt", 1, 1)]
SLOT = [3, 4, 5, 7, 9, 10, 11, 13, 14, 15, 16, 17, 19, 20, 21, 22, 23, 24]
CONV_UNITS = 2
FREE_BANKS = 4
EVAC = 2
SILU_AT = [11, 21]
SERIES_AT = [18, 26]
SERIES_STEPS = 8
AFTER = 4


def after(kind, b, c=0):
    return ITEMS.index((kind, b, c)) + 1


class MambaTiles:
    def __init__(self, chip, ctx):
        sb = lambda n, shape, dt=F32: chip.sb(ctx, "m_" + n, shape, dt)
        self.res = sb("res", [P, NT, D])
        self.xs, self.zs = sb("xs", [P, NCH, TOK]), sb("zs", [P, NCH, TOK])
        self.dt, self.u = sb("dt", [P, NCH, TOK]), sb("u", [P, NCH, TOK])
        self.bc = sb("bc", [REP, TOK], BF16)
        self.pick = sb("pick", [REP, 2 * DS, P], BF16)
        self.in_w, self.taps = sb("in_w", [D, 2 * DI]), sb("taps", [D, DC, DI])
        self.xp_w, self.dtp_full = sb("xp_w", [P, NCH, DR + 2 * DS]), sb("dtp_w", [P, DI])
        self.dtp_w = self.dtp_full[P - DR:P]
        self.col = sb("col", [P, 2, 2 + 3 * NCH])
        self.a = sb("a", [P, 2, NCH, DS])
        self.out_w = sb("out_w", [P, 2, NCH, D])
        self.xn = sb("xn", [P, HTT, D])
        self.h_t = sb("h_t", [P, HB, PAD + S])
        by_batch = lambda t: t.rearrange("p (b t) d -> p b (t d)", b=HB)
        self.rest = by_batch(self.xn[0:2 * DS])
        self.mid = self.xn[2 * DS:4 * DS].bitcast(BF16)[:, 0:HTT // 2, :].rearrange("p (b t) d -> p b (t d)", b=HB)
        self.rank = by_batch(self.xn[P - DR:P])
        self.mag, self.big = sb("mag", [P, HB, NCH, S]), sb("big", [P, HB, NCH, S])
        self.series = sb("series", [P, HB, NCH, S])
        self.one, self.log_small = sb("one", [P, 1]), sb("log_small", [P, 1])
        self.decay, self.inp = sb("decay", [P, RA, HB, S]), sb("inp", [P, RA, HT])
        self.state, self.read = sb("state", [P, RA, HT]), sb("read", [P, NR, HT])
        self.c_rep = sb("c_rep", [P, 2, HB, S])


def mamba(chip):
    nc, dram = chip.nc, chip.dram
    with ExitStack() as stage:
        m = MambaTiles(chip, stage)
        work = MambaStage(chip, m, stage)
        with ExitStack() as ctx:
            first = LayerNorm(chip, ctx, "m_first", chip.x, m.res)
            here, zero, cast = chip.sem("m_here"), chip.sem("m_zero"), chip.sem("m_cast")
            small = chip.sem("m_small")
            pick32 = m.xs[0:REP].rearrange("p c t -> p (c t)")
            with nc.Block() as block:
                @block.sync
                def _(sp):
                    sp.dma_start(pick32, dram["pick"][:, :]).then_inc(here, 16)
                    work.load(sp, 0)

                @block.gpsimd
                def _(g):
                    g.memset(m.h_t[:], 0.0).then_inc(zero, 1)
                    g.memset(m.decay[:], 0.0).then_inc(zero, 1)
                    g.memset(m.one[:], 1.0).then_inc(small, 1)
                    g.memset(m.log_small[:], SMALL).then_inc(small, 1)

                @block.vector
                def _(v):
                    first.vector(v)

                @block.scalar
                def _(a):
                    first.scalar(a)
                    a.wait_ge(small, 2)
                    a.activation(m.log_small[:], m.log_small[:], ACT.Ln, bias=m.one[:]).then_inc(small, 1)
                    a.wait_ge(here, 16)
                    a.activation(m.pick[:].rearrange("r n p -> r (n p)"), pick32, ACT.Copy).then_inc(cast, 1)
        work.block(core=None, front=0, layer=0, loaded=True)
        with nc.Fori(0, NL - 1) as layer:
            work.block(core=0, front=1, layer=layer)
            work.block(core=1, front=0, layer=layer + 1)
        work.block(core=0, front=1, layer=NL - 1)
        work.block(core=1, front=None)
        mamba_out(chip, m)


class MambaStage:

    def __init__(self, chip, m, ctx):
        self.chip, self.m = chip, m
        names = ("w_here", "tapped", "a_exp", "a_neg", "filled", "emptied", "x_silu", "z_silu", "bc_hi", "bc_mid",
                 "bc_midcopy", "bc_lo", "u_ready")
        names += tuple(n + str(b) for n in ("abs_ready", "exp_ready", "step", "log_ready", "dt_ready") for b in range(HB))
        self.f = {n: chip.sem("mf_" + n) for n in names}
        names = ("reps_b", "reps_c", "decay", "c_out", "input", "state", "read", "summed", "direct", "gated",
                 "projected", "added")
        self.s = {n: chip.sem("mc_" + n) for n in names}
        self.core, self.front, self.new = None, 0, True
        self.ln = LayerNorm(chip, ctx, "mf_ln", m.res[:, 0:HTT, :], m.xn)

    def block(self, core, front, layer=0, loaded=False):
        self.core, self.front = core, front
        self.banks = FREE_BANKS if core is None else 1
        if front is not None:
            self.ln.src = self.m.res[:, front * HTT:(front + 1) * HTT, :]
        self.new = front == 0
        self.loads = 7 if self.new else 3
        with self.chip.nc.Block() as block:
            @block.sync
            def _(sp):
                if front is not None and not loaded:
                    self.load(sp, layer)

            @block.tensor
            def _(pe):
                for u in range(NU + LAG):
                    if core is not None:
                        self.core_tensor(pe, u)
                    if front is not None:
                        self.front_tensor(pe, u)
                if core is not None:
                    self.project(pe)

            @block.scalar
            def _(a):
                a.preload_act_table_set(EXP_AND_LN)
                for u in range(NU + AFTER):
                    if core is not None:
                        self.core_scalar(a, u)
                    if front is not None:
                        self.front_scalar(a, u)

            @block.vector
            def _(v):
                for u in range(NU + AFTER):
                    if core is not None and u < NU:
                        self.core_vector(v, u)
                    if front is not None:
                        self.front_vector(v, u)
                if core is not None:
                    self.join(v)
                    self.add_to_residual(v)

            @block.gpsimd
            def _(g):
                for u in range(NU):
                    if core is not None:
                        self.core_pool(g, u)
                    if front is not None:
                        self.front_pool(g, u)
                if front is not None:
                    self.inputs(g, 1)
        self.chip.clear(list(self.s.values()) + list(self.f.values()) + self.ln.sems())


    def wide(self, i):
        return self.chip.bank[:, i:i + 2, :].rearrange("p k q -> p (k q)")

    def half(self, tile, c, core):
        return tile[:, c, core * HT:(core + 1) * HT]

    def core_tensor(self, pe, u):
        m, s, bank = self.m, self.s, self.chip.bank
        n, c = u // NCH, u % NCH
        cols = lambda bb: m.bc[:, self.core * HT + bb * S:self.core * HT + (bb + 1) * S]
        if u < NU:
            if u >= 1:
                pe.wait_ge(s["c_out"], u)
            pe.matmul(bank[:, 6, :], m.pick[:, DS + n, :], cols(c), start=True, stop=True).then_inc(s["reps_c"], 1)
            if c == 0:
                if n >= 1:
                    pe.wait_ge(s["input"], u)
                for bb in range(HB):
                    last = pe.matmul(bank[:, 4 + bb, :], m.pick[:, n, :], cols(bb), start=True, stop=True)
                last.then_inc(s["reps_b"], 1)
        if u >= LAG:
            n, c = (u - LAG) // NCH, (u - LAG) % NCH
            pe.wait_ge(s["read"], u - LAG + 1)
            for bb in range(HB):
                last = pe.matmul(bank[:, 2 * c + bb, :], self.chip.ident[:],
                                 m.read[:, (u - LAG) % NR, bb * S:(bb + 1) * S], start=(n == 0), stop=(n == DS - 1))
            last.then_inc(s["summed"], 1)

    def project(self, pe):
        m, s, bank = self.m, self.s, self.chip.bank
        for c in range(NCH):
            pe.wait_ge(s["gated"], c + 1)
            for t in range(HTT):
                last = pe.matmul(bank[:, 4 + t // ST, (t % ST) * D:(t % ST + 1) * D], self.half(m.xs, c, self.core)[:, t * P:(t + 1) * P],
                                 m.out_w[:, self.core, c, :], start=(c == 0 and t % ST == 0),
                                 stop=(c == NCH - 1 and t % ST == ST - 1))
        last.then_inc(s["projected"], 1)

    def core_scalar(self, a, u):
        m, s = self.m, self.s
        n, c = u // NCH, u % NCH
        if u < NU:
            if u >= RA:
                a.wait_ge(s["state"], u - RA + 1)
            dt = self.half(m.dt, c, self.core).rearrange("p (b t) -> p b t", b=HB)
            a.activation(m.decay[:, u % RA, :, 1:], dt[:, :, 1:], ACT.Exp, scale=m.a[:, self.core, c, n:n + 1])\
                .then_inc(s["decay"], 1)
        if 1 <= u <= NU:
            n, bb = (u - 1) // NCH, (u - 1) % NCH
            a.wait_ge(s["reps_c"], u)
            if n >= 2:
                a.wait_ge(s["read"], NCH * (n - 1))
            a.activation(m.c_rep[:, n % 2, bb, :], self.chip.bank[:, 6, :], ACT.Copy).then_inc(s["c_out"], 1)

    def core_vector(self, v, u):
        m, s = self.m, self.s
        if u % NCH == 0:
            v.wait_ge(s["reps_b"], u // NCH + 1)
            for c in range(NCH):
                i = u + c
                if i >= RA:
                    v.wait_ge(s["state"], i - RA + 1)
                v.tensor_tensor(m.inp[:, i % RA, :], self.half(m.u, c, self.core), self.wide(4), ALU.mult)\
                    .then_inc(s["input"], 1)
        v.wait_ge(s["input"], u + 1)
        v.wait_ge(s["decay"], u + 1)
        if u >= RA:
            v.wait_ge(s["read"], u - RA + 1)
        v.tensor_tensor_scan(m.state[:, u % RA, :], m.decay[:, u % RA].rearrange("p b t -> p (b t)"),
                             m.inp[:, u % RA, :], 0.0, ALU.mult, ALU.add).then_inc(s["state"], 1)

    def core_pool(self, g, u):
        m, s = self.m, self.s
        n = u // NCH
        g.wait_ge(s["c_out"], HB * (n + 1))
        g.wait_ge(s["state"], u + 1)
        if u >= NR:
            g.wait_ge(s["summed"], u - NR + 1)
        g.tensor_tensor(m.read[:, u % NR, :], m.state[:, u % RA, :], m.c_rep[:, n % 2].rearrange("p b t -> p (b t)"),
                        ALU.mult).then_inc(s["read"], 1)

    def join(self, v):
        m, s, core = self.m, self.s, self.core
        for c in range(NCH):
            v.wait_ge(s["summed"], NU - NCH + c + 1)
            x = self.half(m.xs, c, core)
            v.scalar_tensor_tensor(x, x,
                                   m.col[:, core, 2 + 2 * NCH + c:3 + 2 * NCH + c], self.wide(2 * c),
                                   ALU.mult, ALU.add).then_inc(s["direct"], 1)
            v.wait_ge(s["direct"], c + 1)
            v.tensor_tensor(x, x, self.half(m.zs, c, core), ALU.mult).then_inc(s["gated"], 1)

    def add_to_residual(self, v):
        m, s = self.m, self.s
        v.wait_ge(s["projected"], 1)
        r = m.res[:, self.core * HTT:(self.core + 1) * HTT, :].rearrange("p t d -> p (t d)")
        v.tensor_tensor(r, r, self.wide(4), ALU.add).then_inc(s["added"], 1)


    def load(self, sp, layer):
        m, here, dram, front = self.m, self.f["w_here"], self.chip.dram, self.front
        flat = lambda t: t.rearrange("p a b -> p (a b)")

        def load(dst, name):
            sp.dma_start(dst, dram[name][bass.ds(layer, 1)].rearrange("l p n -> (l p) n")).then_inc(here, 16)
        load(m.col[:, front, :], "mb_col")
        load(flat(m.a[:, front]), "mb_a")
        load(flat(m.out_w[:, front]), "mb_out")
        if self.new:
            load(m.in_w[:], "mb_in")
            sp.dma_start(flat(m.taps[:]), dram["mb_conv"][bass.ds(layer, 1), :].broadcast_to([D, DC * DI]))\
                .then_inc(here, 16)
            load(flat(m.xp_w[:]), "mb_xp")
            load(m.dtp_w, "mb_dtp")

    def item_bank(self, k):
        return self.chip.bank[:, 7 - k % self.banks, :]

    def cols(self, b):
        return slice(self.front * HT + b * S, self.front * HT + (b + 1) * S)

    def front_tensor(self, pe, u):
        m, f = self.m, self.f
        for k, (kind, b, c) in enumerate(ITEMS):
            bank = self.item_bank(k)
            if u == SLOT[k]:
                if k == 0:
                    pe.wait_ge(self.ln.ready, 1)
                reads = {"conv": "turn", "gate": "turn", "dt": "rank"}.get(kind)
                emptied = max(k - self.banks + 1, after(reads, b) if reads else 0)
                if emptied > 0:
                    pe.wait_ge(f["emptied"], emptied)
                if kind == "turn":
                    for j in range(ST):
                        last = pe.transpose(bank[:, j * P:(j + 1) * P], m.xn[:, b * ST + j, :], self.chip.ident[:])
                elif kind == "conv":
                    pe.wait_ge(f["w_here"], 16 * self.loads)
                    if self.new:
                        pe.wait_ge(f["tapped"], 1)
                    last = self.convolve(pe, bank, b, c, range(DC // CONV_UNITS))
                    if CONV_UNITS > 1:
                        continue
                elif kind == "gate":
                    last = pe.matmul(bank, m.in_w[:, DI + c * P:DI + (c + 1) * P], m.h_t[:, b, PAD:],
                                     start=True, stop=True)
                elif kind == "dt":
                    last = pe.matmul(bank, m.dtp_w[:, c * P:(c + 1) * P], m.rank[:, b, :], start=True, stop=True)
                else:
                    pe.wait_ge(f["x_silu"], b + 1)
                    which = slice(0, DR) if kind == "rank" else slice(DR, DR + 2 * DS)
                    for c in range(NCH):
                        last = pe.matmul(bank[0:which.stop - which.start], m.xp_w[:, c, which], m.xs[:, c, self.cols(b)],
                                         start=(c == 0), stop=(c == NCH - 1))
                last.then_inc(f["filled"], 1)
            elif kind == "conv" and SLOT[k] < u < SLOT[k] + CONV_UNITS:
                part, taps = u - SLOT[k], DC // CONV_UNITS
                last = self.convolve(pe, bank, b, c, range(part * taps, (part + 1) * taps))
                if part == CONV_UNITS - 1:
                    last.then_inc(f["filled"], 1)

    def convolve(self, pe, bank, b, c, taps):
        m = self.m
        for k in taps:
            last = pe.matmul(bank, m.taps[:, k, c * P:(c + 1) * P], m.h_t[:, b, k:k + S],
                             start=(k == 0), stop=(k == DC - 1))
        return last

    def front_scalar(self, a, u):
        m, f, front = self.m, self.f, self.front
        col = m.col[:, front, :]
        if u == 1:
            a.wait_ge(f["w_here"], 16 * self.loads)
            a.activation(m.a[:, front], m.a[:, front], ACT.Exp).then_inc(f["a_exp"], 1)
        if u == 3:
            self.ln.scalar(a, load=False)
        for k, (kind, b, c) in enumerate(ITEMS):
            if u != SLOT[k] + EVAC + (CONV_UNITS - 1 if kind == "conv" else 0):
                continue
            a.wait_ge(f["filled"], k + 1)
            bank, done = self.item_bank(k), f["emptied"]
            if kind == "dt" and c == 0:
                a.wait_ge(done, k)
            if kind == "turn":
                last = a.activation(m.h_t[:, b, PAD:], bank, ACT.Identity, scale=col[:, 0:1], bias=col[:, 1:2])
            elif kind == "conv":
                last = a.activation(m.xs[:, c, self.cols(b)], bank, ACT.Identity, bias=col[:, 2 + c:3 + c])
            elif kind == "gate":
                last = a.activation(m.zs[:, c, self.cols(b)], bank, ACT.Copy)
            elif kind == "rank":
                last = a.activation(m.rank[:, b, :], bank[0:DR], ACT.Copy)
            elif kind == "dt":
                last = a.activation(m.dt[:, c, self.cols(b)], bank, ACT.Identity, bias=col[:, 2 + NCH + c:3 + NCH + c])
            else:
                last, done = a.activation(m.bc[0:2 * DS, self.cols(b)], bank[0:2 * DS], ACT.Copy), f["bc_hi"]
            last.then_inc(done, 1)
            if kind == "dt" and c == 0:
                a.activation(m.mid[:, b, :], m.rest[:, b, :], ACT.Copy).then_inc(f["bc_mid"], 1)
                a.activation(m.bc[2 * DS:4 * DS, self.cols(b)], m.rest[:, b, :], ACT.Copy).then_inc(f["bc_midcopy"], 1)
        for b in range(HB):
            if u == SILU_AT[b]:
                self.silu(a, m.xs[:, :, self.cols(b)], after("conv", b, NCH - 1), f["x_silu"])
                a.preload_act_table_set(EXP_AND_LN)
        if u == NU + AFTER - 1:
            self.silu(a, m.zs[:, :, front * HT:(front + 1) * HT], after("gate", HB - 1, NCH - 1), f["z_silu"])
        for b in range(HB):
            if u == SERIES_AT[b]:
                self.exponential(a, b)
            if u == SERIES_AT[b] + 5:
                self.logarithm(a, b)

    def silu(self, a, part, count, done):
        a.wait_ge(self.f["emptied"], count)
        a.activation(part, part, ACT.Silu).then_inc(done, 1)


    def exponential(self, a, b):
        m, f = self.m, self.f
        a.wait_ge(f["emptied"], after("dt", b, NCH - 1))
        a.activation(m.mag[:, b], m.dt[:, :, self.cols(b)], ACT.Abs).then_inc(f[f"abs_ready{b}"], 1)
        a.wait_ge(f[f"abs_ready{b}"], 1)
        a.activation(m.mag[:, b], m.mag[:, b], ACT.Exp, scale=-1.0).then_inc(f[f"exp_ready{b}"], 1)

    def logarithm(self, a, b):
        m, f = self.m, self.f
        a.wait_ge(f[f"step{b}"], 1)
        a.activation(m.big[:, b], m.big[:, b], ACT.Ln, bias=m.one[:]).then_inc(f[f"log_ready{b}"], 1)

    def soft_plus(self, v, b, i):
        m, f = self.m, self.f
        e, p, big, dt = m.mag[:, b], m.series[:, b], m.big[:, b], m.dt[:, :, self.cols(b)]
        step = f[f"step{b}"]
        if i == 0:
            v.wait_ge(f[f"exp_ready{b}"], 1)
            v.tensor_scalar(big, e, SMALL, None, ALU.max).then_inc(step, 1)
            return
        v.wait_ge(step, i)
        if i == 1:
            v.tensor_scalar(e, e, SMALL, None, ALU.min).then_inc(step, 1)
        if i == 2:
            v.tensor_scalar(p, e, SERIES[3], SERIES[2], ALU.mult, ALU.add).then_inc(step, 1)
        if i == 3:
            v.tensor_tensor(p, p, e, ALU.mult).then_inc(step, 1)
        if i == 4:
            v.scalar_tensor_tensor(p, p, SERIES[1], e, ALU.add, ALU.mult).then_inc(step, 1)
        if i == 5:
            v.scalar_tensor_tensor(p, p, SERIES[0], e, ALU.add, ALU.mult).then_inc(step, 1)
        if i == 6:
            v.scalar_tensor_tensor(p, dt, 0.0, p, ALU.max, ALU.add).then_inc(step, 1)
        if i == 7:
            v.wait_ge(f[f"log_ready{b}"], 1)
            v.scalar_tensor_tensor(dt, big, m.log_small[:], p, ALU.subtract, ALU.add)\
                .then_inc(f[f"dt_ready{b}"], 1)

    def front_vector(self, v, u):
        m, f = self.m, self.f
        if u == 0:
            self.ln.statistics(v)
        if u == 2:
            self.ln.normalise(v)
        for b in range(HB):
            if u == SLOT[after("bc", b) - 1] + 1:
                v.wait_ge(f["bc_hi"], b + 1)
                v.tensor_tensor(m.rest[:, b, :], self.item_bank(after("bc", b) - 1)[0:2 * DS], m.bc[0:2 * DS, self.cols(b)],
                                ALU.subtract).then_inc(f["emptied"], 1)
            if u == SLOT[after("bc", b) - 1] + 4:
                v.wait_ge(f["bc_mid"], b + 1)
                v.wait_ge(f["emptied"], after("bc", b))
                v.tensor_tensor(m.bc[4 * DS:6 * DS, self.cols(b)], m.rest[:, b, :], m.mid[:, b, :],
                                ALU.subtract).then_inc(f["bc_lo"], 1)
        for b in range(HB):
            if SERIES_AT[b] <= u < SERIES_AT[b] + SERIES_STEPS:
                self.soft_plus(v, b, u - SERIES_AT[b])

    def front_pool(self, g, u):
        m, f, front = self.m, self.f, self.front
        if u == 0 and self.new:
            g.wait_ge(f["w_here"], 16 * self.loads)
            g.tensor_tensor(m.taps[:], m.in_w[:, 0:DI].unsqueeze(1).broadcast_to([D, DC, DI]), m.taps[:],
                            ALU.mult).then_inc(f["tapped"], 1)
        if u == 1:
            g.wait_ge(f["a_exp"], 1)
            g.tensor_scalar(m.a[:, front], m.a[:, front], -1.0, None, ALU.mult).then_inc(f["a_neg"], 1)
        if u == NU - 1:
            self.inputs(g, 0)

    def inputs(self, g, b):
        m, f = self.m, self.f
        g.wait_ge(f[f"dt_ready{b}"], 1)
        g.wait_ge(f["x_silu"], b + 1)
        g.tensor_tensor(m.u[:, :, self.cols(b)], m.dt[:, :, self.cols(b)], m.xs[:, :, self.cols(b)], ALU.mult)\
            .then_inc(f["u_ready"], 1)


def mamba_out(chip, m):
    nc, dram = chip.nc, chip.dram
    with ExitStack() as ctx:
        w, b = chip.sb(ctx, "mo_w", [P, D]), chip.sb(ctx, "mo_b", [P, D])
        xn = m.u[:, 0, :].rearrange("p (t d) -> p t d", d=D)
        ln = LayerNorm(chip, ctx, "mo_ln", m.res, xn)
        here, step = chip.sem("mo_here"), chip.sem("mo_step")
        over_t = lambda row: row[:].unsqueeze(1).broadcast_to([P, NT, D])
        with nc.Block() as block:
            @block.sync
            def _(sp):
                sp.dma_start(w[:], dram["mb_fw"][0:1, :].broadcast_to([P, D])).then_inc(here, 16)
                sp.dma_start(b[:], dram["mb_fb"][0:1, :].broadcast_to([P, D])).then_inc(here, 16)

            @block.scalar
            def _(a):
                ln.scalar(a)

            @block.gpsimd
            def _(g):
                g.wait_ge(here, 32)
                g.tensor_tensor(chip.x[:], chip.x[:], over_t(b), ALU.add).then_inc(step, 1)

            @block.vector
            def _(v):
                ln.vector(v)
                v.wait_ge(here, 32)
                v.wait_ge(ln.ready, 1)
                v.wait_ge(step, 1)
                v.tensor_tensor(xn[:], xn[:], over_t(w), ALU.mult).then_inc(step, 1)
                v.wait_ge(step, 2)
                v.tensor_tensor(chip.x[:], chip.x[:], xn[:], ALU.add).then_inc(step, 1)


def more_mamba(r, a):
    g = lambda n: a["L1_attn_" + n]
    f = np.float32
    by_chunk = lambda v: v.reshape(NL, NCH, P, -1).transpose(0, 2, 1, 3).reshape(NL, P, -1)
    rows, n = np.arange(REP), np.arange(2 * DS)
    pick = np.repeat((rows[:, None] % (2 * DS) == n[None, :]).astype(f)[:, :, None], P, axis=2)
    r.update(
        mb_in=g("in_proj_w").transpose(0, 2, 1), mb_xp=by_chunk(g("x_proj_w").transpose(0, 2, 1)),
        mb_dtp=g("dt_proj_w").transpose(0, 2, 1), mb_out=by_chunk(g("out_proj_w").transpose(0, 2, 1)),
        mb_col=np.concatenate([g("norm_w")[:, :, None], g("norm_b")[:, :, None], by_chunk(g("conv_b")),
                               by_chunk(g("dt_proj_b")), by_chunk(g("D_param"))], axis=2),
        mb_a=by_chunk(g("A_log")), mb_conv=g("conv_w").transpose(0, 2, 1).reshape(NL, -1),
        mb_fw=g("fnorm_w").reshape(1, -1), mb_fb=g("fnorm_b").reshape(1, -1), pick=pick.reshape(REP, -1))


NC = 7
CW = 74
LAST_CW = S - (NC - 1) * CW
LANES = 32
STEPS = CTX + NC - 1
RING = 8
BIG = 1e30


def alignment(chip):
    nc = chip.nc
    dist_dram = nc.dram_tensor("dist_scratch", (CTX, B, S), F32, kind="Internal").ap()
    cost_dram = nc.dram_tensor("cost_scratch", (CTX + 1, B, S + 1), F32, kind="Internal").ap()
    with ExitStack() as stage:
        c = chip.sb(stage, "d_c", [CTX, B, D])
        big_row = chip.sb(stage, "d_big", [CTX + 1, B, S + 1])
        dist = chip.sb(stage, "d_dist", [LANES, STEPS, CW])
        distances(chip, c, dist, dist_dram, cost_dram, big_row)
        accumulate_costs(chip, dist, dist_dram, cost_dram)
        trace_back(chip, c, cost_dram)


def distances(chip, c, dist, dist_dram, cost_dram, big):
    nc, dram, bank = chip.nc, chip.dram, chip.bank
    with ExitStack() as ctx:
        sb = lambda n, shape, dt=F32: chip.sb(ctx, "dd_" + n, shape, dt)
        xn, xnt, sq = sb("xn", [P, NT, D]), sb("xnt", [P, TOK]), sb("sq", [P, TOK])
        ct, ones = sb("ct", [D, B * CTX]), sb("ones", [D, CTX])
        csq, cc = sb("csq", [CTX, B, D]), sb("cc", [CTX, B])
        d2, safe = sb("d2", [CTX, B, S]), sb("safe", [CTX, B, S])
        log, inv = sb("log", [CTX, B, S]), sb("inv", [CTX, B, S])
        root, err = sb("root", [CTX, B, S]), sb("err", [CTX, B, S])
        ln = LayerNorm(chip, ctx, "dd_ln", chip.x, xn)
        names = ("here", "ct_done", "ct_ready", "t_done", "xnt_ready", "sq_ready", "ones_set", "prod", "csqd", "ccd",
                 "d2d", "safed", "logd", "invd", "squared", "step", "dist", "stored", "big_set", "border")
        s = {n: chip.sem("dd_" + n) for n in names}
        with nc.Block() as block:
            @block.sync
            def _(sp):
                sp.dma_start(c[:], dram["ctx"].rearrange("b k d -> k b d")).then_inc(s["here"], 16)
                sp.wait_ge(s["big_set"], 1)
                sp.dma_start(cost_dram[:, :, :], big[:]).then_inc(s["border"], 16)
                sp.wait_ge(s["border"], 16)
                for b in range(B):
                    sp.wait_ge(s["dist"], b + 1)
                    sp.dma_start(dist_dram[:, b, :], root[:, b, :]).then_inc(s["stored"], 16)
                sp.wait_ge(s["stored"], 16 * B)

            @block.gpsimd
            def _(g):
                g.memset(big[:], BIG).then_inc(s["big_set"], 1)
                g.memset(ones[:], 1.0).then_inc(s["ones_set"], 1)
                g.memset(dist[:], BIG).then_inc(s["big_set"], 1)

            @block.tensor
            def _(pe):
                pe.wait_ge(s["here"], 16)
                for b in range(B):
                    last = pe.transpose(bank[:, 4, b * CTX:(b + 1) * CTX], c[:, b, :], chip.ident[0:CTX, 0:CTX])
                last.then_inc(s["ct_done"], 1)
                pe.wait_ge(ln.ready, 1)
                feature_major(pe, chip, xn, s["t_done"])
                pe.wait_ge(s["ones_set"], 1)
                pe.wait_ge(s["ct_ready"], 1)
                for b in range(B):
                    cols = slice(b * S, (b + 1) * S)
                    pe.wait_ge(s["xnt_ready"], b + 1)
                    pe.wait_ge(s["sq_ready"], b + 1)
                    pe.matmul(bank[0:CTX, b, :], ones[:], sq[:, cols], start=True, stop=False)
                    pe.matmul(bank[0:CTX, b, :], ct[:, b * CTX:(b + 1) * CTX], xnt[:, cols], start=False, stop=True)\
                        .then_inc(s["prod"], 1)

            @block.scalar
            def _(a):
                a.wait_ge(s["ct_done"], 1)
                a.activation(ct[:], bank[:, 4, 0:B * CTX], ACT.Copy, scale=-2.0).then_inc(s["ct_ready"], 1)
                ln.scalar(a)
                for b in range(B):
                    cols = slice(b * S, (b + 1) * S)
                    a.wait_ge(s["t_done"], b + 1)
                    a.activation(xnt[:, cols], bank[:, b, :], ACT.Copy).then_inc(s["xnt_ready"], 1)
                    a.activation(sq[:, cols], bank[:, b, :], ACT.Square).then_inc(s["sq_ready"], 1)
                for b in range(B):
                    a.wait_ge(s["safed"], b + 1)
                    a.activation(log[:, b, :], safe[:, b, :], ACT.Ln).then_inc(s["logd"], 1)
                    a.wait_ge(s["logd"], b + 1)
                    a.activation(inv[:, b, :], log[:, b, :], ACT.Exp, scale=-0.5).then_inc(s["invd"], 1)
                for b in range(B):
                    a.wait_ge(s["step"], b + 1)
                    a.activation(err[:, b, :], root[:, b, :], ACT.Square).then_inc(s["squared"], 1)

            @block.vector
            def _(v):
                v.wait_ge(s["here"], 16)
                v.tensor_tensor(csq[:], c[:], c[:], ALU.mult).then_inc(s["csqd"], 1)
                v.wait_ge(s["csqd"], 1)
                v.tensor_reduce(cc[:], csq[:], AX.X, ALU.add).then_inc(s["ccd"], 1)
                ln.vector(v)
                v.wait_ge(s["ccd"], 1)
                for b in range(B):
                    v.wait_ge(s["prod"], b + 1)
                    v.tensor_scalar(d2[:, b, :], bank[0:CTX, b, :], cc[:, b:b + 1], 0.0, ALU.add, ALU.max)\
                        .then_inc(s["d2d"], 1)
                    v.wait_ge(s["d2d"], b + 1)
                    v.tensor_scalar(safe[:, b, :], d2[:, b, :], 1e-18, None, ALU.max).then_inc(s["safed"], 1)
                for b in range(B):
                    v.wait_ge(s["invd"], b + 1)
                    v.tensor_tensor(root[:, b, :], d2[:, b, :], inv[:, b, :], ALU.mult).then_inc(s["step"], 1)
                for b in range(B):
                    v.wait_ge(s["squared"], b + 1)
                    v.tensor_tensor(err[:, b, :], d2[:, b, :], err[:, b, :], ALU.subtract).then_inc(s["step"], 1)
                for b in range(B):
                    v.wait_ge(s["step"], B + b + 1)
                    v.tensor_tensor(err[:, b, :], err[:, b, :], inv[:, b, :], ALU.mult).then_inc(s["step"], 1)
                for b in range(B):
                    v.wait_ge(s["step"], 2 * B + b + 1)
                    v.scalar_tensor_tensor(root[:, b, :], err[:, b, :], 0.5, root[:, b, :], ALU.mult, ALU.add)\
                        .then_inc(s["dist"], 1)


def accumulate_costs(chip, dist, dist_dram, cost_dram):
    nc = chip.nc
    with ExitStack() as ctx:
        sb = lambda n, shape, dt=F32: chip.sb(ctx, "dc_" + n, shape, dt)
        cost = sb("cost", [LANES, STEPS, CW])
        ring, least = sb("ring", [LANES, RING, CW + 1]), sb("least", [LANES, 2, CW])
        first = sb("first", [LANES, 1])
        names = ("set", "dist_here", "least", "row", "passed", "kept", "border", "stored")
        s = {n: chip.sem("dc_" + n) for n in names}
        shift = [(p - B) % LANES for p in range(LANES)]

        def above(v, at):
            up = ring[:, (at - 1) % RING, :]
            v.tensor_tensor(least[:, at % 2, :], up[:, 1:CW + 1], up[:, 0:CW], ALU.min).then_inc(s["least"], 1)

        with nc.Block() as block:
            @block.sync
            def _(sp):
                for c in range(NC):
                    w = CW if c < NC - 1 else LAST_CW
                    sp.dma_start(dist[c * B:(c + 1) * B, c:c + CTX, 0:w],
                                 dist_dram[:, :, c * CW:c * CW + w].rearrange("i b j -> b i j"))\
                        .then_inc(s["dist_here"], 16)
                sp.wait_ge(s["kept"], STEPS)
                for c in range(NC):
                    w = CW if c < NC - 1 else LAST_CW
                    sp.dma_start(cost_dram[1:CTX + 1, :, 1 + c * CW:1 + c * CW + w].rearrange("i b j -> b i j"),
                                 cost[c * B:(c + 1) * B, c:c + CTX, 0:w]).then_inc(s["stored"], 16)
                sp.wait_ge(s["stored"], 16 * NC)

            @block.vector
            def _(v):
                v.memset(ring[:], BIG).then_inc(s["set"], 1)
                v.memset(first[:], BIG).then_inc(s["set"], 1)
                v.wait_ge(s["set"], 2)
                v.memset(first[0:B, :], 0.0).then_inc(s["set"], 1)
                v.wait_ge(s["set"], 3)
                v.wait_ge(s["dist_here"], 16 * NC)
                above(v, 0)
                for at in range(STEPS):
                    j = at % RING
                    v.wait_ge(s["least"], at + 1)
                    if at > 0:
                        v.wait_ge(s["passed"], at)
                    if at >= RING:
                        v.wait_ge(s["kept"], at - RING + 1)
                    v.tensor_tensor_scan(ring[:, j, 1:CW + 1], least[:, at % 2, :], dist[:, at, :],
                                         ring[:, j, 0:1] if at > 0 else first[:], ALU.min, ALU.add)\
                        .then_inc(s["row"], 1)
                    v.wait_ge(s["row"], at + 1)
                    if at < STEPS - 1:
                        v.stream_shuffle(ring[:, (j + 1) % RING, 0:1], ring[:, j, CW:CW + 1], shift)\
                            .then_inc(s["passed"], 1)
                        above(v, at + 1)

            @block.scalar
            def _(a):
                for at in range(STEPS):
                    a.wait_ge(s["row"], at + 1)
                    a.activation(cost[:, at, :], ring[:, at % RING, 1:CW + 1], ACT.Copy).then_inc(s["kept"], 1)


def trace_back(chip, c, cost_dram):
    nc, dram, bank = chip.nc, chip.dram, chip.bank
    with ExitStack() as ctx:
        sb = lambda n, shape, dt=F32: chip.sb(ctx, "db_" + n, shape, dt)
        here_cost, above = sb("cur", [CTX, B, S + 1]), sb("above", [CTX, B, S + 1])
        leave, diag = sb("leave", [CTX, B, S]), sb("diag", [CTX, B, S])
        start = sb("start", [CTX, B, S])
        follow16 = sb("follow16", [CTX, B, S], F16)
        column = sb("column", [P, S])
        table = sb("table", [B, CTX, S], F16)
        end, hit = sb("end", [B, CTX]), sb("hit", [B, 2, S])
        endt, startt, picked = sb("endt", [CTX, B]), sb("startt", [CTX, B]), sb("picked", [CTX, B, S])
        names = ("here", "diagonal", "enters", "step", "table_ready", "table_here", "end_set", "hop", "end_done", "onpath", "spread", "pick",
                 "scanned")
        s = {n: chip.sem("db_" + n) for n in names}
        with nc.Block() as block:
            @block.sync
            def _(sp):
                sp.dma_start(here_cost[:], cost_dram[1:CTX + 1, :, :]).then_inc(s["here"], 16)
                sp.dma_start(above[:], cost_dram[0:CTX, :, :]).then_inc(s["here"], 16)
                sp.dma_start(column[:], dram["column"][0:1, :].broadcast_to([P, S])).then_inc(s["here"], 16)
                for b in range(B):
                    sp.wait_ge(s["table_ready"], b + 1)
                    sp.dma_start(table[b:b + 1, :, :], follow16[:, b, :]).then_inc(s["table_here"], 16)

            @block.gpsimd
            def _(g):
                g.wait_ge(s["here"], 48)
                g.wait_ge(s["diagonal"], 1)
                g.tensor_tensor(picked[:], column[0:CTX, :].unsqueeze(1).broadcast_to([CTX, B, S]), diag[:],
                                ALU.subtract).then_inc(s["enters"], 1)

            @block.vector
            def _(v):
                chain = Chain(v, s["step"])
                col = column[0:CTX, :].unsqueeze(1).broadcast_to([CTX, B, S])
                up, up_left, left = above[:, :, 1:S + 1], above[:, :, 0:S], here_cost[:, :, 0:S]
                v.wait_ge(s["here"], 48)
                v.tensor_tensor(diag[:], up_left, up, ALU.is_le).then_inc(s["diagonal"], 1)
                chain.do(v.tensor_tensor(leave[:], up, up_left, ALU.min))
                chain.do(v.tensor_tensor(leave[:], leave[:], left, ALU.is_le))
                v.wait_ge(s["enters"], 1)
                chain.do(v.tensor_tensor(diag[:], picked[:], leave[:], ALU.mult))
                for b in range(B):
                    v.tensor_tensor_scan(follow16[:, b, :], diag[:, b, :], diag[:, b, :], 0.0, ALU.max, ALU.max)\
                        .then_inc(s["table_ready"], 1)
                v.tensor_tensor(leave[:], col, leave[:], ALU.mult).then_inc(s["step"], 1)
                chain.at += 1
                v.memset(end[:, CTX - 1:CTX], float(S)).then_inc(s["end_set"], 1)
                v.wait_ge(s["step"], chain.at)
                for b in range(B):
                    v.tensor_tensor_scan(start[:, b, :], leave[:, b, :], leave[:, b, :], 0.0, ALU.max, ALU.max)\
                        .then_inc(s["scanned"], 1)
                v.wait_ge(s["end_set"], 1)
                v.wait_ge(s["table_here"], 16 * B)
                for j in range(CTX - 1):
                    i = CTX - 1 - j
                    v.scalar_tensor_tensor(hit[:, j % 2, :], column[0:B, :], end[:, i:i + 1], table[:, i, :],
                                           ALU.is_equal, ALU.mult, accum_out=end[:, i - 1:i]).then_inc(s["hop"], 1)
                    v.wait_ge(s["hop"], j + 1)
                v.wait_ge(s["end_done"], 1)
                v.tensor_copy(endt[:], bank[0:CTX, 0, 0:B]).then_inc(s["step"], 1)
                chain.at += 1
                v.wait_ge(s["step"], chain.at)
                v.wait_ge(s["scanned"], B)
                for b in range(B):
                    v.scalar_tensor_tensor(picked[:, b, :], column[0:CTX, :], endt[:, b:b + 1], start[:, b, :],
                                           ALU.is_equal, ALU.mult, accum_out=startt[:, b:b + 1]).then_inc(s["step"], 1)
                    v.tensor_scalar(diag[:, b, :], column[0:CTX, :], endt[:, b:b + 1], None, ALU.is_le)\
                        .then_inc(s["step"], 1)
                chain.at += 2 * B
                v.wait_ge(s["step"], chain.at)
                for b in range(B):
                    v.scalar_tensor_tensor(picked[:, b, :], column[0:CTX, :], startt[:, b:b + 1], diag[:, b, :],
                                           ALU.is_ge, ALU.mult).then_inc(s["onpath"], 1)
                for b in range(B):
                    v.wait_ge(s["spread"], b + 1)
                    xb = chip.x[:, b * ST:(b + 1) * ST, :].rearrange("p t d -> p (t d)")
                    v.tensor_tensor(xb, xb, bank[:, 4 + b, :], ALU.add).then_inc(s["pick"], 1)

            @block.tensor
            def _(pe):
                pe.wait_ge(s["hop"], CTX - 1)
                pe.wait_ge(s["end_set"], 1)
                pe.transpose(bank[0:CTX, 0, 0:B], end[:], chip.ident[0:B, 0:B]).then_inc(s["end_done"], 1)
                for b in range(B):
                    pe.wait_ge(s["onpath"], b + 1)
                    for j in range(ST):
                        last = pe.matmul(bank[:, 4 + b, j * D:(j + 1) * D], picked[:, b, j * P:(j + 1) * P], c[:, b, :],
                                         start=True, stop=True)
                    last.then_inc(s["spread"], 1)


def more_alignment(r, a):
    r["column"] = np.arange(1, S + 1, dtype=np.float32).reshape(1, -1)


INNER = 512
NI = INNER // P
DOWN_LAG = 3
ROUND = 1.5 * 2.0 ** 23


def ternary_feed_forward(chip):
    with ExitStack() as stage:
        wg = chip.sb(stage, "t_wg", [P, INNER], BF16)
        wu = chip.sb(stage, "t_wu", [P, INNER], BF16)
        wd = chip.sb(stage, "t_wd", [P, NI, D], BF16)
        unit = chip.sb(stage, "t_unit", [P, 3])
        identb = chip.sb(stage, "t_identb", [P, P], BF16)
        xq = chip.sb(stage, "t_xq", [P, NT, D], BF16)
        step_x = chip.sb(stage, "t_step_x", [P, NT])
        quantize_inputs(chip, (wg, wu, wd), unit, identb, xq, step_x)
        feed_forward(chip, (wg, wu, wd), unit, identb, xq, step_x)


def quantize_inputs(chip, weights, unit, identb, xq, step_x):
    nc, dram, bank = chip.nc, chip.dram, chip.bank
    names = ("t_wg", "t_wu", "t_wd")
    with ExitStack() as ctx:
        sb = lambda n, shape, dt=F32: chip.sb(ctx, "q_" + n, shape, dt)
        xn, scaled = sb("xn", [P, NT, D]), sb("scaled", [P, NT, D])
        raw = [sb("raw" + n, [P, INNER]) for n in names]
        absum, ones, mean, scale = sb("absum", [P, 3]), sb("ones", [P, P]), sb("mean", [P, 3]), sb("scale", [P, 3])
        peak, rpeak, scale_x = sb("peak", [P, NT]), sb("rpeak", [P, NT]), sb("scale_x", [P, NT])
        ln = LayerNorm(chip, ctx, "q_ln", chip.x, xn)
        here, ones_set, summed, step = (chip.sem("q_" + n) for n in ("here", "ones_set", "summed", "step"))
        idb = chip.sem("q_idb")
        with nc.Block() as block:
            @block.sync
            def _(sp):
                for n, t in zip(names, raw):
                    sp.dma_start(t[:], dram[n][:, :]).then_inc(here, 16)

            @block.gpsimd
            def _(g):
                g.memset(ones[:], 1.0).then_inc(ones_set, 1)
                g.tensor_copy(identb[:], chip.ident[:]).then_inc(idb, 1)

            @block.tensor
            def _(pe):
                pe.wait_ge(ones_set, 1)
                pe.wait_ge(step, 3)
                pe.matmul(bank[:, 0, 0:3], ones[:], absum[:], start=True, stop=True).then_inc(summed, 1)

            @block.scalar
            def _(a):
                ln.scalar(a)

            @block.vector
            def _(v):
                chain = Chain(v, step)
                ln.vector(v)
                v.wait_ge(here, 48)
                for n in range(3):
                    v.tensor_reduce(absum[:, n:n + 1], raw[n][:], AX.X, ALU.add, apply_absolute_value=True)\
                        .then_inc(step, 1)
                chain.at = 3
                v.wait_ge(ln.ready, 1)
                chain.do(v.tensor_reduce(peak[:], xn[:], AX.X, ALU.max, apply_absolute_value=True))
                chain.do(v.tensor_scalar(peak[:], peak[:], 1e-5, None, ALU.max))
                chain.do(v.reciprocal(rpeak[:], peak[:]))
                chain.do(v.tensor_scalar(scale_x[:], rpeak[:], 127.0, None, ALU.mult))
                v.reciprocal(step_x[:], scale_x[:]).then_inc(step, 1)
                chain.at += 1
                chain.do(v.tensor_tensor(scaled[:], xn[:], scale_x[:].unsqueeze(2).broadcast_to([P, NT, D]), ALU.mult))
                chain.do(v.tensor_scalar(scaled[:], scaled[:], ROUND, -ROUND, ALU.add, ALU.add))
                chain.do(v.tensor_scalar(xq[:], scaled[:], 127.0, -128.0, ALU.min, ALU.max))
                v.wait_ge(summed, 1)
                chain.do(v.tensor_scalar(mean[:], bank[:, 0, 0:3], 1.0 / (INNER * D), 1e-5, ALU.mult, ALU.max))
                chain.do(v.reciprocal(scale[:], mean[:]))
                v.reciprocal(unit[:], scale[:]).then_inc(step, 1)
                chain.at += 1
                for n in range(3):
                    v.tensor_scalar(raw[n][:], raw[n][:], scale[:, n:n + 1], ROUND, ALU.mult, ALU.add).then_inc(step, 1)
                chain.at += 3
                v.wait_ge(step, chain.at)
                for n in range(3):
                    v.tensor_scalar(raw[n][:], raw[n][:], ROUND, 1.0, ALU.subtract, ALU.min).then_inc(step, 1)
                chain.at += 3
                v.wait_ge(step, chain.at)
                for n in range(3):
                    w = weights[n][:] if n < 2 else weights[n][:].rearrange("p i o -> p (i o)")
                    v.tensor_scalar(w, raw[n][:], -1.0, None, ALU.max).then_inc(step, 1)
                chain.at += 3


def feed_forward(chip, weights, unit, identb, xq, step_x):
    nc, bank = chip.nc, chip.bank
    wg, wu, wd = weights
    with ExitStack() as ctx:
        sb = lambda n, shape, dt=F32: chip.sb(ctx, "f_" + n, shape, dt)
        per_gate, per_up = sb("per_gate", [P, NT]), sb("per_up", [P, NT])
        xt, hqt = sb("xt", [P, 2, P], BF16), sb("hqt", [P, 2, NI, P], BF16)
        act, h, hs = sb("act", [P, 2, INNER]), sb("h", [P, 2, INNER]), sb("hs", [P, 2, INNER])
        hq = sb("hq", [P, 2, INNER], BF16)
        peak, rpeak, scale = sb("peak", [P, NT]), sb("rpeak", [P, NT]), sb("scale", [P, NT])
        per_down = sb("per_down", [P, NT])
        names = ("per", "xt_done", "xt_out", "gated", "acted", "joined", "hq_ready", "hqt_done", "hqt_out", "down",
                 "added", "peaked", "clipped", "recip", "scaled", "rounded", "stepd")
        s = {n: chip.sem("f_" + n) for n in names}
        xt_ps = lambda t: bank[:, 4, :].bitcast(BF16)[:, (t % 2) * 512:(t % 2) * 512 + P]
        hqt_ps = lambda t: bank[:, 5, :].bitcast(BF16)[:, (t % 2) * 512:(t % 2) * 512 + INNER]
        with nc.Block() as block:
            @block.tensor
            def _(pe):
                def turn_inputs(t):
                    if t >= 2:
                        pe.wait_ge(s["xt_out"], t - 1)
                    pe.transpose(xt_ps(t), xq[:, t, :], identb[:]).then_inc(s["xt_done"], 1)

                turn_inputs(0)
                for n in range(NT + DOWN_LAG + 1):
                    if n < NT:
                        t = n
                        pe.wait_ge(s["xt_out"], t + 1)
                        if t >= 2:
                            pe.wait_ge(s["joined"], t - 1)
                        pe.matmul(bank[:, 2 * (t % 2), :], xt[:, t % 2, :], wg[:], start=True, stop=True)
                        pe.matmul(bank[:, 2 * (t % 2) + 1, :], xt[:, t % 2, :], wu[:], start=True, stop=True)\
                            .then_inc(s["gated"], 1)
                    if n + 1 < NT:
                        turn_inputs(n + 1)
                    if n > DOWN_LAG:
                        t = n - DOWN_LAG - 1
                        pe.wait_ge(s["hqt_out"], t + 1)
                        if t >= 2:
                            pe.wait_ge(s["added"], t - 1)
                        for i in range(NI):
                            last = pe.matmul(bank[:, 6 + t % 2, 0:D], hqt[:, t % 2, i, :], wd[:, i, :],
                                             start=(i == 0), stop=(i == NI - 1))
                        last.then_inc(s["down"], 1)
                    if DOWN_LAG <= n < NT + DOWN_LAG:
                        t = n - DOWN_LAG
                        pe.wait_ge(s["hq_ready"], t + 1)
                        if t >= 2:
                            pe.wait_ge(s["hqt_out"], t - 1)
                        for i in range(NI):
                            last = pe.transpose(hqt_ps(t)[:, i * P:(i + 1) * P], hq[:, t % 2, i * P:(i + 1) * P], identb[:])
                        last.then_inc(s["hqt_done"], 1)

            @block.scalar
            def _(a):
                def keep_inputs(t):
                    a.wait_ge(s["xt_done"], t + 1)
                    if t >= 2:
                        a.wait_ge(s["gated"], t - 1)
                    a.activation(xt[:, t % 2, :], xt_ps(t), ACT.Copy).then_inc(s["xt_out"], 1)

                keep_inputs(0)
                a.wait_ge(s["per"], 2)
                for n in range(NT + DOWN_LAG):
                    if n < NT:
                        t = n
                        a.wait_ge(s["gated"], t + 1)
                        if t >= 2:
                            a.wait_ge(s["joined"], t - 1)
                        a.activation(act[:, t % 2, :], bank[:, 2 * (t % 2), :], ACT.Silu, scale=per_gate[:, t:t + 1])\
                            .then_inc(s["acted"], 1)
                    if n + 1 < NT:
                        keep_inputs(n + 1)
                    if n >= DOWN_LAG:
                        t = n - DOWN_LAG
                        a.wait_ge(s["hqt_done"], t + 1)
                        if t >= 2:
                            a.wait_ge(s["down"], t - 1)
                        a.activation(hqt[:, t % 2].rearrange("p i q -> p (i q)"), hqt_ps(t), ACT.Copy)\
                            .then_inc(s["hqt_out"], 1)

            @block.vector
            def _(v):
                v.tensor_scalar(per_gate[:], step_x[:], unit[:, 0:1], None, ALU.mult).then_inc(s["per"], 1)
                v.tensor_scalar(per_up[:], step_x[:], unit[:, 1:2], None, ALU.mult).then_inc(s["per"], 1)
                v.wait_ge(s["per"], 2)
                for n in range(NT + DOWN_LAG + 2):
                    if n < NT:
                        t = n
                        v.wait_ge(s["acted"], t + 1)
                        if t >= 2:
                            v.wait_ge(s["scaled"], t - 1)
                        v.scalar_tensor_tensor(h[:, t % 2, :], bank[:, 2 * (t % 2) + 1, :], per_up[:, t:t + 1],
                                               act[:, t % 2, :], ALU.mult, ALU.mult).then_inc(s["joined"], 1)
                    if 1 <= n <= NT:
                        t = n - 1
                        v.wait_ge(s["recip"], t + 1)
                        if t >= 2:
                            v.wait_ge(s["hq_ready"], t - 1)
                        v.tensor_scalar(hs[:, t % 2, :], h[:, t % 2, :], rpeak[:, t:t + 1], ROUND, ALU.mult, ALU.add)\
                            .then_inc(s["scaled"], 1)
                    if n < NT:
                        t = n
                        v.wait_ge(s["joined"], t + 1)
                        v.tensor_reduce(peak[:, t:t + 1], h[:, t % 2, :], AX.X, ALU.max, apply_absolute_value=True)\
                            .then_inc(s["peaked"], 1)
                    if 1 <= n <= NT:
                        t = n - 1
                        v.wait_ge(s["scaled"], t + 1)
                        v.tensor_scalar(hs[:, t % 2, :], hs[:, t % 2, :], ROUND, 127.0, ALU.subtract, ALU.min)\
                            .then_inc(s["rounded"], 1)
                    if n < NT:
                        t = n
                        v.wait_ge(s["peaked"], t + 1)
                        v.tensor_scalar(peak[:, t:t + 1], peak[:, t:t + 1], 1e-5, 1.0 / 127.0, ALU.max, ALU.mult)\
                            .then_inc(s["clipped"], 1)
                    if n > DOWN_LAG + 1:
                        t = n - DOWN_LAG - 2
                        v.wait_ge(s["down"], t + 1)
                        v.scalar_tensor_tensor(chip.x[:, t, :], bank[:, 6 + t % 2, 0:D], per_down[:, t:t + 1],
                                               chip.x[:, t, :], ALU.mult, ALU.add).then_inc(s["added"], 1)
                    if n < NT:
                        t = n
                        v.wait_ge(s["clipped"], t + 1)
                        v.reciprocal(rpeak[:, t:t + 1], peak[:, t:t + 1]).then_inc(s["recip"], 1)
                        v.tensor_scalar(per_down[:, t:t + 1], peak[:, t:t + 1], unit[:, 2:3], None, ALU.mult)\
                            .then_inc(s["stepd"], 1)

            @block.gpsimd
            def _(g):
                for t in range(NT):
                    g.wait_ge(s["rounded"], t + 1)
                    if t >= 2:
                        g.wait_ge(s["hqt_done"], t - 1)
                    g.tensor_scalar(hq[:, t % 2, :], hs[:, t % 2, :], -128.0, None, ALU.max)\
                        .then_inc(s["hq_ready"], 1)


def more_ternary(r, a):
    r.update(t_wg=a["L1_ffn_w_gate"].T, t_wu=a["L1_ffn_w_up"].T,
             t_wd=a["L1_ffn_w_down"].T.reshape(NI, P, D).transpose(1, 0, 2).reshape(P, INNER))


def self_attention_stage(chip):
    with ExitStack() as stage:
        mixt = chip.sb(stage, "mixt", [P, TOK])
        with ExitStack() as inner:
            values = chip.sb(inner, "values", [P, NT, D])
            qparts = chip.sb(inner, "qparts", [P, 3, TOK], BF16)
            kparts = chip.sb(inner, "kparts", [P, 3, TOK], BF16)
            stacks = Stacks(chip, inner, qparts, kparts)
            self_attention_inputs(chip, stacks, qparts, kparts, values)
            self_attention(chip, stacks, values, mixt)
        project_and_add(chip, "a_out", mixt, "wo")


STAGES = (self_attention_stage, cross_attention, experts, mamba, alignment, ternary_feed_forward)


def build(nc, dram, out, stages=STAGES):
    with ExitStack() as ctx:
        chip = Chip(nc, ctx, dram)
        for stage in stages:
            chip.run(stage)
        with nc.semaphore("stored") as stored, nc.Block() as block:
            @block.sync
            def _(sp):
                sp.dma_start(out.rearrange("b (t p) d -> p (b t) d", p=P), chip.x[:]).then_inc(stored, 16)
                sp.wait_ge(stored, 16)


def laid_out(a):
    c = np.ascontiguousarray
    f = np.float32
    by_d = np.arange(D).reshape(H, HD).T.reshape(-1)
    swap = by_d.reshape(HD, H)[np.arange(HD) ^ 1].reshape(-1)
    half = np.arange(HD // 2, dtype=f)
    inv_freq = (f(10000.0) ** (-(half * f(2.0) / f(HD)))).astype(f)
    ang = np.arange(S, dtype=f)[:, None] * inv_freq[None, :]
    of_row = np.arange(D) // H
    cos, sin = np.cos(ang).astype(f).T[of_row // 2], np.sin(ang).astype(f).T[of_row // 2]
    sin = np.where((of_row % 2 == 0)[:, None], -sin, sin)
    k = np.arange(P)
    r = {
        "x": a["x"], "ctx": a["ctx_1024"],
        "ident": np.eye(P, dtype=f),
        "keep": np.concatenate([np.ones((P, 2 * P), f)] + 2 * [(k[:, None] <= k[None, :]).astype(f)], 1),
        "rope_cos": cos, "rope_sin": sin,
        "wq": a["L0_attn_w_q"][by_d].T, "wq_swap": a["L0_attn_w_q"][swap].T,
        "wk": a["L0_attn_w_k"][by_d].T, "wk_swap": a["L0_attn_w_k"][swap].T,
        "wv": a["L0_attn_w_v"].T, "wo": a["L0_attn_w_o"].T,
    }
    for part in (more, more_experts, more_mamba, more_alignment, more_ternary):
        part(r, a)
    return {n: c(v) for n, v in r.items()}


def kernel(**inputs):
    import concourse.bacc as bacc
    from concourse.bass_utils import run_bass_kernel_spmd

    arrays = laid_out({n: np.asarray(v) for n, v in inputs.items()})
    nc = bacc.Bacc("TRN2", target_bir_lowering=False, num_devices=1)
    dram = {n: nc.dram_tensor("in_" + n, a.shape, mybir.dt.from_np(a.dtype), kind="ExternalInput").ap()
            for n, a in arrays.items()}
    out = nc.dram_tensor("out", (B, S, D), F32, kind="ExternalOutput").ap()
    build(nc, dram, out)
    return run_bass_kernel_spmd(nc, [{"in_" + n: a for n, a in arrays.items()}], core_ids=[0]).results[0]["out"]
```
